# Optimizing a Trainium2 kernel written in Bass

```python
import numpy as np
import jax
import jax.numpy as jnp

def _softmax(x, axis=-1):
    return jax.nn.softmax(x, axis=axis)

def _gelu(x):
    return jax.nn.gelu(x, approximate=True)

def _silu(x):
    return jax.nn.silu(x)

def _sigmoid(x):
    return jax.nn.sigmoid(x)

def _layernorm(x, axis=-1, eps=1e-05):
    m = jnp.mean(x, axis=axis, keepdims=True)
    v = jnp.var(x, axis=axis, keepdims=True)
    return (x - m) / jnp.sqrt(v + eps)

def _scatter_add(tgt, idx, src, axis=0):
    return tgt.at[idx].add(src)

def _segment_sum(src, seg, n):
    return jax.ops.segment_sum(src, seg, n)
kernel_name = 'mk_gps_d2_gnn_r16_2d9c27'

def setup_inputs(seed: int=0):
    np.random.seed(seed)
    _w = jnp.asarray

    def _rec_inputs():
        import jax
        import jax.numpy as jnp
        _gk = jax.random.key(seed)
        x = -6.415e-05 + 1 * jax.random.normal(jax.random.fold_in(_gk, 1), (625, 1024), jnp.float32)
        _s = jax.random.randint(jax.random.fold_in(_gk, 2), (10000,), 0, 625, jnp.int32)
        _d = jax.random.randint(jax.random.fold_in(_gk, 3), (10000,), 0, 625, jnp.int32)
        _loop = jnp.arange(625, dtype=jnp.int32)
        src = jnp.concatenate([_s, _d, _loop])
        dst = jnp.concatenate([_d, _s, _loop])
        _o = jnp.argsort(dst, stable=True)
        src = src[_o]
        dst = dst[_o]
        edge_type_8 = jax.random.randint(jax.random.fold_in(_gk, 12), (20625,), 0, 8, jnp.int32)
        return (x, src, dst, edge_type_8)
    x, src, dst, edge_type_8 = _rec_inputs()

    def _L0_gnn_setup():
        import jax, jax.numpy as jnp
        import numpy as np
        N, D, R, E = (625, 1024, 8, 5000)

        def _rgcn(x, edge_index, edge_type, weight, root, bias):
            src, dst = (edge_index[0], edge_index[1])
            msgs = x[src]
            out = x @ root + bias
            n = x.shape[0]
            for r in range(weight.shape[0]):
                mask = (edge_type == r).astype(x.dtype)
                sums = jax.ops.segment_sum(msgs * mask[:, None], dst, num_segments=n)
                cnt = jax.ops.segment_sum(mask, dst, num_segments=n)
                mean = sums / jnp.maximum(cnt, 1.0)[:, None]
                out = out + mean @ weight[r]
            return out
        key = jax.random.key(seed)
        ks = jax.random.split(key, 8)
        s = 1.0 / np.sqrt(D)
        x = jax.random.normal(ks[0], (N, D), dtype=jnp.float32)
        edge_index = jax.random.randint(ks[1], (2, E), 0, N, dtype=jnp.int64)
        edge_type = jax.random.randint(ks[2], (E,), 0, R, dtype=jnp.int64)
        weight = jax.random.normal(ks[3], (R, D, D), dtype=jnp.float32) * s
        root = jax.random.normal(ks[4], (D, D), dtype=jnp.float32) * s
        bias = jnp.zeros((D,), dtype=jnp.float32)
        w_gate = jax.random.normal(ks[5], (2 * D, D), dtype=jnp.float32) * (1.0 / np.sqrt(2 * D))
        b_gate = jnp.zeros((D,), dtype=jnp.float32)
        return {'x': x, 'edge_index': edge_index, 'edge_type': edge_type, 'weight': weight, 'root': root, 'bias': bias, 'w_gate': w_gate, 'b_gate': b_gate}
    _L0_gnn_all = _L0_gnn_setup()
    _L0_gnn_in = {k: v for k, v in _L0_gnn_all.items() if k in ('weight', 'root', 'bias', 'w_gate', 'b_gate')}
    del _L0_gnn_all

    def _L0_mix_setup():
        import jax, jax.numpy as jnp
        import numpy as np
        EMBED_DIM = 1024
        N_HEADS = 16
        HEAD_DIM = EMBED_DIM // N_HEADS
        N_FEATURES = 64
        EPS = 0.0001

        def softmax_kernel(data, projection_matrix, eps=EPS):
            data_normalizer = data.shape[-1] ** (-0.25)
            proj = jnp.einsum('bhnd,fd->bhnf', data, projection_matrix) * data_normalizer
            proj_max = jnp.max(proj, axis=-1, keepdims=True)
            return jnp.exp(proj - proj_max + eps)
        key = jax.random.key(seed)
        k_x, k_w1, k_b1, k_w2, k_b2, k_p = jax.random.split(key, 6)
        B, N, D = (4, 256, EMBED_DIM)
        s1 = 1.0 / np.sqrt(D)
        x = jax.random.normal(k_x, (B, N, D), dtype=jnp.float32)
        W_qkv = jax.random.uniform(k_w1, (3 * D, D), dtype=jnp.float32, minval=-s1, maxval=s1)
        b_qkv = jax.random.uniform(k_b1, (3 * D,), dtype=jnp.float32, minval=-s1, maxval=s1)
        W_proj = jax.random.uniform(k_w2, (D, D), dtype=jnp.float32, minval=-s1, maxval=s1)
        b_proj = jax.random.uniform(k_b2, (D,), dtype=jnp.float32, minval=-s1, maxval=s1)
        pm = jax.random.normal(k_p, (N_FEATURES, HEAD_DIM), dtype=jnp.float32)
        pm = pm / jnp.linalg.norm(pm, axis=-1, keepdims=True)
        return {'x': x, 'W_qkv': W_qkv, 'b_qkv': b_qkv, 'W_proj': W_proj, 'b_proj': b_proj, 'proj_mat': pm}
    _L0_mix_all = _L0_mix_setup()
    _L0_mix_in = {k: v for k, v in _L0_mix_all.items() if k in ('W_qkv', 'b_qkv', 'W_proj', 'b_proj', 'proj_mat')}
    del _L0_mix_all

    def _L0_ffn_setup():
        import jax, jax.numpy as jnp
        import numpy as np
        BIT = 8
        QMAX = 2 ** (BIT - 1) - 1
        QMIN = -2 ** (BIT - 1)
        BOUNDARY_RANGE = 0.005
        EPS = 1e-05

        def _quant_act_int8(x):
            amax = jnp.maximum(jnp.quantile(jnp.abs(x), 1.0 - BOUNDARY_RANGE), EPS)
            s = QMAX / amax
            q = jnp.clip(jnp.round(x * s), QMIN, QMAX) / s
            return x + jax.lax.stop_gradient(q - x)

        def _quant_w_ternary(w):
            gamma = jnp.mean(jnp.abs(w)) + EPS
            q = jnp.clip(jnp.round(w / gamma), -1.0, 1.0) * gamma
            return w + jax.lax.stop_gradient(q - w)

        def _qlinear(x, w):
            xq = _quant_act_int8(x)
            wq = _quant_w_ternary(w)
            return jnp.einsum('btd,hd->bth', xq, wq)

        def _layernorm(x, g, b):
            mu = jnp.mean(x, axis=-1, keepdims=True)
            var = jnp.mean(jnp.square(x - mu), axis=-1, keepdims=True)
            return (x - mu) * jax.lax.rsqrt(var + 1e-05) * g + b
        key = jax.random.key(seed)
        k_x, k_w1, k_w2 = jax.random.split(key, 3)
        B, T, D, H = (64, 256, 1024, 256)
        x = jax.random.normal(k_x, (B, T, D), dtype=jnp.float32)
        ln_g = jnp.ones((D,), dtype=jnp.float32)
        ln_b = jnp.zeros((D,), dtype=jnp.float32)
        w1 = jax.random.normal(k_w1, (H, D), dtype=jnp.float32) * (1.0 / np.sqrt(D))
        w2 = jax.random.normal(k_w2, (D, H), dtype=jnp.float32) * (1.0 / np.sqrt(H))
        return {'x': x, 'ln_g': ln_g, 'ln_b': ln_b, 'w1': w1, 'w2': w2}
    _L0_ffn_all = _L0_ffn_setup()
    _L0_ffn_in = {k: v for k, v in _L0_ffn_all.items() if k in ('ln_g', 'ln_b', 'w1', 'w2')}
    del _L0_ffn_all

    def _L1_gnn_setup():
        import jax, jax.numpy as jnp
        import numpy as np
        N = 1250
        E = 20000
        D_IN = 1024
        D_OUT = 1024
        key = jax.random.key(seed)
        k1, k2, k3, k4 = jax.random.split(key, 4)
        x = jax.random.normal(k1, (N, D_IN), dtype=jnp.float32)
        edge_index = jax.random.randint(k2, (2, E), 0, N, dtype=jnp.int64)
        W = jax.random.normal(k3, (D_OUT, D_IN), dtype=jnp.float32) * (1.0 / np.sqrt(D_IN))
        b = jax.random.normal(k4, (D_OUT,), dtype=jnp.float32) * 0.01
        return {'x': x, 'edge_index': edge_index, 'W': W, 'b': b}
    _L1_gnn_all = _L1_gnn_setup()
    _L1_gnn_in = {k: v for k, v in _L1_gnn_all.items() if k in ('W', 'b')}
    del _L1_gnn_all

    def _L1_mix_setup():
        import math
        import jax, jax.numpy as jnp
        import numpy as np
        D_MODEL = 1024
        N_HEADS = 16
        D_K = D_MODEL // N_HEADS
        EPS = 1e-06

        def _kernel_feats(data, P):
            norm = 1.0 / math.sqrt(math.sqrt(D_K))
            proj = jnp.einsum('bhnd,fd->bhnf', data * norm, P)
            return jax.nn.relu(proj) + 1e-06
        key = jax.random.key(seed)
        ks = jax.random.split(key, 10)
        B, N = (4, 512)
        s = 1.0 / math.sqrt(D_MODEL)
        inp = {'x': jax.random.normal(ks[0], (B, N, D_MODEL), jnp.float32), 'Wq': jax.random.normal(ks[1], (D_MODEL, D_MODEL), jnp.float32) * s, 'bq': jnp.zeros((D_MODEL,), jnp.float32), 'Wk': jax.random.normal(ks[2], (D_MODEL, D_MODEL), jnp.float32) * s, 'bk': jnp.zeros((D_MODEL,), jnp.float32), 'Wv': jax.random.normal(ks[3], (D_MODEL, D_MODEL), jnp.float32) * s, 'bv': jnp.zeros((D_MODEL,), jnp.float32), 'Wo': jax.random.normal(ks[4], (D_MODEL, D_MODEL), jnp.float32) * s, 'bo': jnp.zeros((D_MODEL,), jnp.float32), 'P': jax.random.normal(ks[5], (D_K, D_K), jnp.float32)}
        return inp
    _L1_mix_all = _L1_mix_setup()
    _L1_mix_in = {k: v for k, v in _L1_mix_all.items() if k in ('Wq', 'bq', 'Wk', 'bk', 'Wv', 'bv', 'Wo', 'bo', 'P')}
    del _L1_mix_all

    def _L1_ffn_setup():
        import jax, jax.numpy as jnp
        import numpy as np
        B, S, H, I, E_ROUTED, TOP_K = (8, 128, 1024, 128, 8, 2)

        def _expert(x, Wg, Wu, Wd):
            return jax.nn.silu(x @ Wg.T) * (x @ Wu.T) @ Wd.T
        key = jax.random.key(seed)
        ks = jax.random.split(key, 9)
        s = 0.02
        return {'x': jax.random.normal(ks[0], (B, S, H), dtype=jnp.float32), 'Wg_s': jax.random.normal(ks[1], (I, H), dtype=jnp.float32) * s, 'Wu_s': jax.random.normal(ks[2], (I, H), dtype=jnp.float32) * s, 'Wd_s': jax.random.normal(ks[3], (H, I), dtype=jnp.float32) * s, 'Wg': jax.random.normal(ks[4], (E_ROUTED, I, H), dtype=jnp.float32) * s, 'Wu': jax.random.normal(ks[5], (E_ROUTED, I, H), dtype=jnp.float32) * s, 'Wd': jax.random.normal(ks[6], (E_ROUTED, H, I), dtype=jnp.float32) * s, 'Wr': jax.random.normal(ks[7], (E_ROUTED, H), dtype=jnp.float32) * s, 'rb': jnp.zeros((E_ROUTED,), dtype=jnp.float32)}
    _L1_ffn_all = _L1_ffn_setup()
    _L1_ffn_in = {k: v for k, v in _L1_ffn_all.items() if k in ('Wg_s', 'Wu_s', 'Wd_s', 'Wg', 'Wu', 'Wd', 'Wr', 'rb')}
    del _L1_ffn_all
    return {'x': x, 'src': src, 'dst': dst, 'edge_type_8': edge_type_8, 'L0_gnn_weight': _L0_gnn_in['weight'], 'L0_gnn_root': _L0_gnn_in['root'], 'L0_gnn_bias': _L0_gnn_in['bias'], 'L0_gnn_w_gate': _L0_gnn_in['w_gate'], 'L0_gnn_b_gate': _L0_gnn_in['b_gate'], 'L0_mix_W_qkv': _L0_mix_in['W_qkv'], 'L0_mix_b_qkv': _L0_mix_in['b_qkv'], 'L0_mix_W_proj': _L0_mix_in['W_proj'], 'L0_mix_b_proj': _L0_mix_in['b_proj'], 'L0_mix_proj_mat': _L0_mix_in['proj_mat'], 'L0_ffn_ln_g': _L0_ffn_in['ln_g'], 'L0_ffn_ln_b': _L0_ffn_in['ln_b'], 'L0_ffn_w1': _L0_ffn_in['w1'], 'L0_ffn_w2': _L0_ffn_in['w2'], 'L1_gnn_W': _L1_gnn_in['W'], 'L1_gnn_b': _L1_gnn_in['b'], 'L1_mix_Wq': _L1_mix_in['Wq'], 'L1_mix_bq': _L1_mix_in['bq'], 'L1_mix_Wk': _L1_mix_in['Wk'], 'L1_mix_bk': _L1_mix_in['bk'], 'L1_mix_Wv': _L1_mix_in['Wv'], 'L1_mix_bv': _L1_mix_in['bv'], 'L1_mix_Wo': _L1_mix_in['Wo'], 'L1_mix_bo': _L1_mix_in['bo'], 'L1_mix_P': _L1_mix_in['P'], 'L1_ffn_Wg_s': _L1_ffn_in['Wg_s'], 'L1_ffn_Wu_s': _L1_ffn_in['Wu_s'], 'L1_ffn_Wd_s': _L1_ffn_in['Wd_s'], 'L1_ffn_Wg': _L1_ffn_in['Wg'], 'L1_ffn_Wu': _L1_ffn_in['Wu'], 'L1_ffn_Wd': _L1_ffn_in['Wd'], 'L1_ffn_Wr': _L1_ffn_in['Wr'], 'L1_ffn_rb': _L1_ffn_in['rb']}

def reference(x, src, dst, edge_type_8, L0_gnn_weight, L0_gnn_root, L0_gnn_bias, L0_gnn_w_gate, L0_gnn_b_gate, L0_mix_W_qkv, L0_mix_b_qkv, L0_mix_W_proj, L0_mix_b_proj, L0_mix_proj_mat, L0_ffn_ln_g, L0_ffn_ln_b, L0_ffn_w1, L0_ffn_w2, L1_gnn_W, L1_gnn_b, L1_mix_Wq, L1_mix_bq, L1_mix_Wk, L1_mix_bk, L1_mix_Wv, L1_mix_bv, L1_mix_Wo, L1_mix_bo, L1_mix_P, L1_ffn_Wg_s, L1_ffn_Wu_s, L1_ffn_Wd_s, L1_ffn_Wg, L1_ffn_Wu, L1_ffn_Wd, L1_ffn_Wr, L1_ffn_rb):
    import jax
    import jax.numpy as jnp

    def _L0_gnn_ref(x, edge_index, edge_type, weight, root, bias, w_gate, b_gate):
        import jax, jax.numpy as jnp
        import numpy as np
        N, D, R, E = (625, 1024, 8, 5000)

        def _rgcn(x, edge_index, edge_type, weight, root, bias):
            src, dst = (edge_index[0], edge_index[1])
            msgs = x[src]
            out = x @ root + bias
            n = x.shape[0]
            for r in range(weight.shape[0]):
                mask = (edge_type == r).astype(x.dtype)
                sums = jax.ops.segment_sum(msgs * mask[:, None], dst, num_segments=n)
                cnt = jax.ops.segment_sum(mask, dst, num_segments=n)
                mean = sums / jnp.maximum(cnt, 1.0)[:, None]
                out = out + mean @ weight[r]
            return out
        u = _rgcn(x, edge_index, edge_type, weight, root, bias)
        z = jnp.concatenate([u, x], axis=1) @ w_gate + b_gate
        h = jnp.tanh(u) * z + x * (1.0 - z)
        return h

    def _L0_mix_ref(x, W_qkv, b_qkv, W_proj, b_proj, proj_mat):
        import jax, jax.numpy as jnp
        import numpy as np
        EMBED_DIM = 1024
        N_HEADS = 16
        HEAD_DIM = EMBED_DIM // N_HEADS
        N_FEATURES = 64
        EPS = 0.0001

        def softmax_kernel(data, projection_matrix, eps=EPS):
            data_normalizer = data.shape[-1] ** (-0.25)
            proj = jnp.einsum('bhnd,fd->bhnf', data, projection_matrix) * data_normalizer
            proj_max = jnp.max(proj, axis=-1, keepdims=True)
            return jnp.exp(proj - proj_max + eps)
        B, N, D = x.shape
        qkv = x @ W_qkv.T + b_qkv
        qkv = qkv.reshape(B, N, 3, N_HEADS, HEAD_DIM)
        qkv = jnp.transpose(qkv, (2, 0, 3, 1, 4))
        q, k, v = (qkv[0], qkv[1], qkv[2])
        q_prime = softmax_kernel(q, proj_mat)
        k_prime = softmax_kernel(k, proj_mat)
        kv = jnp.einsum('bhnf,bhnv->bhfv', k_prime, v)
        out = jnp.einsum('bhnf,bhfv->bhnv', q_prime, kv)
        k_sum = jnp.sum(k_prime, axis=2)
        normalizer = jnp.einsum('bhnf,bhf->bhn', q_prime, k_sum)[..., None]
        out = out / (normalizer + 1e-06)
        out = jnp.transpose(out, (0, 2, 1, 3)).reshape(B, N, D)
        return out @ W_proj.T + b_proj

    def _L0_ffn_ref(x, ln_g, ln_b, w1, w2):
        import jax, jax.numpy as jnp
        import numpy as np
        BIT = 8
        QMAX = 2 ** (BIT - 1) - 1
        QMIN = -2 ** (BIT - 1)
        BOUNDARY_RANGE = 0.005
        EPS = 1e-05

        def _quant_act_int8(x):
            amax = jnp.maximum(jnp.quantile(jnp.abs(x), 1.0 - BOUNDARY_RANGE), EPS)
            s = QMAX / amax
            q = jnp.clip(jnp.round(x * s), QMIN, QMAX) / s
            return x + jax.lax.stop_gradient(q - x)

        def _quant_w_ternary(w):
            gamma = jnp.mean(jnp.abs(w)) + EPS
            q = jnp.clip(jnp.round(w / gamma), -1.0, 1.0) * gamma
            return w + jax.lax.stop_gradient(q - w)

        def _qlinear(x, w):
            xq = _quant_act_int8(x)
            wq = _quant_w_ternary(w)
            return jnp.einsum('btd,hd->bth', xq, wq)

        def _layernorm(x, g, b):
            mu = jnp.mean(x, axis=-1, keepdims=True)
            var = jnp.mean(jnp.square(x - mu), axis=-1, keepdims=True)
            return (x - mu) * jax.lax.rsqrt(var + 1e-05) * g + b
        h = _layernorm(x, ln_g, ln_b)
        h = _qlinear(h, w1)
        h = jax.nn.gelu(h, approximate=False)
        out = _qlinear(h, w2)
        return out

    def _L1_gnn_ref(x, edge_index, W, b):
        import jax, jax.numpy as jnp
        import numpy as np
        N = 1250
        E = 20000
        D_IN = 1024
        D_OUT = 1024
        num_nodes = x.shape[0]
        self_idx = jnp.arange(num_nodes, dtype=edge_index.dtype)
        ei = jnp.concatenate([edge_index, jnp.stack([self_idx, self_idx], axis=0)], axis=1)
        row, col = (ei[0], ei[1])
        h = jnp.einsum('nd,od->no', x, W) + b
        deg = jnp.zeros((num_nodes,), dtype=h.dtype).at[row].add(1.0)
        deg_inv_sqrt = deg ** (-0.5)
        norm = deg_inv_sqrt[row] * deg_inv_sqrt[col]
        msg = norm[:, None] * h[col]
        out = jax.ops.segment_sum(msg, row, num_segments=num_nodes)
        return out

    def _L1_mix_ref(x, Wq, bq, Wk, bk, Wv, bv, Wo, bo, P):
        import math
        import jax, jax.numpy as jnp
        import numpy as np
        D_MODEL = 1024
        N_HEADS = 16
        D_K = D_MODEL // N_HEADS
        EPS = 1e-06

        def _kernel_feats(data, P):
            norm = 1.0 / math.sqrt(math.sqrt(D_K))
            proj = jnp.einsum('bhnd,fd->bhnf', data * norm, P)
            return jax.nn.relu(proj) + 1e-06
        B, N, _ = x.shape
        H, dk = (N_HEADS, D_K)

        def heads(W, b):
            y = x @ W.T + b
            return y.reshape(B, N, H, dk).transpose(0, 2, 1, 3)
        Q, K, V = (heads(Wq, bq), heads(Wk, bk), heads(Wv, bv))
        Qf = _kernel_feats(Q, P)
        Kf = _kernel_feats(K, P)
        KV = jnp.einsum('bhnf,bhnd->bhfd', Kf, V)
        Ksum = Kf.sum(axis=2)
        denom = jnp.einsum('bhnf,bhf->bhn', Qf, Ksum) + EPS
        out = jnp.einsum('bhnf,bhfd->bhnd', Qf, KV) / denom[..., None]
        out = out.transpose(0, 2, 1, 3).reshape(B, N, D_MODEL)
        return out @ Wo.T + bo

    def _L1_ffn_ref(x, Wg_s, Wu_s, Wd_s, Wg, Wu, Wd, Wr, rb):
        import jax, jax.numpy as jnp
        import numpy as np
        B, S, H, I, E_ROUTED, TOP_K = (8, 128, 1024, 128, 8, 2)

        def _expert(x, Wg, Wu, Wd):
            return jax.nn.silu(x @ Wg.T) * (x @ Wu.T) @ Wd.T
        shared = _expert(x, Wg_s, Wu_s, Wd_s)
        logits = jnp.einsum('bsh,eh->bse', x, Wr) + rb
        probs = jax.nn.sigmoid(logits)
        scores, idx = jax.lax.top_k(probs, TOP_K)
        cw = (jax.nn.one_hot(idx, E_ROUTED, dtype=x.dtype) * scores[..., None]).sum(-2)
        out = shared
        for e in range(E_ROUTED):
            out = out + cw[..., e:e + 1] * _expert(x, Wg[e], Wu[e], Wd[e])
        return out
    edge_index = jnp.stack([src, dst])
    xn = _layernorm(x, axis=-1)
    x = x + _L0_gnn_ref(xn, edge_index, edge_type_8, L0_gnn_weight, L0_gnn_root, L0_gnn_bias, L0_gnn_w_gate, L0_gnn_b_gate) + _L0_mix_ref(xn[None], L0_mix_W_qkv, L0_mix_b_qkv, L0_mix_W_proj, L0_mix_b_proj, L0_mix_proj_mat)[0]
    x = x + _L0_ffn_ref(_layernorm(x, axis=-1)[None], L0_ffn_ln_g, L0_ffn_ln_b, L0_ffn_w1, L0_ffn_w2)[0]
    xn = _layernorm(x, axis=-1)
    x = x + _L1_gnn_ref(xn, edge_index, L1_gnn_W, L1_gnn_b) + _L1_mix_ref(xn[None], L1_mix_Wq, L1_mix_bq, L1_mix_Wk, L1_mix_bk, L1_mix_Wv, L1_mix_bv, L1_mix_Wo, L1_mix_bo, L1_mix_P)[0]
    x = x + _L1_ffn_ref(_layernorm(x, axis=-1)[None], L1_ffn_Wg_s, L1_ffn_Wu_s, L1_ffn_Wd_s, L1_ffn_Wg, L1_ffn_Wu, L1_ffn_Wd, L1_ffn_Wr, L1_ffn_rb)[0]
    return x

_drawn_inputs = setup_inputs


def setup_inputs(seed=0):
    import zlib

    import numpy as np

    out = dict(_drawn_inputs(seed))
    spreads = {'L0_gnn_bias': (0.0, 0.1),
     'L0_gnn_b_gate': (0.0, 0.1),
     'L0_ffn_ln_g': (1.0, 0.6),
     'L0_ffn_ln_b': (0.0, 0.74),
     'L1_mix_bq': (0.0, 0.8),
     'L1_mix_bk': (0.0, 0.8),
     'L1_mix_bv': (0.0, 0.1),
     'L1_mix_bo': (0.0, 0.1),
     'L1_ffn_rb': (0.0, 0.8)}
    factors = {'L0_mix_W_qkv': 8.0,
     'L0_mix_b_qkv': 8.0,
     'L0_mix_W_proj': 8.0,
     'L0_mix_b_proj': 7.859,
     'L0_mix_proj_mat': 8.0,
     'L1_gnn_b': 8.0,
     'L1_mix_Wq': 8.0,
     'L1_mix_Wk': 8.0,
     'L1_mix_Wv': 2.73,
     'L1_mix_P': 8.0,
     'L1_ffn_Wg': 3.352,
     'L1_ffn_Wu': 3.225,
     'L1_ffn_Wd': 3.21,
     'L1_ffn_Wr': 3.755}
    for name, (base, spread) in spreads.items():
        noise = np.random.default_rng([zlib.crc32(name.encode()), seed]).standard_normal(out[name].shape)
        drawn = base * np.exp(spread * noise) if base else spread * noise
        out[name] = jnp.asarray(drawn.astype(out[name].dtype))
    for name, factor in factors.items():
        out[name] = (out[name] * factor).astype(out[name].dtype)
    return out
```

```python
import numpy as np
import concourse.bass as bass
from concourse import mybir
from concourse.alu_op_type import AluOpType as ALU

F32 = mybir.dt.float32
F32R = mybir.dt.float32r
F16 = mybir.dt.float16
BF16 = mybir.dt.bfloat16
I32 = mybir.dt.int32
I16 = mybir.dt.int16
ACT = mybir.ActivationFunctionType
AX = mybir.AxisListType

NODES, D = 625, 1024
P, T = 125, 5
KT = D // 128
REL = 8
EDGES, EC = 20625, 165
NBUCKET = REL * T
GROUP = 256
NGROUP = (EDGES + NBUCKET * (GROUP - 1)) // GROUP
NCHUNK = 2 * NGROUP
HEADS2 = 8
NEXP = 8
HID = 128
FFN0 = 256
NP2 = 626
C1, C2 = 500, 125
H0, H1 = 313, 312

G_PRE0 = 10
G_PROJ = 2
G_REL = 2 * REL
G_GATE = 2
G_PRE1 = 8
G_UP = 4
C_TAIL = 4 + 2 * (NEXP + 1)
NSTREAM = KT * (G_PRE0 + G_PROJ + G_REL + G_GATE + G_PRE1 + G_PROJ + G_UP) + C_TAIL
NST = 4
NSL = 8
B_PRE0, B_PROJ0, B_PRE1, B_PROJ1, NBIAS = 0, 10, 12, 20, 22


def build(nc, a, out):
    PE, DVE, ALE, POOL, SP = nc.tensor, nc.vector, nc.scalar, nc.gpsimd, nc.sync

    sems = {}

    def S(name):
        if name not in sems:
            sems[name] = nc.alloc_semaphore(name)
        return sems[name]

    place = [nc.sbuf_base + (-nc.sbuf_base) % 64]

    def region(size):
        o = place[0]
        place[0] += size + (-size) % 64
        assert place[0] <= nc.sbuf_usable_end, place[0]
        return o

    def at(name, shape, dt, offset):
        return nc.alloc_sbuf_tensor_at(name, shape, dt, offset=offset)

    R_STREAM = region(NST * 2048 + 2 * NSL * 2048)
    R_XT = region(2 * KT * NP2 * 4)
    R_A = region(50176)
    R_XN = region(2 * T * D * 2)
    R_NAT = region(T * D * 4)
    R_RING = region(T * 2048)
    R_EXTRA = region(20480)
    R_CONST = region(6144)
    R_SMALL = region(1536)

    w_stage = at("w_stage", [128, NST, 512], F32, R_STREAM)
    w_hi = at("w_hi", [128, NSL, 512], F32R, R_STREAM + NST * 2048)
    w_lo = at("w_lo", [128, NSL, 512], F32R, R_STREAM + NST * 2048 + NSL * 2048)
    xt_hi = at("xt_hi", [128, KT, NP2], F32R, R_XT)
    xt_lo = at("xt_lo", [128, KT, NP2], F32R, R_XT + KT * NP2 * 4)
    xn_hi = at("xn_hi", [P, T, D], F16, R_XN)
    xn_lo = at("xn_lo", [P, T, D], F16, R_XN + T * D * 2)
    nat = at("nat", [P, T, D], F32, R_NAT)
    ring = at("ring", [P, T, 512], F32, R_RING)
    ps = nc.alloc_psum_tensor("ps", [128, 8, 512], F32)

    cpl = [R_CONST]

    def const(name, shape, dt):
        o = cpl[0]
        n = int(np.prod(shape[1:])) * mybir.dt.size(dt)
        cpl[0] += n + (-n) % 32
        assert cpl[0] <= R_CONST + 6144
        return at(name, shape, dt, o)

    ident = const("ident", [128, 128], F32)
    ident16 = const("ident16", [128, 128], BF16)
    iota_i = const("iota_i", [128, NP2], I16)
    iota16 = const("iota16", [128, NP2], F16)
    iota1_16 = const("iota1_16", [128, NP2], F16)
    ones16 = const("ones16", [128, 128], F16)
    ones = const("ones", [128, 128], F32)
    zero = const("zero", [128, 1], F32)
    ltri = const("ltri", [128, 128], F32)
    spl = [R_SMALL]

    def small(name, shape, dt):
        o = spl[0]
        n = int(np.prod(shape[1:])) * mybir.dt.size(dt)
        spl[0] += n + (-n) % 32
        assert spl[0] <= R_SMALL + 1536, name
        return at(name, shape, dt, o)

    stats = small("stats", [P, T, 2, 6], F32)
    mv = small("mv", [P, T, 2], F32)
    va = small("va", [P, T], F32)
    rs = small("rs", [P, T], F32)
    t5 = small("t5", [P, T], F32)
    dis = small("dis", [P, T], F32)
    flag = small("flag", [128, 1], F32)
    flag_i = small("flag_i", [128, 1], I32)
    gam = small("gam", [128, 2], F32)
    rgam = small("rgam", [128, 2], F32)
    qcur = small("qcur", [128, 1], I32)
    qbit = small("qbit", [128, 1], I32)
    qcand = small("qcand", [128, 1], I32)
    qcnt = small("qcnt", [128, 1], F32)
    qok = small("qok", [128, 1], I32)
    qs = small("qs", [128, 1], F32)
    qrs = small("qrs", [128, 1], F32)

    pre = nc.dram_tensor("pre", [G_PRE0, T, P, 512], F32, kind="Internal").ap()
    x1p = nc.dram_tensor("x1p", [P, T * D], F32, kind="Internal").ap()
    c_dram = nc.dram_tensor("c_dram", [P, T * NODES], F32, kind="Internal").ap()

    lanes = {"pe": PE, "dve": DVE, "act": ALE}
    phase_no = [0]

    def meet():
        phase_no[0] += 1
        for n, e in lanes.items():
            e.drain().then_inc(S("ph_" + n), 1)
        for n, e in lanes.items():
            for o in lanes:
                if o != n:
                    e.wait_ge(S("ph_" + o), phase_no[0])

    seq = {}

    def nxt(name, by=1):
        seq[name] = seq.get(name, 0) + by
        return seq[name]

    def sig(ins, name):
        ins.then_inc(S(name), 1)
        return (name, nxt(name))

    def dma(dst, src, name, eng=None):
        (eng or ALE).dma_start(dst, src).then_inc(S(name), 16)
        return (name, nxt(name, 16))

    def dma_after(mark, dst, src, name):
        ALE.wait_ge(S(mark[0]), mark[1])
        return dma(dst, src, name)

    def wait(eng, *marks):
        for name, v in marks:
            eng.wait_ge(S(name), v)

    stream = a["stream"]
    def load_chunk(c, q):
        SP.wait_ge(S("split_done"), c + 1)
        SP.dma_start(w_stage[:, q % NST, :],
                     stream[bass.ds(c, 1)].rearrange("a p f -> p (a f)")).then_inc(S(f"landed{q % NST}"), 16)

    nloop = NSTREAM // NSL
    with SP.Fori(0, nloop) as i:
        for q in range(NSL):
            load_chunk(i * NSL + q, q)
    for q in range(NSTREAM - nloop * NSL):
        load_chunk(nloop * NSL + q, q)

    POOL.iota(iota_i[:], pattern=[[1, NP2]], base=0, channel_multiplier=0)
    POOL.memset(ident[:], 0.0)
    POOL.memset(ones[:], 1.0)
    POOL.memset(zero[:], 0.0)
    POOL.drain()
    POOL.affine_select(out=ident[:], in_=ident[:], compare_op=ALU.not_equal, fill=1.0, base=0,
                       pattern=[[-1, 128]], channel_multiplier=1)
    POOL.affine_select(out=ltri[:], in_=ones[:], compare_op=ALU.is_gt, fill=0.0, base=0,
                       pattern=[[1, 128]], channel_multiplier=-1)
    POOL.drain().then_inc(S("consts"), 1)

    POOL.sem_inc(S("split_done"), NST)

    def split_chunk(c, q, turn):
        POOL.wait_ge(S(f"landed{q % NST}"), 16 * turn)
        POOL.wait_ge(S("w_used"), c + 1)
        POOL.tensor_tensor(w_hi[:, q, :], w_stage[:, q % NST, :], zero[:].to_broadcast([128, 512]),
                           ALU.add).then_inc(S("hi_done"), 1)
        POOL.wait_ge(S("hi_done"), c + 1)
        POOL.tensor_tensor(w_lo[:, q, :], w_stage[:, q % NST, :], w_hi[:, q, :].bitcast(F32),
                           ALU.subtract).then_inc(S("split_done"), 1)

    with POOL.Fori(0, nloop) as i:
        for q in range(NSL):
            split_chunk(i * NSL + q, q, 2 * i + q // NST + 1)
    for q in range(NSTREAM - nloop * NSL):
        split_chunk(nloop * NSL + q, q, 2 * nloop + q // NST + 1)

    PE.sem_inc(S("w_used"), NSL)

    DVE.wait_ge(S("consts"), 1)
    DVE.tensor_copy(iota16[:], iota_i[:])
    DVE.tensor_scalar(iota1_16[:], iota_i[:], 1.0, None, ALU.add)
    DVE.tensor_copy(ident16[:], ident[:])
    DVE.memset(ones16[:], 1.0)

    done = {"chunks": 0, "groups": 0}
    DVE.sem_inc(S("bank_free"), T)

    def ln(src, dst):
        for m in range(T):
            for h in range(2):
                DVE.bn_stats(stats[:, m, h, :], src[:, m, h * 512:(h + 1) * 512])
        DVE.drain()
        for m in range(T):
            DVE.bn_aggr(mv[:, m, :], stats[:, m, :, :])
        DVE.drain()
        DVE.tensor_scalar(va[:], mv[:, :, 1], 1e-5, None, ALU.add)
        mk = sig(DVE.drain(), "dve_step")
        wait(ALE, mk)
        mk = sig(ALE.activation(t5[:], va[:], ACT.Sqrt), "act_step")
        wait(DVE, mk)
        newton_rsqrt()
        for m in range(T):
            DVE.tensor_scalar(dst[:, m, :], src[:, m, :], mv[:, m, 0:1], rs[:, m:m + 1],
                              ALU.subtract, ALU.mult)
        DVE.drain()

    def newton_rsqrt():
        DVE.reciprocal(rs[:], t5[:])
        DVE.drain()
        DVE.tensor_tensor(t5[:], rs[:], rs[:], ALU.mult)
        DVE.drain()
        DVE.tensor_tensor(t5[:], t5[:], va[:], ALU.mult)
        DVE.drain()
        DVE.tensor_scalar(t5[:], t5[:], -0.5, 1.5, ALU.mult, ALU.add)
        DVE.drain()
        DVE.tensor_tensor(rs[:], rs[:], t5[:], ALU.mult)
        DVE.drain()

    def transpose_split(src, width, nk, hi, lo):
        free = []
        for k in range(nk):
            b = 2 * (k % 4)
            if k >= 4:
                wait(PE, free[k - 4])
            for m in range(T):
                dst = ps[0:width, b, m * P:(m + 1) * P] if m < 4 else ps[0:width, b + 1, 0:P]
                t_ = PE.transpose(dst, src[:, m, k * width:(k + 1) * width], ident[0:P, 0:P])
            mk = sig(t_, "tr_full")
            wait(ALE, mk)
            ALE.activation(hi[0:width, k, 0:C1], ps[0:width, b, 0:C1], ACT.Copy)
            mk = sig(ALE.activation(hi[0:width, k, C1:NODES], ps[0:width, b + 1, 0:C2], ACT.Copy), "tr_hi")
            wait(DVE, mk)
            DVE.tensor_tensor(lo[0:width, k, 0:C1], ps[0:width, b, 0:C1],
                              hi[0:width, k, 0:C1].bitcast(F32), ALU.subtract)
            free.append(sig(DVE.tensor_tensor(lo[0:width, k, C1:NODES], ps[0:width, b + 1, 0:C2],
                                              hi[0:width, k, C1:NODES].bitcast(F32), ALU.subtract), "tr_lo"))

    def three(dst, l_hi, l_lo, r_hi, r_lo, first, last):
        PE.matmul(dst, l_hi, r_hi, start=first, stop=False)
        PE.matmul(dst, l_hi, r_lo, start=False, stop=False)
        return PE.matmul(dst, l_lo, r_hi, start=False, stop=last)

    def dense_pe(g, c0, g0, extra_wait=None):
        for k in range(KT):
            if extra_wait:
                extra_wait(k)
            PE.wait_ge(S("split_done"), NST + c0 + g * KT + k + 1)
            for m in range(T):
                if k == 0:
                    PE.wait_ge(S("bank_free"), (g + g0) * T + m + 1)
                last = three(ps[0:P, m, :], xt_hi[:, k, m * P:(m + 1) * P], xt_lo[:, k, m * P:(m + 1) * P],
                             w_hi[:, k, :], w_lo[:, k, :], k == 0, k == KT - 1)
                if m == T - 1:
                    last.then_inc(S("w_used"), 1)
                elif k == KT - 1:
                    last.then_inc(S("bank_full"), 1)

    def wait_bank(eng, g, m, c0, g0):
        if m < T - 1:
            eng.wait_ge(S("bank_full"), (g + g0) * (T - 1) + m + 1)
        else:
            eng.wait_ge(S("w_used"), NSL + c0 + (g + 1) * KT)

    def dense_to_pre(groups, bias0):
        c0, g0 = done["chunks"], done["groups"]
        tag = f"pre{g0}"
        with PE.Fori(0, groups) as g:
            dense_pe(g, c0, g0)
        bias_t = at("bias_" + tag, [P, 512], F32, R_EXTRA)
        for m in range(T):
            ALE.sem_inc(S(f"st{tag}_{m}"), 16)
        with ALE.Fori(0, groups) as g:
            ALE.wait_ge(S("bank_free"), (g + g0) * T + T)
            ALE.dma_start(bias_t[:], a["bias"][bass.ds(g + bias0, 1), :].to_broadcast([P, 512])).then_inc(S("b" + tag), 16)
            for m in range(T):
                ALE.wait_ge(S("bank_free"), (g + g0 + 1) * T + m + 1)
                ALE.dma_start(pre[bass.ds(g, 1), m].rearrange("a p f -> p (a f)"), ring[:, m, :]).then_inc(S(f"st{tag}_{m}"), 16)
        with DVE.Fori(0, groups) as g:
            DVE.wait_ge(S("b" + tag), 16 * g + 16)
            for m in range(T):
                wait_bank(DVE, g, m, c0, g0)
                DVE.wait_ge(S(f"st{tag}_{m}"), 16 * g + 16)
                DVE.tensor_tensor(ring[:, m, :], ps[0:P, m, :], bias_t[:], ALU.add).then_inc(S("bank_free"), 1)
        for m in range(T):
            ALE.wait_ge(S(f"st{tag}_{m}"), 16 * groups + 16)
        done["chunks"] += groups * KT
        done["groups"] += groups

    def dense_add(acc, bias0, name, extra_wait=None):
        c0, g0 = done["chunks"], done["groups"]
        if bias0 is not None:
            bias_t = at("bias_" + name, [P, 2, 512], F32, R_RING)
            mk = dma(bias_t[:], a["bias"][bias0:bias0 + 2, :].rearrange("(o g) f -> o g f", o=1).to_broadcast([P, 2, 512]),
                     "ld_" + name)
        for g in range(2):
            dense_pe(g, c0, g0)
            for m in range(T):
                wait_bank(DVE, g, m, c0, g0)
                o = acc[:, m, g * 512:(g + 1) * 512]
                DVE.tensor_tensor(o, o, ps[0:P, m, :], ALU.add).then_inc(S("bank_free"), 1)
        if bias0 is not None:
            wait(DVE, mk)
            DVE.drain()
            for g in range(2):
                for m in range(T):
                    o = acc[:, m, g * 512:(g + 1) * 512]
                    DVE.tensor_tensor(o, o, bias_t[:, g, :], ALU.add)
        DVE.drain()
        done["chunks"] += 2 * KT
        done["groups"] += 2

    def attention(layer, group0, pmt):
        tag = f"at{layer}_"
        o = [R_XT]

        def tmp(name, shape, dt=F32):
            n = int(np.prod(shape[1:])) * 4
            p_ = o[0]
            o[0] += n + (-n) % 64
            assert o[0] <= R_XT + 2 * KT * NP2 * 4
            return at(tag + name, shape, dt, p_)

        qk = [tmp(f"qk{i}", [P, 2, T, 128]) for i in range(2)]
        vx = [tmp(f"vx{i}", [P, T, 130]) for i in range(2)]
        qt = tmp("qt", [128, 2, NODES])
        ft = tmp("ft", [P, 2, T, 128])
        qft = tmp("qft", [128, NODES])
        kv = tmp("kv", [128, 130])
        bd = tmp("bd", [128, 128])
        mx = tmp("mx", [P, 2, 2 * T])
        den = tmp("den", [P, T, 2])
        eps_t = tmp("eps", [P, 1])
        DVE.memset(kv[:], 0.0)
        DVE.memset(bd[:], 0.0)
        DVE.memset(eps_t[:], 1e-4)
        for i in range(2):
            DVE.memset(vx[i][:, :, 128:130], 1.0)
        mk = sig(DVE.drain(), "dve_step")
        wait(ALE, mk)
        dma(bd[0:64, 0:64], pmt, tag + "bd")
        mk_bd = dma(bd[64:128, 64:128], pmt, tag + "bd")
        scale = 64.0 ** -0.25
        loads, freed = {}, {}

        def load(h):
            b = h % 2
            if h >= 2:
                wait(ALE, freed[h - 2])
            for i, dst in enumerate((qk[b][:, 0], qk[b][:, 1], vx[b][:, :, 0:128])):
                g = group0 + 2 * i + h // 4
                c = (h % 4) * 128
                loads[h] = dma(dst, pre[g, :, :, c:c + 128].rearrange("t p f -> p t f"), tag + f"ld{b}")

        load(0)
        for h in range(HEADS2):
            b = h % 2
            if h + 1 < HEADS2:
                load(h + 1)
            wait(PE, loads[h])
            for i in range(2):
                for m in range(T):
                    dst = ps[:, 2 * i, m * P:(m + 1) * P] if m < 4 else ps[:, 2 * i + 1, 0:P]
                    t_ = PE.transpose(dst, qk[b][:, i, m, :], ident[0:P, 0:P])
                mk = sig(t_, tag + "pe")
                eng = (DVE, ALE)[i]
                wait(eng, mk)
                sc = scale if layer else 1.0
                if i == 0:
                    DVE.tensor_scalar(qt[:, 0, 0:C1], ps[:, 0, 0:C1], sc, None, ALU.mult)
                    mq = sig(DVE.tensor_scalar(qt[:, 0, C1:NODES], ps[:, 1, 0:C2], sc, None, ALU.mult), tag + "dve")
                else:
                    ALE.activation(qt[:, 1, 0:C1], ps[:, 2, 0:C1], ACT.Copy, scale=sc)
                    mkk = sig(ALE.activation(qt[:, 1, C1:NODES], ps[:, 3, 0:C2], ACT.Copy, scale=sc), tag + "act")
            wait(PE, mq, mkk, mk_bd)
            for i in range(2):
                for m in range(T):
                    dst = ps[0:P, 4 + i, m * 128:(m + 1) * 128] if m < 4 else ps[0:P, 6, i * 128:(i + 1) * 128]
                    t_ = PE.matmul(dst, qt[:, i, m * P:(m + 1) * P], bd[:], start=True, stop=True)
            mk = sig(t_, tag + "pe")
            wait(DVE, mk)
            fview = ft[:].rearrange("p i t f -> p (i t) f")
            if layer:
                for i in range(2):
                    DVE.tensor_scalar(ft[:, i, 0:4, :], ps[0:P, 4 + i, :].rearrange("p (t f) -> p t f", t=4), 0.0, 1e-6,
                                      ALU.max, ALU.add)
                mf = sig(DVE.tensor_scalar(ft[:, :, 4, :], ps[0:P, 6, 0:256].rearrange("p (i f) -> p i f", i=2), 0.0, 1e-6,
                                           ALU.max, ALU.add), tag + "dve")
            else:
                for i in range(2):
                    DVE.tensor_reduce(mx[:, i, 0:8], ps[0:P, 4 + i, :].rearrange("p (t f) -> p t f", f=64), AX.X, ALU.max)
                DVE.tensor_reduce(mx[:, :, 8:10], ps[0:P, 6, 0:256].rearrange("p (i t f) -> p i t f", i=2, f=64), AX.X, ALU.max)
                DVE.drain()
                for i in range(2):
                    DVE.tensor_tensor(ft[:, i, 0:4, :].rearrange("p t (s f) -> p (t s) f", s=2),
                                      ps[0:P, 4 + i, :].rearrange("p (t f) -> p t f", f=64),
                                      mx[:, i, 0:8].unsqueeze(2).to_broadcast([P, 8, 64]), ALU.subtract)
                mf = sig(DVE.tensor_tensor(ft[:, :, 4, :].rearrange("p i (s f) -> p i s f", s=2),
                                           ps[0:P, 6, 0:256].rearrange("p (i s f) -> p i s f", i=2, f=64),
                                           mx[:, :, 8:10].unsqueeze(3).to_broadcast([P, 2, 2, 64]), ALU.subtract),
                         tag + "dve")
                wait(ALE, mf)
                mf = sig(ALE.activation(fview, fview, ACT.Exp, scale=scale, bias=eps_t[:]), tag + "act")
            wait(PE, mf)
            for m in range(T):
                dst = ps[:, 0, m * P:(m + 1) * P] if m < 4 else ps[:, 1, 0:P]
                t_ = PE.transpose(dst, ft[:, 0, m, :], ident[0:P, 0:P])
            mk = sig(t_, tag + "pe")
            wait(ALE, mk)
            ALE.activation(qft[:, 0:C1], ps[:, 0, 0:C1], ACT.Copy)
            mq = sig(ALE.activation(qft[:, C1:NODES], ps[:, 1, 0:C2], ACT.Copy), tag + "act")
            for m in range(T):
                t_ = PE.matmul(ps[:, 7, 0:130], ft[:, 1, m, :], vx[b][:, m, :], start=(m == 0), stop=(m == T - 1))
            mk = sig(t_, tag + "pe")
            freed[h] = mk
            wait(DVE, mk)
            for s in range(2):
                r = slice(64 * s, 64 * s + 64)
                DVE.tensor_copy(kv[r, 64 * s:64 * s + 64], ps[r, 7, 64 * s:64 * s + 64])
                DVE.tensor_copy(kv[r, 128 + s:129 + s], ps[r, 7, 128:129])
            mkv = sig(DVE.drain(), tag + "dve")
            wait(PE, mq, mkv)
            for m in range(T):
                t_ = PE.matmul(ps[0:P, 2 + m // 3, 130 * (m % 3):130 * (m % 3) + 130], qft[:, m * P:(m + 1) * P], kv[:],
                               start=True, stop=True)
            mk = sig(t_, tag + "pe")
            wait(DVE, mk)
            for bk, m0, n in ((2, 0, 3), (3, 3, 2)):
                v_ = ps[0:P, bk, 0:130 * n].rearrange("p (t f) -> p t f", f=130)
                DVE.tensor_scalar(den[:, m0:m0 + n, :], v_[:, :, 128:130], 1e-6, None, ALU.add)
            DVE.drain()
            DVE.reciprocal(den[:], den[:])
            DVE.drain()
            for bk, m0, n in ((2, 0, 3), (3, 3, 2)):
                v_ = ps[0:P, bk, 0:130 * n].rearrange("p (t f) -> p t f", f=130)
                DVE.tensor_tensor(nat[:, m0:m0 + n, h * 128:(h + 1) * 128].rearrange("p t (s f) -> p t s f", s=2),
                                  v_[:, :, 0:128].rearrange("p t (s f) -> p t s f", s=2),
                                  den[:, m0:m0 + n, :].unsqueeze(3).to_broadcast([P, n, 2, 64]), ALU.mult)
            mk = sig(DVE.drain(), tag + "dve")
            wait(PE, mk)

    mk = dma(nat[:], a["x"].rearrange("(t p) d -> p t d", p=P), "ld_x")
    wait(DVE, mk)
    ln(nat, nat)
    DVE.tensor_copy(xn_hi[:], nat[:])
    DVE.drain()
    DVE.tensor_tensor(xn_lo[:], nat[:], xn_hi[:], ALU.subtract)
    meet()
    transpose_split(nat, 128, KT, xt_hi, xt_lo)
    meet()
    dense_to_pre(G_PRE0, B_PRE0)
    meet()

    adj = at("adj", [P, T, NBUCKET * P], I16, R_A)
    o_ = [R_XT]

    def tmp(name, shape, dt, base=None):
        n = int(np.prod(shape[1:])) * mybir.dt.size(dt)
        p_ = o_[0]
        o_[0] += n + (-n) % 64
        assert o_[0] <= R_XT + 2 * KT * NP2 * 4, name
        return at(name, shape, dt, p_)

    scan = tmp("scan", [P, NBUCKET, EC], F32)
    key_hot = at("key_hot", [P, NBUCKET, EC], BF16, R_EXTRA)
    ed_src = tmp("ed_src", [P, EC], I32)
    ed_dst = tmp("ed_dst", [P, EC], I32)
    ed_typ = tmp("ed_typ", [P, EC], I32)
    e_tile = at("e_tile", [P, EC], F32, R_RING)
    e_key = at("e_key", [P, EC], F32, R_RING + 704)
    e_src1 = at("e_src1", [P, EC], F32, R_RING + 2 * 704)
    e_dl1 = at("e_dl1", [P, EC], F32, R_RING + 3 * 704)
    e_pos = at("e_pos", [P, EC], F32, R_RING + 4 * 704)
    e_posi = at("e_posi", [P, EC], I32, R_RING + 5 * 704)
    e_tmpi = at("e_tmpi", [P, EC], I32, R_RING + 6 * 704)
    e_lo = at("e_lo", [P, EC], F32, R_RING + 7 * 704)
    e_hi = at("e_hi", [P, EC], F32, R_RING + 8 * 704)
    b_tot = tmp("b_tot", [P, NBUCKET], F32)
    b_beg = tmp("b_beg", [P, NBUCKET], F32)
    b_off = tmp("b_off", [P, NBUCKET], F32)
    b_grp = tmp("b_grp", [128, NBUCKET], F32)
    b_grpi = tmp("b_grpi", [128, NBUCKET], I32)
    b_cum = tmp("b_cum", [128, NBUCKET], F32)
    gcol = tmp("gcol", [1, NGROUP], F32)
    goff = tmp("goff", [1, NGROUP], I32)

    for nm, dst in (("src", ed_src), ("dst", ed_dst), ("typ", ed_typ)):
        mk = dma(dst[:], a[nm].rearrange("(p c) -> p c", c=EC), "ld_edges")
    DVE.memset(adj[:], 0.0)
    wait(DVE, mk)
    DVE.tensor_scalar(e_tile[:], ed_dst[:], float(P), None, ALU.is_ge)
    DVE.tensor_scalar(e_src1[:], ed_src[:], 1.0, None, ALU.add)
    DVE.drain()
    for j in range(2, T):
        DVE.tensor_scalar(e_key[:], ed_dst[:], float(j * P), None, ALU.is_ge)
        DVE.drain()
        DVE.tensor_tensor(e_tile[:], e_tile[:], e_key[:], ALU.add)
        DVE.drain()
    DVE.tensor_scalar(e_dl1[:], e_tile[:], -float(P), 1.0, ALU.mult, ALU.add)
    DVE.tensor_scalar(e_key[:], ed_typ[:], float(T), None, ALU.mult)
    DVE.drain()
    DVE.tensor_tensor(e_dl1[:], e_dl1[:], ed_dst[:], ALU.add)
    DVE.tensor_tensor(e_key[:], e_key[:], e_tile[:], ALU.add)
    DVE.drain()
    DVE.tensor_tensor(key_hot[:], e_key[:].unsqueeze(1).to_broadcast([P, NBUCKET, EC]),
                      iota16[0:P, 0:NBUCKET].unsqueeze(2).to_broadcast([P, NBUCKET, EC]), ALU.is_equal)
    DVE.drain()
    kh = key_hot[:].rearrange("p b c -> p (b c)")
    DVE.tensor_tensor_scan(scan[:].rearrange("p b c -> p (b c)"), kh, kh, 0.0, ALU.add, ALU.max)
    DVE.drain()
    DVE.memset(b_beg[:, 0:1], 0.0)
    DVE.tensor_copy(b_beg[:, 1:NBUCKET], scan[:, 0:NBUCKET - 1, EC - 1])
    DVE.drain()
    DVE.tensor_tensor(b_tot[:], scan[:, :, EC - 1], b_beg[:], ALU.subtract)
    mk = sig(DVE.drain(), "dve_step")
    wait(PE, mk)
    PE.matmul(ps[0:P, 0, 0:NBUCKET], ltri[0:P, 0:P], b_tot[:], start=True, stop=True)
    mk = sig(PE.matmul(ps[:, 1, 0:NBUCKET], ones[0:P, :], b_tot[:], start=True, stop=True), "pe_step")
    wait(DVE, mk)
    DVE.tensor_scalar(b_grp[:], ps[:, 1, 0:NBUCKET], GROUP / 2 - 0.75, 1.0 / GROUP, ALU.add, ALU.mult)
    DVE.drain()
    DVE.tensor_copy(b_grpi[:], b_grp[:])
    DVE.drain()
    DVE.tensor_copy(b_grp[:], b_grpi[:])
    DVE.drain()
    DVE.tensor_tensor_scan(b_cum[:], b_grp[:], b_grp[:], 0.0, ALU.add, ALU.max)
    DVE.drain()
    DVE.tensor_tensor(b_cum[:], b_cum[:], b_grp[:], ALU.subtract)
    DVE.drain()
    DVE.tensor_scalar(b_off[:], b_cum[0:P, :], float(GROUP), -1.0, ALU.mult, ALU.add)
    DVE.drain()
    DVE.tensor_tensor(b_off[:], b_off[:], ps[0:P, 0, 0:NBUCKET], ALU.add)
    DVE.drain()
    DVE.tensor_tensor(b_off[:], b_off[:], b_beg[:], ALU.subtract)
    DVE.drain()
    DVE.tensor_tensor(scan[:], scan[:], b_off[:].unsqueeze(2).to_broadcast([P, NBUCKET, EC]), ALU.add)
    DVE.drain()
    DVE.tensor_tensor(scan[:], scan[:], key_hot[:], ALU.mult)
    DVE.drain()
    DVE.tensor_reduce(e_pos[:], scan[:].rearrange("p b c -> p c b"), AX.X, ALU.add)
    DVE.drain()
    DVE.tensor_copy(e_posi[:], e_pos[:])
    DVE.drain()
    DVE.tensor_scalar(e_tmpi[:], e_posi[:], 7, None, ALU.logical_shift_right)
    DVE.drain()
    DVE.tensor_copy(e_hi[:], e_tmpi[:])
    DVE.drain()
    DVE.tensor_scalar(e_tmpi[:], e_posi[:], 127, None, ALU.bitwise_and)
    DVE.drain()
    DVE.tensor_copy(e_lo[:], e_tmpi[:])
    gb = at("gb", [1, NGROUP, NBUCKET], F32, R_EXTRA)
    DVE.drain()
    DVE.tensor_tensor(gb[:], b_cum[0:1, :].unsqueeze(1).to_broadcast([1, NGROUP, NBUCKET]),
                      iota16[0:1, 0:NGROUP].unsqueeze(2).to_broadcast([1, NGROUP, NBUCKET]), ALU.is_le)
    DVE.drain()
    DVE.tensor_reduce(gcol[:], gb[:], AX.X, ALU.add)
    DVE.drain()
    DVE.tensor_scalar(goff[:], gcol[:], float(P), -float(P), ALU.mult, ALU.add)
    DVE.drain()

    hot_lo = [at(f"hot_lo{i}", [P, 128], F16, R_EXTRA + i * 2048) for i in range(3)]
    hot_hi = [at(f"hot_hi{i}", [P, 2, NCHUNK], F16, R_EXTRA + i * 2048 + 512) for i in range(3)]
    slot = at("slot", [128, 2, NCHUNK], F32, R_EXTRA + 3 * 2048)
    DVE.drain()

    with DVE.Fori(0, EC // 3) as i:
        for j in range(3):
            c = i * 3 + j
            DVE.wait_ge(S("sc_pe"), c + 1)
            DVE.tensor_scalar(hot_lo[j][:], iota16[0:P, 0:128], e_lo[:, bass.ds(c, 1)], None, ALU.is_equal)
            DVE.tensor_scalar(hot_hi[j][:, 0, :], iota16[0:P, 0:NCHUNK], e_hi[:, bass.ds(c, 1)],
                              e_src1[:, bass.ds(c, 1)], ALU.is_equal, ALU.mult)
            DVE.tensor_scalar(hot_hi[j][:, 1, :], iota16[0:P, 0:NCHUNK], e_hi[:, bass.ds(c, 1)],
                              e_dl1[:, bass.ds(c, 1)], ALU.is_equal, ALU.mult).then_inc(S("sc_dve"), 1)
    zero16 = at("zero16", [P, 128], F16, R_EXTRA + 6 * 2048 + 1024)
    DVE.memset(zero16[:], 0.0)
    DVE.drain()
    PE.sem_inc(S("sc_pe"), 3)
    slot_ps = ps[:, 0, 0:2 * NCHUNK]

    def scatter(c, j, first, last):
        PE.wait_ge(S("sc_dve"), c + 1)
        PE.matmul(slot_ps, hot_lo[j][:], hot_hi[j][:].rearrange("p a c -> p (a c)"), start=first,
                  stop=last).then_inc(S("sc_pe"), 1)

    for j in range(3):
        scatter(j, j, j == 0, False)
    with PE.Fori(1, EC // 3 - 1) as i:
        for j in range(3):
            scatter(i * 3 + j, j, False, False)
    for j in range(3):
        scatter(EC - 3 + j, j, False, j == 2)
    DVE.wait_ge(S("sc_pe"), 3 + EC)
    DVE.tensor_copy(slot[:].rearrange("p a c -> p (a c)"), slot_ps)
    DVE.drain()

    hot_s = [at(f"hot_s{i}", [128, NODES], F16, R_XT + i * 1280) for i in range(4)]
    hot_d = [at(f"hot_d{i}", [128, P], F16, R_XT + 4 * 1280 + i * 256) for i in range(4)]
    DVE.sem_inc(S("hi_add"), 4)
    with DVE.Fori(0, NGROUP // 2) as i:
        for gg in range(2):
            for j in range(2):
                q = 2 * gg + j
                c = i * 4 + q
                DVE.wait_ge(S("hi_pe"), c + 1)
                DVE.tensor_scalar(hot_s[q][:], iota1_16[:, 0:NODES], slot[:, 0, bass.ds(c, 1)], None, ALU.is_equal)
                DVE.tensor_scalar(hot_d[q][:], iota1_16[:, 0:P], slot[:, 1, bass.ds(c, 1)], None,
                                  ALU.is_equal).then_inc(S("hi_dve"), 1)
            g = i * 2 + gg
            off = DVE.value_load(goff[0:1, bass.ds(g, 1)], min_val=0, max_val=(NBUCKET - 1) * P)
            DVE.wait_ge(S("hi_pe"), 4 + 2 * g + 2)
            DVE.wait_ge(S("hi_add"), 4 + 2 * g)
            a0 = adj[:, 0:4, bass.ds(off, P)]
            DVE.tensor_tensor(a0, a0, ps[0:P, 2 * gg, 0:C1].rearrange("p (t d) -> p t d", t=4), ALU.add).then_inc(S("hi_add"), 1)
            a1 = adj[:, 4, bass.ds(off, P)]
            DVE.tensor_tensor(a1, a1, ps[0:P, 2 * gg + 1, 0:P], ALU.add).then_inc(S("hi_add"), 1)
    PE.sem_inc(S("hi_pe"), 4)
    with PE.Fori(0, NGROUP // 2) as i:
        for gg in range(2):
            for j in range(2):
                q = 2 * gg + j
                c = i * 4 + q
                PE.wait_ge(S("hi_dve"), c + 1)
                if j == 0:
                    PE.wait_ge(S("hi_add"), 2 * (i * 2 + gg) + 2)
                for m in range(T):
                    dst = ps[0:P, 2 * gg, m * P:(m + 1) * P] if m < 4 else ps[0:P, 2 * gg + 1, 0:P]
                    t_ = PE.matmul(dst, hot_s[q][:, m * P:(m + 1) * P], hot_d[q][:], start=(j == 0 and m in (0, 4)),
                                   stop=(j == 1), skip_group_check=True)
                t_.then_inc(S("hi_pe"), 1)
    meet()

    mxa = at("mxa", [P, 1], F32, R_RING)
    mxt = at("mxt", [1, P], F32, R_RING + 64)
    DVE.tensor_reduce(mxa[:], adj[:].rearrange("p t c -> p (t c)"), AX.X, ALU.max)
    DVE.tensor_copy(flag[:], ones[:, 0:1])
    mk = sig(DVE.drain(), "dve_step")
    wait(PE, mk)
    mk = sig(PE.transpose(ps[0:1, 0, 0:P], mxa[:], ident[0:P, 0:P]), "pe_step")
    wait(DVE, mk)
    DVE.tensor_reduce(mxt[:, 0:1], ps[0:1, 0, 0:P], AX.X, ALU.max)
    DVE.drain()
    DVE.tensor_scalar(flag_i[0:1, :], mxt[:, 0:1], 2048.0, None, ALU.is_gt)
    meet()

    attention(0, 4, a["pm0"])
    meet()
    transpose_split(nat, 128, KT, xt_hi, xt_lo)
    x_res = at("x_res", [P, T, D], F32, R_EXTRA)
    mk = dma(x_res[:], a["x"].rearrange("(t p) d -> p t d", p=P), "ld_x2")
    meet()
    wait(DVE, mk)
    dense_add(x_res, B_PROJ0, "proj0")
    meet()
    mk = dma(x1p[:], x_res[:].rearrange("p t d -> p (t d)"), "st_x1p")
    wait(ALE, mk)

    for g in range(2):
        mk = dma(nat[:, :, g * 512:(g + 1) * 512], pre[g].rearrange("t p f -> p t f"), "ld_u")
    meet()
    wait(DVE, mk)
    a_hi = at("a_hi", [P, T, NODES], F16, R_EXTRA)
    a_lo = at("a_lo", [P, T, NODES], F16, R_EXTRA + 6272)
    rcnt = at("rcnt", [128, NP2], F32, R_EXTRA + 2 * 6272)
    mtmp = [at(f"mtmp{i}", [128, H0], F32, R_EXTRA + 2 * 6272 + 2560 + i * 1280) for i in range(4)]
    halves = ((0, H0), (H0, H1))
    c0, g0 = done["chunks"], done["groups"]
    many = PE.value_load(flag_i[0:1, 0:1], min_val=0, max_val=1)
    DVE.sem_inc(S("ag_free"), 3)
    DVE.sem_inc(S("mt_ready"), 1)
    PE.sem_inc(S("ag_full"), 1)
    with PE.Fori(0, REL) as r:
        PE.wait_ge(S("a_ready"), r + 1)
        for i in range(18):
            bank = 5 + i % 3
            h0, hn = halves[i % 2]
            PE.wait_ge(S("ag_free"), r * 18 + i + 1)
            if i < 2:
                for lo in range(2):
                    for t in range(T):
                        t_ = PE.matmul(ps[:, bank, 0:hn], ones16[0:P, :], (a_hi, a_lo)[lo][:, t, h0:h0 + hn],
                                       start=(lo == 0 and t == 0), stop=(lo == 1 and t == T - 1))
                t_.then_inc(S("ag_full"), 1)
                continue
            k = i // 2 - 1
            dst = ps[:, bank, 0:hn]

            def agg(x16, a16, t, first, last):
                return PE.matmul(dst, x16[:, t, k * 128:(k + 1) * 128], a16[:, t, h0:h0 + hn], start=first, stop=last)

            for t in range(T):
                agg(xn_hi, a_hi, t, t == 0, False)
            with PE.If(many):
                for t in range(T):
                    agg(xn_hi, a_lo, t, False, False)
                    agg(xn_lo, a_lo, t, False, False)
            for t in range(T):
                t_ = agg(xn_lo, a_hi, t, False, t == T - 1)
            t_.then_inc(S("ag_full"), 1)

        for gg in range(2):
            def mean_ready(k):
                if gg == 0:
                    PE.wait_ge(S("mt_ready"), 1 + r * 16 + 2 * k + 2)
            dense_pe(r * 2 + gg, c0, g0, mean_ready)
    with ALE.Fori(0, REL) as r:
        for i in range(2, 18):
            h0, hn = halves[i % 2]
            j = i - 2
            ALE.wait_ge(S("ag_scaled"), r * 16 + j + 1)
            ALE.activation(xt_hi[:, j // 2, h0:h0 + hn], mtmp[j % 4][:, 0:hn], ACT.Copy).then_inc(S("mt_hi"), 1)
    with DVE.Fori(0, REL) as r:
        DVE.wait_ge(S("ag_full"), r * 18 + 1)
        DVE.tensor_copy(a_hi[:], adj[:, :, bass.ds(r * NODES, NODES)]).then_inc(S("a_hi"), 1)
        DVE.wait_ge(S("a_hi"), r + 1)
        DVE.tensor_tensor(a_lo[:], adj[:, :, bass.ds(r * NODES, NODES)], a_hi[:], ALU.subtract).then_inc(S("a_ready"), 1)
        for i in range(2):
            h0, hn = halves[i]
            DVE.wait_ge(S("ag_full"), r * 18 + i + 2)
            DVE.tensor_scalar(rcnt[:, h0:h0 + hn], ps[:, 5 + i, 0:hn], 1.0, None, ALU.max).then_inc(S("ag_free"), 1)
        DVE.wait_ge(S("ag_free"), 3 + r * 18 + 2)
        DVE.reciprocal(rcnt[:, 0:NODES], rcnt[:, 0:NODES]).then_inc(S("rcnt"), 1)
        DVE.wait_ge(S("rcnt"), r + 1)

        def low(j):
            h0, hn = halves[j % 2]
            DVE.wait_ge(S("mt_hi"), r * 16 + j + 1)
            DVE.tensor_tensor(xt_lo[:, j // 2, h0:h0 + hn], mtmp[j % 4][:, 0:hn],
                              xt_hi[:, j // 2, h0:h0 + hn].bitcast(F32), ALU.subtract).then_inc(S("mt_ready"), 1)

        for j in range(16):
            i = j + 2
            h0, hn = halves[i % 2]
            DVE.wait_ge(S("ag_full"), r * 18 + i + 2)
            if j >= 4:
                DVE.wait_ge(S("mt_ready"), 1 + r * 16 + j - 3)
            else:
                DVE.wait_ge(S("mt_ready"), 1 + r * 16)
            DVE.tensor_tensor(mtmp[j % 4][:, 0:hn], ps[:, 5 + i % 3, 0:hn], rcnt[:, h0:h0 + hn],
                              ALU.mult).then_inc(S("ag_free"), 1)
            DVE.wait_ge(S("ag_free"), 3 + r * 18 + i + 1)
            DVE.sem_inc(S("ag_scaled"), 1)
            if j >= 1:
                low(j - 1)
        low(15)
        for gg in range(2):
            for m in range(T):
                wait_bank(DVE, r * 2 + gg, m, c0, g0)
                u_ = nat[:, m, gg * 512:(gg + 1) * 512]
                DVE.wait_ge(S("bank_free"), (r * 2 + g0) * T + T)
                DVE.tensor_tensor(u_, u_, ps[0:P, m, :], ALU.add).then_inc(S("bank_free"), 1)
    done["chunks"] += REL * 2 * KT
    done["groups"] += REL * 2
    meet()

    c_all = at("c_all", [P, T, NODES], F32, R_EXTRA)
    DVE.tensor_reduce(c_all[:], adj[:].rearrange("p t (r d) -> p t d r", r=REL), AX.X, ALU.add)
    DVE.drain()
    DVE.tensor_reduce(va[:], c_all[:], AX.X, ALU.add)
    DVE.drain()
    DVE.tensor_scalar(va[:], va[:], 1.0, None, ALU.add)
    mk = sig(DVE.drain(), "dve_step")
    mc = dma_after(mk, c_dram[:], c_all[:].rearrange("p t d -> p (t d)"), "st_c")
    mk = sig(ALE.activation(t5[:], va[:], ACT.Sqrt), "act_step")
    wait(DVE, mk)
    newton_rsqrt()
    DVE.tensor_copy(dis[:], rs[:])
    wait(ALE, mc)
    meet()

    transpose_split(nat, 128, KT, xt_hi, xt_lo)
    z = at("z", [P, T, D], F32, R_A)
    x1 = at("x1", [P, T, D], F32, R_A + T * D * 4)
    for g in range(2):
        mk = dma(z[:, :, g * 512:(g + 1) * 512], pre[2 + g].rearrange("t p f -> p t f"), "ld_z")
    mx1 = dma(x1[:].rearrange("p t d -> p (t d)"), x1p[:], "ld_x1")
    meet()
    for m in range(T):
        ALE.activation(nat[:, m, :], nat[:, m, :], ACT.Tanh)
    wait(DVE, mk)
    dense_add(z, None, "gate")
    meet()
    wait(DVE, mx1)
    xnf = at("xnf", [P, T, D], F32, R_EXTRA)
    for m in range(T):
        DVE.tensor_tensor(xnf[:, m, :], xn_hi[:, m, :], xn_lo[:, m, :], ALU.add)
    DVE.drain()
    for m in range(T):
        DVE.tensor_tensor(nat[:, m, :], nat[:, m, :], xnf[:, m, :], ALU.subtract)
        DVE.tensor_tensor(x1[:, m, :], x1[:, m, :], xnf[:, m, :], ALU.add)
    DVE.drain()
    for m in range(T):
        DVE.tensor_tensor(z[:, m, :], z[:, m, :], nat[:, m, :], ALU.mult)
    DVE.drain()
    for m in range(T):
        DVE.tensor_tensor(x1[:, m, :], x1[:, m, :], z[:, m, :], ALU.add)
    DVE.drain()

    w1 = at("w1", [128, KT, FFN0], F32, R_XT)
    w2 = at("w2", [128, FFN0 // 128, D], F32, R_XT + 8192)
    w1q = at("w1q", [128, KT, FFN0], BF16, R_XT + 16384)
    w2q = at("w2q", [128, FFN0 // 128, D], BF16, R_XT + 20480)
    wt_ = at("wt_", [128, 2048], F32, R_XT + 24576)
    gsum = small("gsum", [128, 2], F32)
    meet()
    mk = dma(w1[:], a["w1t"], "ld_w12")
    mk = dma(w2[:], a["w2t"], "ld_w12")
    wait(DVE, mk)
    for i, w in enumerate((w1, w2)):
        DVE.tensor_reduce(gsum[:, i:i + 1], w[:].rearrange("p k f -> p (k f)"), AX.X, ALU.add, apply_absolute_value=True)
    mk = sig(DVE.drain(), "dve_step")
    wait(PE, mk)
    mk = sig(PE.matmul(ps[:, 0, 0:2], ones[:], gsum[:], start=True, stop=True), "pe_step")
    wait(DVE, mk)
    DVE.tensor_scalar(gam[:], ps[:, 0, 0:2], 1.0 / (FFN0 * D), 1e-5, ALU.mult, ALU.add)
    DVE.drain()
    DVE.reciprocal(rgam[:], gam[:])
    DVE.drain()
    MAGIC = 1.5 * 2.0 ** 23
    for i, (w, wq) in enumerate(((w1, w1q), (w2, w2q))):
        DVE.tensor_scalar(wt_[:], w[:].rearrange("p k f -> p (k f)"), rgam[:, i:i + 1], 1.0, ALU.mult, ALU.min)
        DVE.drain()
        DVE.tensor_scalar(wt_[:], wt_[:], -1.0, MAGIC, ALU.max, ALU.add)
        DVE.drain()
        DVE.tensor_scalar(wq[:].rearrange("p k f -> p (k f)"), wt_[:], MAGIC, None, ALU.subtract)
        DVE.drain()

    def quantise(h, width, rank, hq, scratch):
        hf = h[:].rearrange("p t d -> p (t d)")
        sf = scratch[:].rearrange("p t d -> p (t d)")
        mk = sig(DVE.drain(), "dve_step")
        wait(ALE, mk)
        mk = sig(ALE.activation(sf, hf, ACT.Abs), "act_step")
        DVE.memset(qcur[:], 0)
        DVE.memset(qbit[:], 1 << 30)
        cmp_ = at(f"cmp{width}", [P, T * width], BF16, R_EXTRA)
        cntp = small(f"cntp{width}", [P, 1], F32)
        wait(DVE, mk)
        DVE.drain()
        tag = f"q{width}"
        with PE.Fori(0, 31) as i:
            PE.wait_ge(S(tag + "_cnt"), i + 1)
            PE.matmul(ps[:, 0, 0:1], ones[0:P, :], cntp[:], start=True, stop=True).then_inc(S(tag + "_sum"), 1)
        with DVE.Fori(0, 31) as i:
            DVE.tensor_tensor(qcand[:], qcur[:], qbit[:], ALU.bitwise_or)
            DVE.drain()
            DVE.tensor_scalar(cmp_[:], sf, qcand[0:P, :].bitcast(F32), None, ALU.is_ge, ALU.add,
                              accum_out=cntp[:])
            DVE.drain().then_inc(S(tag + "_cnt"), 1)
            DVE.wait_ge(S(tag + "_sum"), i + 1)
            DVE.tensor_scalar(qok[:], ps[:, 0, 0:1], float(rank), None, ALU.is_ge)
            DVE.tensor_scalar(qbit[:], qbit[:], 1, None, ALU.logical_shift_right)
            DVE.drain()
            DVE.copy_predicated(qcur[:], qok[:], qcand[:])
            DVE.drain()
        DVE.tensor_scalar(qs[:], qcur[:].bitcast(F32), 1e-5, None, ALU.max)
        DVE.drain()
        DVE.tensor_scalar(qrs[:], qs[:], 1.0 / 127.0, None, ALU.mult)
        DVE.reciprocal(qs[:], qs[:])
        DVE.drain()
        DVE.tensor_scalar(qs[:], qs[:], 127.0, None, ALU.mult)
        DVE.drain()
        DVE.tensor_scalar(sf, hf, qs[0:P, :], 127.0, ALU.mult, ALU.min)
        DVE.drain()
        DVE.tensor_scalar(sf, sf, -128.0, MAGIC, ALU.max, ALU.add)
        DVE.drain()
        DVE.tensor_scalar(hq[:].rearrange("p t d -> p (t d)"), sf, MAGIC, None, ALU.subtract)
        DVE.drain()

    ps16 = ps[:].bitcast(BF16)

    def transpose16(src, nk, dst):
        free = []
        for k in range(nk):
            b = k % 4
            if k >= 4:
                wait(PE, free[k - 4])
            for m in range(T):
                t_ = PE.transpose(ps16[:, b, m * 128:m * 128 + P], src[:, m, k * 128:(k + 1) * 128], ident16[0:P, 0:P])
            mk = sig(t_, "tr_full")
            wait(DVE, mk)
            free.append(sig(DVE.tensor_copy(dst[:, k, :].rearrange("p (t n) -> p t n", t=T),
                                            ps16[:, b, 0:T * 128].rearrange("p (t n) -> p t n", t=T)[:, :, 0:P]), "tr_lo"))

    lng = at("lng", [P, D], F32, R_RING)
    lnb = at("lnb", [P, D], F32, R_RING + 4096)
    mk = dma(lng[:], a["ln_g"].to_broadcast([P, D]), "ld_ln")
    mk = dma(lnb[:], a["ln_b"].to_broadcast([P, D]), "ld_ln")
    ln(x1, nat)
    ln(nat, nat)
    wait(DVE, mk)
    for m in range(T):
        DVE.tensor_tensor(nat[:, m, :], nat[:, m, :], lng[:], ALU.mult)
    DVE.drain()
    for m in range(T):
        DVE.tensor_tensor(nat[:, m, :], nat[:, m, :], lnb[:], ALU.add)
    habs = at("habs", [P, T, D], F32, R_XN)
    hq = at("hq", [P, T, D], BF16, R_EXTRA + 10240)
    hqt = at("hqt", [128, KT, NODES], BF16, R_A)
    quantise(nat, D, 3201, hq, habs)
    meet()
    transpose16(hq, KT, hqt)
    meet()
    for m in range(T):
        for k in range(KT):
            t_ = PE.matmul(ps[0:P, m, 0:FFN0], hqt[:, k, m * P:(m + 1) * P], w1q[:, k, :], start=(k == 0), stop=(k == KT - 1))
    mk = sig(t_, "pe_step")
    gl = at("gl", [P, T, FFN0], F32, R_NAT)
    gabs = at("gabs", [P, T, FFN0], F32, R_NAT + 5120)
    glq = at("glq", [P, T, FFN0], BF16, R_EXTRA + 10240)
    glt = at("glt", [128, FFN0 // 128, NODES], BF16, R_A)
    DVE.tensor_tensor(qrs[:], qrs[:], gam[:, 0:1], ALU.mult)
    DVE.drain()
    wait(DVE, mk)
    mk = sig(DVE.tensor_scalar(gl[:], ps[0:P, 0:T, 0:FFN0], qrs[0:P, :], None, ALU.mult), "dve_step")
    wait(ALE, mk)
    mk = sig(ALE.activation(gl[:], gl[:], ACT.Gelu), "act_step")
    wait(DVE, mk)
    meet()
    quantise(gl, FFN0, 801, glq, gabs)
    meet()
    transpose16(glq, FFN0 // 128, glt)
    meet()
    DVE.tensor_tensor(qrs[:], qrs[:], gam[:, 1:2], ALU.mult)
    DVE.drain()
    free = []
    for n in range(2 * T):
        m, h = n // 2, n % 2
        if n >= 8:
            wait(PE, free[n - 8])
        for k in range(FFN0 // 128):
            t_ = PE.matmul(ps[0:P, n % 8, :], glt[:, k, m * P:(m + 1) * P], w2q[:, k, h * 512:(h + 1) * 512], start=(k == 0),
                           stop=(k == FFN0 // 128 - 1))
        mk = sig(t_, "pe_step")
        wait(DVE, mk)
        o = x1[:, m, h * 512:(h + 1) * 512]
        free.append(sig(DVE.scalar_tensor_tensor(o, ps[0:P, n % 8, :], qrs[0:P, :], o, ALU.mult, ALU.add), "dve_step"))
    DVE.drain()
    meet()

    ln(x1, nat)
    meet()
    transpose_split(nat, 128, KT, xt_hi, xt_lo)
    meet()
    dense_to_pre(G_PRE1, B_PRE1)
    meet()
    ct_hi = at("ct_hi", [P, T, NP2], F32R, R_XT)
    ct_lo = at("ct_lo", [P, T, NP2], F32R, R_XT + 12544)
    c_nat = at("c_nat", [P, T, NODES], F32, R_XT + 2 * 12544)
    hp_hi = at("hp_hi", [P, T, D], F32R, R_XN)
    hp_lo = at("hp_lo", [P, T, D], F32R, R_EXTRA)
    mc = dma(c_nat[:].rearrange("p t d -> p (t d)"), c_dram[:], "ld_c")
    for g in range(2):
        mk = dma(nat[:, :, g * 512:(g + 1) * 512], pre[g].rearrange("t p f -> p t f"), "ld_h")
    wait(PE, mc)
    transpose_split(c_nat, P, T, ct_hi, ct_lo)
    wait(DVE, mk)
    for m in range(T):
        DVE.tensor_scalar(nat[:, m, :], nat[:, m, :], dis[:, m:m + 1], None, ALU.mult)
    DVE.drain()
    DVE.tensor_copy(hp_hi[:], nat[:])
    DVE.drain()
    DVE.tensor_tensor(hp_lo[:], nat[:], hp_hi[:].bitcast(F32), ALU.subtract)
    meet()
    free = []
    for n in range(2 * T):
        m, h = n // 2, n % 2
        if n >= 8:
            wait(PE, free[n - 8])
        for k in range(T):
            t_ = three(ps[0:P, n % 8, :], ct_hi[:, k, m * P:(m + 1) * P], ct_lo[:, k, m * P:(m + 1) * P],
                       hp_hi[:, k, h * 512:(h + 1) * 512], hp_lo[:, k, h * 512:(h + 1) * 512], k == 0, k == T - 1)
        mk = sig(t_, "pe_step")
        wait(DVE, mk)
        o = nat[:, m, h * 512:(h + 1) * 512]
        free.append(sig(DVE.tensor_tensor(o, ps[0:P, n % 8, :], o, ALU.add), "dve_step"))
    DVE.drain()
    for m in range(T):
        DVE.scalar_tensor_tensor(x1[:, m, :], nat[:, m, :], dis[:, m:m + 1], x1[:, m, :], ALU.mult, ALU.add)
    DVE.drain()
    meet()
    attention(1, 2, a["pm1"])
    meet()
    transpose_split(nat, 128, KT, xt_hi, xt_lo)
    meet()
    dense_add(x1, B_PROJ1, "proj1")
    meet()

    ln(x1, nat)
    meet()
    transpose_split(nat, 128, KT, xt_hi, xt_lo)
    wr = at("wr", [128, KT, NEXP], F32, R_RING)
    wr_hi = at("wr_hi", [128, KT, NEXP], F32R, R_RING + 256)
    wr_lo = at("wr_lo", [128, KT, NEXP], F32R, R_RING + 512)
    rb = at("rb", [P, NEXP], F32, R_RING + 768)
    pr = at("pr", [P, T, NEXP], F32, R_RING + 1024)
    cw = at("cw", [P, T, NEXP], F32, R_RING + 1280)
    gt = at("gt", [P, T, NEXP, NEXP], F32, R_RING + 1536)
    eq = at("eq", [P, T, NEXP, NEXP], F32, R_RING + 1536 + 1280)
    sil = [at(f"sil{i}", [P, 2, HID], F32, R_RING + 4608 + i * 1024) for i in range(4)]
    mk = dma(wr[:], a["wrt"], "ld_wr")
    mk = dma(rb[:], a["rb"].to_broadcast([P, NEXP]), "ld_wr")
    wait(DVE, mk)
    DVE.tensor_copy(wr_hi[:], wr[:])
    DVE.drain()
    DVE.tensor_tensor(wr_lo[:], wr[:], wr_hi[:].bitcast(F32), ALU.subtract)
    meet()
    for m in range(T):
        for k in range(KT):
            t_ = three(ps[0:P, 5, m * NEXP:(m + 1) * NEXP], xt_hi[:, k, m * P:(m + 1) * P], xt_lo[:, k, m * P:(m + 1) * P],
                       wr_hi[:, k, :], wr_lo[:, k, :], k == 0, k == KT - 1)
    mk = sig(t_, "pe_step")
    wait(DVE, mk)
    DVE.tensor_tensor(pr[:], ps[0:P, 5, 0:T * NEXP].rearrange("p (t e) -> p t e", t=T),
                      rb[:].unsqueeze(1).to_broadcast([P, T, NEXP]), ALU.add)
    mk = sig(DVE.drain(), "dve_step")
    wait(ALE, mk)
    mk = sig(ALE.activation(pr[:], pr[:], ACT.Sigmoid), "act_step")
    wait(DVE, mk)
    pj = pr[:].unsqueeze(2).to_broadcast([P, T, NEXP, NEXP])
    pe_ = pr[:].unsqueeze(3).to_broadcast([P, T, NEXP, NEXP])
    DVE.tensor_tensor(gt[:], pj, pe_, ALU.is_gt)
    DVE.tensor_tensor(eq[:], pj, pe_, ALU.is_equal)
    low = at("low", [P, NEXP, NEXP], F32, R_RING + 1536 + 2560)
    DVE.memset(low[:], 0.0)
    DVE.drain()
    for e in range(1, NEXP):
        DVE.memset(low[:, e, 0:e], 1.0)
    DVE.drain()
    DVE.tensor_tensor(eq[:], eq[:], low[:].unsqueeze(1).to_broadcast([P, T, NEXP, NEXP]), ALU.mult)
    DVE.drain()
    DVE.tensor_tensor(gt[:], gt[:], eq[:], ALU.add)
    DVE.drain()
    DVE.tensor_reduce(cw[:], gt[:], AX.X, ALU.add)
    DVE.drain()
    DVE.tensor_scalar(cw[:], cw[:], 2.0, None, ALU.is_lt)
    DVE.drain()
    DVE.tensor_tensor(cw[:], cw[:], pr[:], ALU.mult)
    DVE.drain()

    hid = at("hid", [P, T, (NEXP + 1) * HID], F32, R_XN)
    meet()
    c0, g0 = done["chunks"], done["groups"]
    with PE.Fori(0, G_UP) as g:
        dense_pe(g, c0, g0)
    n_sil = 0
    for g in range(G_UP + 1):
        experts = 2 if g < G_UP else 1
        if g == G_UP:
            for c in range(4):
                PE.wait_ge(S("split_done"), NST + c0 + g * KT + c + 1)
                for m in range(T):
                    if c == 0:
                        PE.wait_ge(S("bank_free"), (g + g0) * T + m + 1)
                    for kk in range(2):
                        k = 2 * c + kk
                        t_ = three(ps[0:P, m, 0:2 * HID], xt_hi[:, k, m * P:(m + 1) * P], xt_lo[:, k, m * P:(m + 1) * P],
                                   w_hi[:, c, kk * 256:kk * 256 + 256], w_lo[:, c, kk * 256:kk * 256 + 256],
                                   k == 0, k == KT - 1)
                    if m == T - 1:
                        t_.then_inc(S("w_used"), 1)
                    elif c == 3:
                        t_.then_inc(S("bank_full"), 1)
        for m in range(T):
            s_ = sil[n_sil % 4]
            blocks = ps[0:P, m, 0:256 * experts].rearrange("p (e w h) -> p e w h", w=2, h=HID)
            for eng in (ALE, DVE):
                if m < T - 1:
                    eng.wait_ge(S("bank_full"), (g + g0) * (T - 1) + m + 1)
                else:
                    eng.wait_ge(S("w_used"), NSL + c0 + (g * KT + KT if g < G_UP else g * KT + 4))
            if n_sil >= 4:
                ALE.wait_ge(S("sil_used"), n_sil - 3)
            mk = sig(ALE.activation(s_[:, 0:experts, :], blocks[:, :, 0, :], ACT.Silu), "sil_done")
            wait(DVE, mk)
            if experts == 2:
                for j in range(2):
                    e = 2 * g + j
                    t_ = DVE.scalar_tensor_tensor(hid[:, m, e * HID:(e + 1) * HID], s_[:, j, :], cw[:, m, e:e + 1],
                                                  blocks[:, j, 1, :], ALU.mult, ALU.mult)
            else:
                t_ = DVE.tensor_tensor(hid[:, m, NEXP * HID:], s_[:, 0, :], blocks[:, 0, 1, :], ALU.mult)
            t_.then_inc(S("bank_free"), 1)
            DVE.wait_ge(S("bank_free"), (g + g0 + 1) * T + m + 1)
            DVE.sem_inc(S("sil_used"), 1)
            n_sil += 1
    done["chunks"] += G_UP * KT + 4
    done["groups"] += G_UP + 1
    meet()
    ht_hi = at("ht_hi", [128, NEXP + 1, NP2], F32R, R_XT)
    ht_lo = at("ht_lo", [128, NEXP + 1, NP2], F32R, R_XT + 22592)
    transpose_split(hid, 128, NEXP + 1, ht_hi, ht_lo)
    meet()
    c0, g0 = done["chunks"], done["groups"]
    y = out.rearrange("(t p) d -> t p d", p=P)
    for h in range(2):
        for e in range(NEXP + 1):
            c = c0 + h * (NEXP + 1) + e
            q = c % NSL
            PE.wait_ge(S("split_done"), NST + c + 1)
            for m in range(T):
                if e == 0:
                    PE.wait_ge(S("bank_free"), (h + g0) * T + m + 1)
                t_ = three(ps[0:P, m, :], ht_hi[:, e, m * P:(m + 1) * P], ht_lo[:, e, m * P:(m + 1) * P],
                           w_hi[:, q, :], w_lo[:, q, :], e == 0, e == NEXP)
                if m == T - 1:
                    t_.then_inc(S("w_used"), 1)
                elif e == NEXP:
                    t_.then_inc(S("bank_full"), 1)
        for m in range(T):
            if m < T - 1:
                DVE.wait_ge(S("bank_full"), (h + g0) * (T - 1) + m + 1)
            else:
                DVE.wait_ge(S("w_used"), NSL + c0 + (h + 1) * (NEXP + 1))
            o = x1[:, m, h * 512:(h + 1) * 512]
            DVE.tensor_tensor(o, o, ps[0:P, m, :], ALU.add).then_inc(S("bank_free"), 1)
            ALE.wait_ge(S("bank_free"), (h + g0 + 1) * T + m + 1)
            mk = dma(y[m, :, h * 512:(h + 1) * 512], o, "st_out")
    wait(ALE, mk)


def kernel(**inputs):
    from concourse import bacc
    from concourse.bass_utils import run_bass_kernel_spmd

    v = {k: np.asarray(x) for k, x in inputs.items()}

    def chunks(wt):
        n = wt.shape[1] // 512
        return wt.reshape(KT, 128, n, 512).transpose(2, 0, 1, 3).reshape(n * KT, 128, 512)

    gate = v["L0_gnn_w_gate"]
    ups = np.stack([v["L1_ffn_Wg"], v["L1_ffn_Wu"]], axis=1).reshape(NEXP * 2 * HID, D).T
    shared = np.concatenate([v["L1_ffn_Wg_s"], v["L1_ffn_Wu_s"]], axis=0).T
    shared = shared.reshape(4, 2, 128, 2 * HID).transpose(0, 2, 1, 3).reshape(4, 128, 512)
    downs = np.concatenate([v["L1_ffn_Wd"], v["L1_ffn_Wd_s"][None]], axis=0)
    downs = downs.transpose(0, 2, 1).reshape(NEXP + 1, 128, 2, 512).transpose(2, 0, 1, 3).reshape(-1, 128, 512)
    stream = np.concatenate(
        [chunks(v["L0_gnn_root"]), chunks(gate[D:]), chunks(v["L0_mix_W_qkv"].T), chunks(v["L0_mix_W_proj"].T)]
        + [chunks(v["L0_gnn_weight"][r]) for r in range(REL)]
        + [chunks(gate[:D])]
        + [chunks(v[n].T) for n in ("L1_gnn_W", "L1_mix_Wq", "L1_mix_Wk", "L1_mix_Wv", "L1_mix_Wo")]
        + [chunks(ups), shared, downs])
    bias = np.concatenate([v[n] for n in ("L0_gnn_bias", "L0_gnn_b_gate", "L0_mix_b_qkv", "L0_mix_b_proj", "L1_gnn_b",
                                          "L1_mix_bq", "L1_mix_bk", "L1_mix_bv", "L1_mix_bo")]).reshape(NBIAS, 512)
    arrays = {
        "stream": stream, "bias": bias, "x": v["x"], "src": v["src"], "dst": v["dst"], "typ": v["edge_type_8"],
        "pm0": v["L0_mix_proj_mat"].T, "pm1": v["L1_mix_P"].T, "ln_g": v["L0_ffn_ln_g"][None], "ln_b": v["L0_ffn_ln_b"][None],
        "w1t": v["L0_ffn_w1"].T.reshape(KT, 128, FFN0).transpose(1, 0, 2),
        "w2t": v["L0_ffn_w2"].T.reshape(FFN0 // 128, 128, D).transpose(1, 0, 2),
        "wrt": v["L1_ffn_Wr"].T.reshape(KT, 128, NEXP).transpose(1, 0, 2), "rb": v["L1_ffn_rb"][None],
    }
    nc = bacc.Bacc("TRN2", target_bir_lowering=False, num_devices=1)
    feed, aps = {}, {}
    for k, x in arrays.items():
        feed["in_" + k] = np.ascontiguousarray(x)
        aps[k] = nc.dram_tensor("in_" + k, x.shape, mybir.dt.from_np(x.dtype), kind="ExternalInput").ap()
    out = nc.dram_tensor("out_x", [NODES, D], F32, kind="ExternalOutput").ap()
    build(nc, aps, out)
    r = run_bass_kernel_spmd(nc, [feed], core_ids=[0])
    return r.results[0]["out_x"]
```

```python
import numpy as np
import concourse.bass as bass
from concourse import mybir
from concourse.alu_op_type import AluOpType as ALU

F32 = mybir.dt.float32
F32R = mybir.dt.float32r
F16 = mybir.dt.float16
BF16 = mybir.dt.bfloat16
I32 = mybir.dt.int32
I16 = mybir.dt.int16
U16 = mybir.dt.uint16
ACT = mybir.ActivationFunctionType
AX = mybir.AxisListType

NODES, D = 625, 1024
P, T = 125, 5
KT = D // 128
REL = 8
EDGES, EC = 20625, 165
NBUCKET = REL * T
GROUP = 256
NGROUP = (EDGES + NBUCKET * (GROUP - 1)) // GROUP
NCHUNK = 2 * NGROUP
HEADS2 = 8
NEXP = 8
HID = 128
FFN0 = 256
NP2 = 626
C1, C2 = 500, 125
H0, H1 = 313, 312

G_PRE0 = 10
G_PROJ = 2
G_REL = 2 * REL
G_GATE = 2
G_PRE1 = 8
G_UP = 4
C_TAIL = 4 + 2 * (NEXP + 1)
NSTREAM = KT * (G_PRE0 + G_PROJ + G_REL + G_GATE + G_PRE1 + G_PROJ + G_UP) + C_TAIL
NST = 4
NSL = 8
B_PRE0, B_PROJ0, B_PRE1, B_PROJ1, NBIAS = 0, 10, 12, 20, 22


def build(nc, a, out):
    PE, DVE, ALE, POOL, SP = nc.tensor, nc.vector, nc.scalar, nc.gpsimd, nc.sync

    sems = {}

    def S(name):
        if name not in sems:
            sems[name] = nc.alloc_semaphore(name)
        return sems[name]

    place = [nc.sbuf_base + (-nc.sbuf_base) % 64]

    def region(size):
        o = place[0]
        place[0] += size + (-size) % 64
        assert place[0] <= nc.sbuf_usable_end, place[0]
        return o

    def at(name, shape, dt, offset):
        return nc.alloc_sbuf_tensor_at(name, shape, dt, offset=offset)

    R_STREAM = region(NST * 2048 + 2 * NSL * 2048)
    R_XT = region(2 * KT * NP2 * 4)
    R_A = region(50176)
    R_XN = region(2 * T * D * 2)
    R_NAT = region(T * D * 4)
    R_RING = region(T * 2048)
    R_EXTRA = region(20480)
    R_CONST = region(6144)
    R_SMALL = region(2560)

    w_stage = at("w_stage", [128, NST, 512], F32, R_STREAM)
    w_hi = at("w_hi", [128, NSL, 512], F32R, R_STREAM + NST * 2048)
    w_lo = at("w_lo", [128, NSL, 512], F32R, R_STREAM + NST * 2048 + NSL * 2048)
    xt_hi = at("xt_hi", [128, KT, NP2], F32R, R_XT)
    xt_lo = at("xt_lo", [128, KT, NP2], F32R, R_XT + KT * NP2 * 4)
    xn_hi = at("xn_hi", [P, T, D], F16, R_XN)
    xn_lo = at("xn_lo", [P, T, D], F16, R_XN + T * D * 2)
    nat = at("nat", [P, T, D], F32, R_NAT)
    ring = at("ring", [P, T, 512], F32, R_RING)
    ps = nc.alloc_psum_tensor("ps", [128, 8, 512], F32)

    cpl = [R_CONST]

    def const(name, shape, dt):
        o = cpl[0]
        n = int(np.prod(shape[1:])) * mybir.dt.size(dt)
        cpl[0] += n + (-n) % 32
        assert cpl[0] <= R_CONST + 6144
        return at(name, shape, dt, o)

    ident = const("ident", [128, 128], F32)
    ident16 = const("ident16", [128, 128], BF16)
    iota_i = const("iota_i", [128, NP2], I16)
    iota16 = const("iota16", [128, NP2], F16)
    iota1_16 = const("iota1_16", [128, NP2], F16)
    ones16 = const("ones16", [128, 128], F16)
    ones = const("ones", [128, 128], F32)
    ones_b = const("ones_b", [128, 1], BF16)
    zero = const("zero", [128, 1], F32)
    ltri = const("ltri", [128, 128], F32)
    spl = [R_SMALL]

    def small(name, shape, dt):
        o = spl[0]
        n = int(np.prod(shape[1:])) * mybir.dt.size(dt)
        spl[0] += n + (-n) % 32
        assert spl[0] <= R_SMALL + 2560, name
        return at(name, shape, dt, o)

    stats = small("stats", [P, T, 2, 6], F32)
    mv = small("mv", [P, T, 2], F32)
    va = small("va", [P, T], F32)
    rs = small("rs", [P, T], F32)
    t5 = small("t5", [P, T], F32)
    dis = small("dis", [P, T], F32)
    flag = small("flag", [128, 1], F32)
    flag_i = small("flag_i", [128, 1], I32)
    gam = small("gam", [128, 2], F32)
    rgam = small("rgam", [128, 2], F32)
    qcur = small("qcur", [128, 1], I32)
    qcand = small("qcand", [128, 1], I32)
    q_rank, q_cand, q_took, q_top, q_part = (
        small(n, [128, 1], F32) for n in ("q_rank", "q_cand", "q_took", "q_top", "q_part"))
    qs = small("qs", [128, 1], F32)
    qrs = small("qrs", [128, 1], F32)

    pre = nc.dram_tensor("pre", [G_PRE0, T, P, 512], F32, kind="Internal").ap()
    x1p = nc.dram_tensor("x1p", [P, T * D], F32, kind="Internal").ap()
    c_dram = nc.dram_tensor("c_dram", [P, T * NODES], I16, kind="Internal").ap()

    lanes = {"pe": PE, "dve": DVE, "act": ALE}
    phase_no = [0]

    def meet():
        phase_no[0] += 1
        for n, e in lanes.items():
            e.drain().then_inc(S("ph_" + n), 1)
        for n, e in lanes.items():
            for o in lanes:
                if o != n:
                    e.wait_ge(S("ph_" + o), phase_no[0])

    seq = {}

    def nxt(name, by=1):
        seq[name] = seq.get(name, 0) + by
        return seq[name]

    def sig(ins, name):
        ins.then_inc(S(name), 1)
        return (name, nxt(name))

    def dma(dst, src, name, eng=None):
        (eng or ALE).dma_start(dst, src).then_inc(S(name), 16)
        return (name, nxt(name, 16))

    def dma_after(mark, dst, src, name):
        ALE.wait_ge(S(mark[0]), mark[1])
        return dma(dst, src, name)

    def wait(eng, *marks):
        for name, v in marks:
            eng.wait_ge(S(name), v)

    stream = a["stream"]
    def load_chunk(c, q):
        SP.wait_ge(S("split_done"), c + 1)
        SP.dma_start(w_stage[:, q % NST, :],
                     stream[bass.ds(c, 1)].rearrange("a p f -> p (a f)")).then_inc(S(f"landed{q % NST}"), 16)

    nloop = NSTREAM // NSL
    with SP.Fori(0, nloop) as i:
        for q in range(NSL):
            load_chunk(i * NSL + q, q)
    for q in range(NSTREAM - nloop * NSL):
        load_chunk(nloop * NSL + q, q)

    POOL.iota(iota_i[:], pattern=[[1, NP2]], base=0, channel_multiplier=0)
    POOL.memset(ident[:], 0.0)
    POOL.memset(ones[:], 1.0)
    POOL.memset(zero[:], 0.0)
    POOL.drain()
    POOL.affine_select(out=ident[:], in_=ident[:], compare_op=ALU.not_equal, fill=1.0, base=0,
                       pattern=[[-1, 128]], channel_multiplier=1)
    POOL.affine_select(out=ltri[:], in_=ones[:], compare_op=ALU.is_gt, fill=0.0, base=0,
                       pattern=[[1, 128]], channel_multiplier=-1)
    POOL.drain().then_inc(S("consts"), 1)

    POOL.sem_inc(S("split_done"), NST)

    def split_chunk(c, q, turn):
        POOL.wait_ge(S(f"landed{q % NST}"), 16 * turn)
        POOL.wait_ge(S("w_used"), c + 1)
        POOL.tensor_tensor(w_hi[:, q, :], w_stage[:, q % NST, :], zero[:].to_broadcast([128, 512]),
                           ALU.add).then_inc(S("hi_done"), 1)
        POOL.wait_ge(S("hi_done"), c + 1)
        POOL.tensor_tensor(w_lo[:, q, :], w_stage[:, q % NST, :], w_hi[:, q, :].bitcast(F32),
                           ALU.subtract).then_inc(S("split_done"), 1)

    with POOL.Fori(0, nloop) as i:
        for q in range(NSL):
            split_chunk(i * NSL + q, q, 2 * i + q // NST + 1)
    for q in range(NSTREAM - nloop * NSL):
        split_chunk(nloop * NSL + q, q, 2 * nloop + q // NST + 1)

    PE.sem_inc(S("w_used"), NSL)

    DVE.wait_ge(S("consts"), 1)
    DVE.tensor_copy(iota16[:], iota_i[:])
    DVE.tensor_scalar(iota1_16[:], iota_i[:], 1.0, None, ALU.add)
    DVE.tensor_copy(ident16[:], ident[:])
    DVE.memset(ones16[:], 1.0)
    DVE.memset(ones_b[:], 1.0)

    done = {"chunks": 0, "groups": 0}
    DVE.sem_inc(S("bank_free"), T)

    def stats_tile(src, m):
        for h in range(2):
            DVE.bn_stats(stats[:, m, h, :], src[:, m, h * 512:(h + 1) * 512])

    def stats_finish():
        DVE.drain()
        for m in range(T):
            DVE.bn_aggr(mv[:, m, :], stats[:, m, :, :])
        DVE.drain()
        DVE.tensor_scalar(va[:], mv[:, :, 1], 1e-5, None, ALU.add)
        mk = sig(DVE.drain(), "dve_step")
        wait(ALE, mk)
        mk = sig(ALE.activation(t5[:], va[:], ACT.Sqrt), "act_step")
        wait(DVE, mk)
        newton_rsqrt()

    def ln_tile(src, dst, m):
        return DVE.tensor_scalar(dst[:, m, :], src[:, m, :], mv[:, m, 0:1], rs[:, m:m + 1], ALU.subtract, ALU.mult)

    def ln_split(src, dst, after_tile=None):
        stats_finish()
        low = {}

        def lower(m):
            b = 2 * (m % 4)
            wait(DVE, high[m])
            for j in range(2):
                t_ = DVE.tensor_tensor(xt_lo[:, 4 * j:4 * j + 4, m * P:(m + 1) * P], bank_view(b + j),
                                       xt_hi[:, 4 * j:4 * j + 4, m * P:(m + 1) * P].bitcast(F32), ALU.subtract)
            low[m] = sig(t_, "tr_lo")

        def bank_view(b):
            return ps[:, b, 0:4 * P].rearrange("p (k n) -> p k n", k=4)

        high = {}
        for m in range(T):
            mk = sig(ln_tile(src, dst, m), "dve_step")
            wait(PE, mk)
            if m >= 4:
                lower(m - 1)
                wait(PE, low[m - 4])
            b = 2 * (m % 4)
            for k in range(KT):
                t_ = PE.transpose(ps[:, b + k // 4, (k % 4) * P:(k % 4 + 1) * P], dst[:, m, k * 128:(k + 1) * 128],
                                  ident[0:P, 0:P])
            wait(ALE, sig(t_, "tr_full"))
            for j in range(2):
                t_ = ALE.activation(xt_hi[:, 4 * j:4 * j + 4, m * P:(m + 1) * P], bank_view(b + j), ACT.Copy)
            high[m] = sig(t_, "tr_hi")
            if after_tile:
                after_tile(m, mk)
            if 1 <= m < 4:
                lower(m - 1)
        lower(T - 1)
        wait(PE, low[T - 1])

    def newton_rsqrt():
        DVE.reciprocal(rs[:], t5[:])
        DVE.drain()
        DVE.tensor_tensor(t5[:], rs[:], rs[:], ALU.mult)
        DVE.drain()
        DVE.tensor_tensor(t5[:], t5[:], va[:], ALU.mult)
        DVE.drain()
        DVE.tensor_scalar(t5[:], t5[:], -0.5, 1.5, ALU.mult, ALU.add)
        DVE.drain()
        DVE.tensor_tensor(rs[:], rs[:], t5[:], ALU.mult)
        DVE.drain()

    def transpose_split(src, width, nk, hi, lo):
        free = []
        for k in range(nk):
            b = 2 * (k % 4)
            if k >= 4:
                wait(PE, free[k - 4])
            for m in range(T):
                dst = ps[0:width, b, m * P:(m + 1) * P] if m < 4 else ps[0:width, b + 1, 0:P]
                t_ = PE.transpose(dst, src[:, m, k * width:(k + 1) * width], ident[0:P, 0:P])
            mk = sig(t_, "tr_full")
            wait(ALE, mk)
            ALE.activation(hi[0:width, k, 0:C1], ps[0:width, b, 0:C1], ACT.Copy)
            mk = sig(ALE.activation(hi[0:width, k, C1:NODES], ps[0:width, b + 1, 0:C2], ACT.Copy), "tr_hi")
            wait(DVE, mk)
            DVE.tensor_tensor(lo[0:width, k, 0:C1], ps[0:width, b, 0:C1],
                              hi[0:width, k, 0:C1].bitcast(F32), ALU.subtract)
            free.append(sig(DVE.tensor_tensor(lo[0:width, k, C1:NODES], ps[0:width, b + 1, 0:C2],
                                              hi[0:width, k, C1:NODES].bitcast(F32), ALU.subtract), "tr_lo"))

    def three(dst, l_hi, l_lo, r_hi, r_lo, first, last):
        PE.matmul(dst, l_hi, r_hi, start=first, stop=False)
        PE.matmul(dst, l_hi, r_lo, start=False, stop=False)
        return PE.matmul(dst, l_lo, r_hi, start=False, stop=last)

    def dense_pe(g, c0, g0, extra_wait=None, between=None):
        for k in range(KT):
            if extra_wait:
                extra_wait(k)
            PE.wait_ge(S("split_done"), NST + c0 + g * KT + k + 1)
            for m in range(T):
                if k == 0:
                    PE.wait_ge(S("bank_free"), (g + g0) * T + m + 1)
                last = three(ps[0:P, m, :], xt_hi[:, k, m * P:(m + 1) * P], xt_lo[:, k, m * P:(m + 1) * P],
                             w_hi[:, k, :], w_lo[:, k, :], k == 0, k == KT - 1)
                if m == T - 1:
                    last.then_inc(S("w_used"), 1)
                elif k == KT - 1:
                    last.then_inc(S("bank_full"), 1)
                if between:
                    between(k, m)

    def wait_bank(eng, g, m, c0, g0):
        if m < T - 1:
            eng.wait_ge(S("bank_full"), (g + g0) * (T - 1) + m + 1)
        else:
            eng.wait_ge(S("w_used"), NSL + c0 + (g + 1) * KT)

    def dense_to_pre(groups, bias0, side, after_two=None):
        c0, g0 = done["chunks"], done["groups"]
        tag = f"pre{g0}"
        bias_t = at("bias_" + tag, [P, 512], F32, R_EXTRA)
        for m in range(T):
            ALE.sem_inc(S(f"st{tag}_{m}"), 16)

        def store(g):
            ALE.wait_ge(S("bank_free"), (g + g0) * T + T)
            ALE.dma_start(bias_t[:], a["bias"][bass.ds(g + bias0, 1), :].to_broadcast([P, 512])).then_inc(S("b" + tag), 16)
            for m in range(T):
                ALE.wait_ge(S("bank_free"), (g + g0 + 1) * T + m + 1)
                ALE.dma_start(pre[bass.ds(g, 1), m].rearrange("a p f -> p (a f)"), ring[:, m, :]).then_inc(S(f"st{tag}_{m}"), 16)

        def stored(g):
            for m in range(T):
                ALE.wait_ge(S(f"st{tag}_{m}"), 16 * g + 32)

        if after_two:
            with ALE.Fori(0, 2) as g:
                store(g)
            after_two(stored)
        with ALE.Fori(2 if after_two else 0, groups) as g:
            store(g)

        def evacuate(g):
            DVE.wait_ge(S("b" + tag), 16 * g + 16)
            for m in range(T):
                wait_bank(DVE, g, m, c0, g0)
                DVE.wait_ge(S(f"st{tag}_{m}"), 16 * g + 16)
                DVE.tensor_tensor(ring[:, m, :], ps[0:P, m, :], bias_t[:], ALU.add).then_inc(S("bank_free"), 1)

        side(lambda g, between=None: dense_pe(g, c0, g0, between=between), evacuate)
        stored(groups - 1)
        done["chunks"] += groups * KT
        done["groups"] += groups

    def dense_add(acc, bias0, name, stats_too=False):
        c0, g0 = done["chunks"], done["groups"]
        bias_t = at("bias_" + name, [P, 2, 512], F32, R_RING)
        mk = dma(bias_t[:], a["bias"][bias0:bias0 + 2, :].rearrange("(o g) f -> o g f", o=1).to_broadcast([P, 2, 512]),
                 "ld_" + name)
        wait(DVE, mk)
        for g in range(2):
            for m in range(T):
                o = acc[:, m, g * 512:(g + 1) * 512]
                DVE.tensor_tensor(o, o, bias_t[:, g, :], ALU.add)
        DVE.drain()
        for g in range(2):
            dense_pe(g, c0, g0)
            for m in range(T):
                wait_bank(DVE, g, m, c0, g0)
                o = acc[:, m, g * 512:(g + 1) * 512]
                DVE.tensor_tensor(o, o, ps[0:P, m, :], ALU.add).then_inc(S("bank_free"), 1)
                if g and stats_too:
                    DVE.drain()
                    stats_tile(acc, m)
        DVE.drain()
        done["chunks"] += 2 * KT
        done["groups"] += 2

    def attention(layer, group0, pmt):
        tag = f"at{layer}_"
        o = [R_XT]

        def tmp(name, shape, dt=F32):
            n = int(np.prod(shape[1:])) * 4
            p_ = o[0]
            o[0] += n + (-n) % 64
            assert o[0] <= R_XT + 2 * KT * NP2 * 4
            return at(tag + name, shape, dt, p_)

        qk = [tmp(f"qk{i}", [P, 2, T, 128]) for i in range(2)]
        vx = [tmp(f"vx{i}", [P, T, 130]) for i in range(3)]
        qt = tmp("qt", [128, 2, NODES])
        ft = tmp("ft", [P, 2, T, 128])
        qft = tmp("qft", [128, NODES])
        kv = tmp("kv", [128, 130])
        bd = tmp("bd", [128, 128])
        mx = tmp("mx", [P, 2, 2 * T])
        den = tmp("den", [P, T, 2])
        eps_t = tmp("eps", [P, 1])
        DVE.memset(kv[:], 0.0)
        DVE.memset(bd[:], 0.0)
        DVE.memset(eps_t[:], 1e-4)
        for i in range(3):
            DVE.memset(vx[i][:, :, 128:130], 1.0)
        mk = sig(DVE.drain(), "dve_step")
        wait(ALE, mk)
        dma(bd[0:64, 0:64], pmt, tag + "bd")
        mk_bd = dma(bd[64:128, 64:128], pmt, tag + "bd")
        scale = 64.0 ** -0.25
        loads, pe, evac = {}, {}, {}

        def load(h):
            if h >= 2:
                wait(ALE, pe["A", h - 2])
            if h >= 3:
                wait(ALE, pe["C", h - 3])
            for i, dst in enumerate((qk[h % 2][:, 0], qk[h % 2][:, 1], vx[h % 3][:, :, 0:128])):
                g = group0 + 2 * i + h // 4
                c = (h % 4) * 128
                loads[h] = dma(dst, pre[g, :, :, c:c + 128].rearrange("t p f -> p t f"), tag + f"ld{h % 3}")

        def step_a(h):
            wait(PE, loads[h])
            if h:
                wait(PE, *evac["A", h - 1])
            for i in range(2):
                for m in range(T):
                    dst = ps[:, i, m * P:(m + 1) * P] if m < 4 else ps[:, 2, 128 * i:128 * i + P]
                    t_ = PE.transpose(dst, qk[h % 2][:, i, m, :], ident[0:P, 0:P])
            pe["A", h] = mk = sig(t_, tag + "pe")
            wait(DVE, mk)
            wait(ALE, mk)
            sc = scale if layer else 1.0
            DVE.tensor_scalar(qt[:, 0, 0:C1], ps[:, 0, 0:C1], sc, None, ALU.mult)
            mq = sig(DVE.tensor_scalar(qt[:, :, C1:NODES], ps[:, 2, 0:256].rearrange("p (i n) -> p i n", i=2)[:, :, 0:P],
                                       sc, None, ALU.mult), tag + "dve")
            mkk = sig(ALE.activation(qt[:, 1, 0:C1], ps[:, 1, 0:C1], ACT.Copy, scale=sc), tag + "act")
            evac["A", h] = (mq, mkk)

        def step_b(h):
            wait(PE, *evac["A", h])
            if h == 0:
                wait(PE, mk_bd)
            for i in range(2):
                for m in range(T):
                    dst = ps[0:P, 3 + i, m * 128:(m + 1) * 128] if m < 4 else ps[0:P, 5, i * 128:(i + 1) * 128]
                    t_ = PE.matmul(dst, qt[:, i, m * P:(m + 1) * P], bd[:], start=True, stop=True)
            wait(DVE, sig(t_, tag + "pe"))
            if layer:
                for i in range(2):
                    DVE.tensor_scalar(ft[:, i, 0:4, :], ps[0:P, 3 + i, :].rearrange("p (t f) -> p t f", t=4), 0.0, 1e-6,
                                      ALU.max, ALU.add)
                mf = sig(DVE.tensor_scalar(ft[:, :, 4, :], ps[0:P, 5, 0:256].rearrange("p (i f) -> p i f", i=2), 0.0, 1e-6,
                                           ALU.max, ALU.add), tag + "dve")
            else:
                for i in range(2):
                    DVE.tensor_reduce(mx[:, i, 0:8], ps[0:P, 3 + i, :].rearrange("p (t f) -> p t f", f=64), AX.X, ALU.max)
                DVE.tensor_reduce(mx[:, :, 8:10], ps[0:P, 5, 0:256].rearrange("p (i t f) -> p i t f", i=2, f=64), AX.X, ALU.max)
                DVE.drain()
                for i in range(2):
                    DVE.tensor_tensor(ft[:, i, 0:4, :].rearrange("p t (s f) -> p (t s) f", s=2),
                                      ps[0:P, 3 + i, :].rearrange("p (t f) -> p t f", f=64),
                                      mx[:, i, 0:8].unsqueeze(2).to_broadcast([P, 8, 64]), ALU.subtract)
                mf = sig(DVE.tensor_tensor(ft[:, :, 4, :].rearrange("p i (s f) -> p i s f", s=2),
                                           ps[0:P, 5, 0:256].rearrange("p (i s f) -> p i s f", i=2, f=64),
                                           mx[:, :, 8:10].unsqueeze(3).to_broadcast([P, 2, 2, 64]), ALU.subtract),
                         tag + "dve")
                wait(ALE, mf)
                fview = ft[:].rearrange("p i t f -> p (i t) f")
                mf = sig(ALE.activation(fview, fview, ACT.Exp, scale=scale, bias=eps_t[:]), tag + "act")
            evac["B", h] = mf

        def step_c(h):
            wait(PE, evac["B", h])
            if h:
                wait(PE, evac["D", h - 1])
            for m in range(T):
                dst = ps[:, 6, m * P:(m + 1) * P] if m < 4 else ps[:, 7, 0:P]
                PE.transpose(dst, ft[:, 0, m, :], ident[0:P, 0:P])
            for m in range(T):
                t_ = PE.matmul(ps[:, 7, 128:258], ft[:, 1, m, :], vx[h % 3][:, m, :], start=(m == 0), stop=(m == T - 1),
                               skip_group_check=True)
            pe["C", h] = mk = sig(t_, tag + "pe")
            wait(ALE, mk)
            wait(DVE, mk)
            mq = sig(ALE.activation(qft[:, 0:C1], ps[:, 6, 0:C1], ACT.Copy), tag + "act")
            DVE.tensor_copy(qft[:, C1:NODES], ps[:, 7, 0:P])
            for s in range(2):
                r = slice(64 * s, 64 * s + 64)
                DVE.tensor_copy(kv[r, 64 * s:64 * s + 64], ps[r, 7, 128 + 64 * s:192 + 64 * s])
                DVE.tensor_copy(kv[r, 128 + s:129 + s], ps[r, 7, 256:257])
            evac["C", h] = (mq, sig(DVE.drain(), tag + "dve"))

        def step_d(h):
            wait(PE, *evac["C", h])
            for m in range(T):
                t_ = PE.matmul(ps[0:P, 6 + m // 3, 130 * (m % 3):130 * (m % 3) + 130], qft[:, m * P:(m + 1) * P], kv[:],
                               start=True, stop=True)
            wait(DVE, sig(t_, tag + "pe"))
            parts = ((6, 0, 3), (7, 3, 2))
            for bk, m0, n in parts:
                v_ = ps[0:P, bk, 0:130 * n].rearrange("p (t f) -> p t f", f=130)
                DVE.tensor_scalar(den[:, m0:m0 + n, :], v_[:, :, 128:130], 1e-6, None, ALU.add)
            DVE.drain()
            DVE.reciprocal(den[:], den[:])
            DVE.drain()
            for bk, m0, n in parts:
                v_ = ps[0:P, bk, 0:130 * n].rearrange("p (t f) -> p t f", f=130)
                t_ = DVE.tensor_tensor(nat[:, m0:m0 + n, h * 128:(h + 1) * 128].rearrange("p t (s f) -> p t s f", s=2),
                                       v_[:, :, 0:128].rearrange("p t (s f) -> p t s f", s=2),
                                       den[:, m0:m0 + n, :].unsqueeze(3).to_broadcast([P, n, 2, 64]), ALU.mult)
            evac["D", h] = sig(t_, tag + "dve")

        load(0)
        load(1)
        for h in range(HEADS2 + 1):
            if h < HEADS2:
                step_a(h)
            if h:
                step_c(h - 1)
            if h < HEADS2:
                step_b(h)
            if h:
                step_d(h - 1)
            if h + 2 < HEADS2:
                load(h + 2)

    for m in range(T):
        wait(DVE, dma(nat[:, m, :], a["x"][m * P:(m + 1) * P, :], f"ld_x{m}"))
        stats_tile(nat, m)

    def natural16(m, mk):
        wait(DVE, mk)
        wait(DVE, sig(DVE.tensor_copy(xn_hi[:, m, :], nat[:, m, :]), "dve_step"))
        DVE.tensor_tensor(xn_lo[:, m, :], nat[:, m, :], xn_hi[:, m, :], ALU.subtract)

    ln_split(nat, nat, natural16)
    meet()

    adj = at("adj", [P, T, NBUCKET * P], I16, R_A)
    o_ = [R_A, R_EXTRA + 2048]

    def tmp(name, shape, dt, w=0):
        n = int(np.prod(shape[1:])) * mybir.dt.size(dt)
        p_ = o_[w]
        o_[w] += n + (-n) % 32
        assert o_[w] <= (R_A + 50176, R_EXTRA + 20480)[w], name
        return at(name, shape, dt, p_)

    scan = tmp("scan", [P, NBUCKET, EC], F32)
    key_hot = tmp("key_hot", [P, NBUCKET, EC], BF16)
    ed_src, ed_dst, ed_typ, e_posi, e_tmpi = (tmp(n, [P, EC], I32) for n in ("ed_src", "ed_dst", "ed_typ", "e_posi", "e_tmpi"))
    e_tile, e_key, e_pos = (tmp(n, [P, EC], F32) for n in ("e_tile", "e_key", "e_pos"))
    b_tot, b_beg, b_off = (tmp(n, [P, NBUCKET], F32) for n in ("b_tot", "b_beg", "b_off"))
    b_grp, b_cum = (tmp(n, [128, NBUCKET], F32) for n in ("b_grp", "b_cum"))
    b_grpi = tmp("b_grpi", [128, NBUCKET], I32)
    gcol = tmp("gcol", [1, NGROUP // 4, 4], F32)
    gsumf = tmp("gsumf", [1, NGROUP // 4], F32)
    gb = at("gb", [1, NGROUP, NBUCKET], F32, R_A)
    e_src1, e_dl1, e_lo, e_hi = (tmp(n, [P, EC], F32, 1) for n in ("e_src1", "e_dl1", "e_lo", "e_hi"))
    gpack = tmp("gpack", [1, NGROUP // 4], I32, 1)
    r_hot = o_[1]
    hot_lo = [tmp(f"hot_lo{i}", [P, 128], F16, 1) for i in range(T)]
    hot_hi = [tmp(f"hot_hi{i}", [P, 2, NCHUNK], F16, 1) for i in range(T)]
    slot = tmp("slot", [128, 2, NCHUNK + 4], F32, 1)
    hot_s = [at(f"hot_s{i}", [128, NODES], F16, r_hot + i * 1280) for i in range(4)]
    hot_s += [tmp(f"hot_s{i}", [128, NODES], F16, 1) for i in range(4, 8)]
    hot_d = [tmp(f"hot_d{i}", [128, P], F16, 1) for i in range(8)]
    slot_ps = ps[:, 5, 0:2 * NCHUNK]

    def bucket_counts():
        wait(DVE, mk_edges)
        DVE.tensor_scalar(e_tile[:], ed_dst[:], float(P), None, ALU.is_ge)
        DVE.tensor_scalar(e_src1[:], ed_src[:], 1.0, None, ALU.add)
        DVE.drain()
        for j in range(2, T):
            DVE.tensor_scalar(e_key[:], ed_dst[:], float(j * P), None, ALU.is_ge)
            DVE.drain()
            DVE.tensor_tensor(e_tile[:], e_tile[:], e_key[:], ALU.add)
            DVE.drain()
        DVE.tensor_scalar(e_dl1[:], e_tile[:], -float(P), 1.0, ALU.mult, ALU.add)
        DVE.tensor_scalar(e_key[:], ed_typ[:], float(T), None, ALU.mult)
        DVE.drain()
        DVE.tensor_tensor(e_dl1[:], e_dl1[:], ed_dst[:], ALU.add)
        DVE.tensor_tensor(e_key[:], e_key[:], e_tile[:], ALU.add)
        DVE.drain()
        DVE.tensor_tensor(key_hot[:], e_key[:].unsqueeze(1).to_broadcast([P, NBUCKET, EC]),
                          iota16[0:P, 0:NBUCKET].unsqueeze(2).to_broadcast([P, NBUCKET, EC]), ALU.is_equal)
        DVE.drain()
        kh = key_hot[:].rearrange("p b c -> p (b c)")
        DVE.tensor_tensor_scan(scan[:].rearrange("p b c -> p (b c)"), kh, kh, 0.0, ALU.add, ALU.max)
        DVE.drain()
        DVE.memset(b_beg[:, 0:1], 0.0)
        DVE.tensor_copy(b_beg[:, 1:NBUCKET], scan[:, 0:NBUCKET - 1, EC - 1])
        DVE.drain()
        DVE.tensor_tensor(b_tot[:], scan[:, :, EC - 1], b_beg[:], ALU.subtract)
        return sig(DVE.drain(), "dve_step")

    def bucket_sums(mk):
        wait(PE, mk)
        PE.matmul(ps[0:P, 6, 0:NBUCKET], ltri[0:P, 0:P], b_tot[:], start=True, stop=True)
        return sig(PE.matmul(ps[:, 7, 0:NBUCKET], ones[0:P, :], b_tot[:], start=True, stop=True), "pe_step")

    def positions(mk, evacuate):
        wait(DVE, mk)
        DVE.tensor_reduce(flag[:], ps[:, 7, 0:NBUCKET], AX.X, ALU.max)
        DVE.tensor_scalar(b_grp[:], ps[:, 7, 0:NBUCKET], GROUP / 2 - 0.75, 1.0 / GROUP, ALU.add, ALU.mult)
        DVE.drain()
        DVE.tensor_scalar(flag_i[:], flag[:], 2048.0, None, ALU.is_gt)
        DVE.tensor_copy(b_grpi[:], b_grp[:])
        DVE.drain()
        DVE.tensor_copy(b_grp[:], b_grpi[:])
        DVE.drain()
        DVE.tensor_tensor_scan(b_cum[:], b_grp[:], b_grp[:], 0.0, ALU.add, ALU.max)
        DVE.drain()
        DVE.tensor_tensor(b_cum[:], b_cum[:], b_grp[:], ALU.subtract)
        DVE.drain()
        DVE.tensor_scalar(b_off[:], b_cum[0:P, :], float(GROUP), -1.0, ALU.mult, ALU.add)
        DVE.drain()
        DVE.tensor_tensor(b_off[:], b_off[:], ps[0:P, 6, 0:NBUCKET], ALU.add)
        DVE.drain()
        DVE.tensor_tensor(b_off[:], b_off[:], b_beg[:], ALU.subtract)
        DVE.drain()
        DVE.tensor_tensor(scan[:], scan[:], b_off[:].unsqueeze(2).to_broadcast([P, NBUCKET, EC]), ALU.add)
        DVE.drain()
        DVE.tensor_tensor(scan[:], scan[:], key_hot[:], ALU.mult)
        evacuate(1)
        DVE.drain()
        DVE.tensor_reduce(e_pos[:], scan[:].rearrange("p b c -> p c b"), AX.X, ALU.add)
        DVE.drain()
        DVE.tensor_copy(e_posi[:], e_pos[:])
        DVE.drain()
        DVE.tensor_scalar(e_tmpi[:], e_posi[:], 7, None, ALU.logical_shift_right)
        DVE.drain()
        DVE.tensor_copy(e_hi[:], e_tmpi[:])
        DVE.drain()
        DVE.tensor_scalar(e_tmpi[:], e_posi[:], 127, None, ALU.bitwise_and)
        DVE.drain()
        DVE.tensor_copy(e_lo[:], e_tmpi[:])
        DVE.tensor_tensor(gb[:], b_cum[0:1, :].unsqueeze(1).to_broadcast([1, NGROUP, NBUCKET]),
                          iota16[0:1, 0:NGROUP].unsqueeze(2).to_broadcast([1, NGROUP, NBUCKET]), ALU.is_le)
        DVE.drain()
        DVE.tensor_reduce(gcol[:].rearrange("o g j -> o (g j)"), gb[:], AX.X, ALU.add)
        DVE.drain()
        DVE.tensor_scalar(gsumf[:], gcol[:, :, 0], -float(1 + 2 ** 6 + 2 ** 12 + 2 ** 18), None, ALU.add)
        for j in range(1, 4):
            DVE.drain()
            DVE.scalar_tensor_tensor(gsumf[:], gcol[:, :, j], 2.0 ** (6 * j), gsumf[:], ALU.mult, ALU.add)
        DVE.drain()
        DVE.tensor_copy(gpack[:], gsumf[:])
        DVE.drain()
        DVE.memset(adj[:], 0)
        DVE.drain()

    def scatter_dve(c, j):
        DVE.wait_ge(S("sc_pe"), c + 1)
        DVE.tensor_scalar(hot_lo[j][:], iota16[0:P, 0:128], e_lo[:, bass.ds(c, 1)], None, ALU.is_equal)
        DVE.tensor_scalar(hot_hi[j][:, 0, :], iota16[0:P, 0:NCHUNK], e_hi[:, bass.ds(c, 1)],
                          e_src1[:, bass.ds(c, 1)], ALU.is_equal, ALU.mult)
        DVE.tensor_scalar(hot_hi[j][:, 1, :], iota16[0:P, 0:NCHUNK], e_hi[:, bass.ds(c, 1)],
                          e_dl1[:, bass.ds(c, 1)], ALU.is_equal, ALU.mult).then_inc(S("sc_dve"), 1)

    def scatter_pe(c, j, last=False):
        PE.wait_ge(S("sc_dve"), c + 1)
        PE.matmul(slot_ps, hot_lo[j][:], hot_hi[j][:].rearrange("p a c -> p (a c)"), start=False,
                  stop=last).then_inc(S("sc_pe"), 1)

    def group_banks(gm):
        return ps[0:P, 5 + gm % 2, 0:C1], ps[0:P, 7, 128 * (gm % 2):128 * (gm % 2) + P]

    def hist_dve_hot(g, gm):
        for j in range(2):
            q = 2 * gm + j
            c = g * 2 + j
            DVE.wait_ge(S("hi_pe"), c + 1)
            DVE.tensor_scalar(hot_s[q][:], iota1_16[:, 0:NODES], slot[:, 0, bass.ds(c, 1)], None, ALU.is_equal)
            DVE.tensor_scalar(hot_d[q][:], iota1_16[:, 0:P], slot[:, 1, bass.ds(c, 1)], None,
                              ALU.is_equal).then_inc(S("hi_dve"), 1)

    def hist_dve_add(g, gm, packed):
        bucket = nc.s_assert_within((packed >> (6 * gm)) & 63, 0, NBUCKET - 1,
                                    skip_runtime_bounds_check_because="a bucket's number is below NBUCKET")
        off = bucket * P
        DVE.wait_ge(S("hi_pe"), 8 + 2 * g + 2)
        DVE.wait_ge(S("hi_add"), 4 + 2 * g)
        b4, b1 = group_banks(gm)
        a1 = adj[:, 4, bass.ds(off, P)]
        DVE.tensor_tensor(a1, a1, b1, ALU.add).then_inc(S("hi_add"), 1)
        a0 = adj[:, 0:4, bass.ds(off, P)]
        DVE.tensor_tensor(a0, a0, b4.rearrange("p (t d) -> p t d", t=4), ALU.add).then_inc(S("hi_add"), 1)

    def hist_pe_tile4(wait_value, gm):
        PE.wait_ge(S("hi_add"), wait_value)
        for j in range(2):
            q = 2 * gm + j
            PE.matmul(group_banks(gm)[1], hot_s[q][:, 4 * P:5 * P], hot_d[q][:], start=(j == 0), stop=(j == 1),
                      skip_group_check=True).then_inc(S("hi_pe"), 1)

    def hist_pe(g, gm):
        hist_pe_tile4(2 * g + 1, (gm - 1) % 4)
        b4, b1 = group_banks(gm)
        for j in range(2):
            q = 2 * gm + j
            PE.wait_ge(S("hi_dve"), g * 2 + j + 1)
            if j == 0:
                PE.wait_ge(S("hi_add"), 2 * g + 2)
            for m in range(4):
                PE.matmul(b4[:, m * P:(m + 1) * P], hot_s[q][:, m * P:(m + 1) * P], hot_d[q][:],
                          start=(j == 0 and m == 0), stop=(j == 1), skip_group_check=True)

    def beside(dense, evacuate):
        dense(0)
        mk = bucket_counts()
        mk = bucket_sums(mk)
        dense(1)
        evacuate(0)
        positions(mk, evacuate)
        dense(2)
        evacuate(2)
        PE.sem_inc(S("sc_pe"), T)
        zero16 = hot_s[4][0:P, 0:128]
        DVE.memset(zero16, 0.0)
        DVE.memset(hot_s[5][0:P, 0:2 * NCHUNK], 0.0)
        DVE.memset(slot[:, :, NCHUNK:NCHUNK + 4], 0.0)
        for q in (6, 7):
            DVE.memset(hot_s[q][:], 0.0)
            DVE.memset(hot_d[q][:], 0.0)
        mk = sig(DVE.drain(), "dve_step")
        wait(PE, mk)
        PE.matmul(slot_ps, zero16, hot_s[5][0:P, 0:2 * NCHUNK], start=True, stop=False)
        g_sc = EC // (KT * T)
        assert g_sc == 4
        with PE.Fori(0, g_sc) as i:
            dense(i + 3, lambda k, m: scatter_pe((i * KT + k) * T + m, m))
        with DVE.Fori(0, g_sc) as i:
            for k in range(KT):
                for m in range(T):
                    scatter_dve((i * KT + k) * T + m, m)
            evacuate(i + 3)
        for c in range(g_sc * KT * T, EC):
            scatter_dve(c, c % T)
            scatter_pe(c, c % T, c == EC - 1)
        DVE.wait_ge(S("sc_pe"), T + EC)
        DVE.tensor_copy(slot[:, :, 0:NCHUNK], slot_ps.rearrange("p (a c) -> p a c", a=2))
        DVE.drain()
        DVE.sem_inc(S("hi_add"), 4)
        PE.sem_inc(S("hi_pe"), 6)
        per = NGROUP // (3 * KT)
        assert per == T and per * 3 * KT == NGROUP
        with PE.Fori(0, 3) as i:
            dense(i + 7, lambda k, m: hist_pe((i * KT + k) * T + m, (k * T + m) % 4))
        hist_pe_tile4(2 * NGROUP + 1, (NGROUP - 1) % 4)
        for n in range(2):
            hist_dve_hot(n, n)
        with DVE.Fori(0, 3) as i:
            for n in range(per * KT):
                if n == per * KT - 1:
                    evacuate(i + 7)
                hist_dve_hot(i * per * KT + n + 2, (n + 2) % 4)
                if n % 4 == 0:
                    packed = DVE.value_load(gpack[0:1, bass.ds(i * (per * KT // 4) + n // 4, 1)],
                                            min_val=0, max_val=2 ** 24 - 1)
                hist_dve_add(i * per * KT + n, n % 4, packed)

    for nm, dst in (("src", ed_src), ("dst", ed_dst), ("typ", ed_typ)):
        mk_edges = dma(dst[:], a[nm].rearrange("(p c) -> p c", c=EC), "ld_edges")
    dense_to_pre(G_PRE0, B_PRE0, beside)
    meet()

    attention(0, 4, a["pm0"])
    meet()
    transpose_split(nat, 128, KT, xt_hi, xt_lo)
    x_res = at("x_res", [P, T, D], F32, R_EXTRA)
    mk = dma(x_res[:], a["x"].rearrange("(t p) d -> p t d", p=P), "ld_x2")
    meet()
    wait(DVE, mk)
    dense_add(x_res, B_PROJ0, "proj0")
    meet()
    mk = dma(x1p[:], x_res[:].rearrange("p t d -> p (t d)"), "st_x1p")
    wait(ALE, mk)

    for g in range(2):
        mk = dma(nat[:, :, g * 512:(g + 1) * 512], pre[g].rearrange("t p f -> p t f"), "ld_u")
    meet()
    wait(DVE, mk)
    a_hi = at("a_hi", [P, T, NODES], F16, R_EXTRA)
    a_lo = at("a_lo", [P, T, NODES], F16, R_EXTRA + 6272)
    rcnt = at("rcnt", [128, NP2], F32, R_EXTRA + 2 * 6272)
    mtmp = [at(f"mtmp{i}", [128, H0], F32, R_EXTRA + 2 * 6272 + 2560 + i * 1280) for i in range(4)]
    halves = ((0, H0), (H0, H1))
    c0, g0 = done["chunks"], done["groups"]
    many = PE.value_load(flag_i[0:1, 0:1], min_val=0, max_val=1)
    DVE.sem_inc(S("ag_free"), 3)
    DVE.sem_inc(S("mt_ready"), 1)
    PE.sem_inc(S("ag_full"), 1)

    def ag_bank(i):
        return 5 + i % 3, *halves[i % 2]

    def counts_pe(r):
        PE.wait_ge(S("a_ready"), r + 1)
        for i in range(2):
            bank, h0, hn = ag_bank(i)
            PE.wait_ge(S("ag_free"), r * 18 + i + 1)
            for lo in range(2):
                for t in range(T):
                    t_ = PE.matmul(ps[:, bank, 0:hn], ones16[0:P, :], (a_hi, a_lo)[lo][:, t, h0:h0 + hn],
                                   start=(lo == 0 and t == 0), stop=(lo == 1 and t == T - 1))
            t_.then_inc(S("ag_full"), 1)

    def relation_pe(r, more):
        for i in range(2, 18):
            bank, h0, hn = ag_bank(i)
            PE.wait_ge(S("ag_free"), r * 18 + i + 1)
            k = i // 2 - 1
            dst = ps[:, bank, 0:hn]

            def agg(x16, a16, t, first, last):
                return PE.matmul(dst, x16[:, t, k * 128:(k + 1) * 128], a16[:, t, h0:h0 + hn], start=first, stop=last)

            for t in range(T):
                agg(xn_hi, a_hi, t, t == 0, False)
            with PE.If(many):
                for t in range(T):
                    agg(xn_hi, a_lo, t, False, False)
                    agg(xn_lo, a_lo, t, False, False)
            for t in range(T):
                t_ = agg(xn_lo, a_hi, t, False, t == T - 1)
            t_.then_inc(S("ag_full"), 1)

        def mean_ready(k):
            PE.wait_ge(S("mt_ready"), 1 + r * 16 + 2 * k + 2)
        dense_pe(r * 2, c0, g0, mean_ready)
        if more:
            counts_pe(r + 1)
        dense_pe(r * 2 + 1, c0, g0)

    counts_pe(0)
    with PE.Fori(0, REL - 1) as r:
        relation_pe(r, True)
    with PE.Fori(REL - 1, REL) as r:
        relation_pe(r, False)
    with ALE.Fori(0, REL) as r:
        for i in range(2, 18):
            h0, hn = halves[i % 2]
            j = i - 2
            ALE.wait_ge(S("ag_scaled"), r * 16 + j + 1)
            ALE.activation(xt_hi[:, j // 2, h0:h0 + hn], mtmp[j % 4][:, 0:hn], ACT.Copy).then_inc(S("mt_hi"), 1)

    def counts_split(r):
        DVE.wait_ge(S("ag_full"), r * 18 + 1)
        DVE.tensor_copy(a_hi[:], adj[:, :, bass.ds(r * NODES, NODES)]).then_inc(S("a_hi"), 1)
        DVE.wait_ge(S("a_hi"), r + 1)
        DVE.tensor_tensor(a_lo[:], adj[:, :, bass.ds(r * NODES, NODES)], a_hi[:], ALU.subtract).then_inc(S("a_ready"), 1)

    def counts_dve(r):
        for i in range(2):
            bank, h0, hn = ag_bank(i)
            DVE.wait_ge(S("ag_full"), r * 18 + i + 2)
            DVE.tensor_scalar(rcnt[:, h0:h0 + hn], ps[:, bank, 0:hn], 1.0, None, ALU.max).then_inc(S("ag_free"), 1)
        DVE.wait_ge(S("ag_free"), 3 + r * 18 + 2)
        DVE.reciprocal(rcnt[:, 0:NODES], rcnt[:, 0:NODES]).then_inc(S("rcnt"), 1)

    def relation_dve(r, more):
        DVE.wait_ge(S("rcnt"), r + 1)

        def low(j):
            h0, hn = halves[j % 2]
            DVE.wait_ge(S("mt_hi"), r * 16 + j + 1)
            DVE.tensor_tensor(xt_lo[:, j // 2, h0:h0 + hn], mtmp[j % 4][:, 0:hn],
                              xt_hi[:, j // 2, h0:h0 + hn].bitcast(F32), ALU.subtract).then_inc(S("mt_ready"), 1)

        for j in range(16):
            i = j + 2
            bank, h0, hn = ag_bank(i)
            DVE.wait_ge(S("ag_full"), r * 18 + i + 2)
            DVE.wait_ge(S("mt_ready"), 1 + r * 16 + max(j - 3, 0))
            DVE.tensor_tensor(mtmp[j % 4][:, 0:hn], ps[:, bank, 0:hn], rcnt[:, h0:h0 + hn],
                              ALU.mult).then_inc(S("ag_free"), 1)
            DVE.wait_ge(S("ag_free"), 3 + r * 18 + i + 1)
            DVE.sem_inc(S("ag_scaled"), 1)
            if j >= 1:
                low(j - 1)
        low(15)
        if more:
            counts_split(r + 1)
        DVE.wait_ge(S("c_sum"), r + 1)
        DVE.tensor_tensor(c_sum[:], c_sum[:], adj[:, :, bass.ds(r * NODES, NODES)], ALU.add).then_inc(S("c_sum"), 1)
        if not more:
            last_relation()
        for gg in range(2):
            if gg and more:
                counts_dve(r + 1)
            for m in range(T):
                wait_bank(DVE, r * 2 + gg, m, c0, g0)
                u_ = nat[:, m, gg * 512:(gg + 1) * 512]
                DVE.wait_ge(S("bank_free"), (r * 2 + g0) * T + T)
                DVE.tensor_tensor(u_, u_, ps[0:P, m, :], ALU.add).then_inc(S("bank_free"), 1)

    c_sum = at("c_sum", [P, T, NODES], I16, R_RING)
    z = at("z", [P, T, D], F32, R_A)
    x1 = at("x1", [P, T, D], F32, R_A + T * D * 4)
    lng = at("lng", [P, D], F32, R_A + 2 * T * D * 4)
    lnb = at("lnb", [P, D], F32, R_A + 2 * T * D * 4 + D * 4)
    w1 = at("w1", [128, KT, FFN0], F32, R_EXTRA)
    w2 = at("w2", [128, FFN0 // 128, D], F32, R_EXTRA + 8192)

    def last_relation():
        DVE.drain()
        DVE.tensor_reduce(va[:], c_sum[:], AX.X, ALU.add)
        DVE.drain()
        DVE.tensor_scalar(va[:], va[:], 1.0, None, ALU.add)
        mk = sig(DVE.drain(), "dve_step")
        wait(ALE, mk)
        loads["c"] = dma(c_dram[:], c_sum[:].rearrange("p t d -> p (t d)"), "st_c")
        loads["x1"] = dma(x1[:].rearrange("p t d -> p (t d)"), x1p[:], "ld_x1")
        dma(w1[:], a["w1t"], "ld_w12")
        loads["w"] = dma(w2[:], a["w2t"], "ld_w12")
        for g in range(2):
            loads["z"] = dma(z[:, :, g * 512:(g + 1) * 512], pre[2 + g].rearrange("t p f -> p t f"), "ld_z")
        dma(lng[:], a["ln_g"].to_broadcast([P, D]), "ld_ln")
        loads["ln"] = dma(lnb[:], a["ln_b"].to_broadcast([P, D]), "ld_ln")
        mk = sig(ALE.activation(t5[:], va[:], ACT.Sqrt), "act_step")
        wait(DVE, mk)
        newton_rsqrt()
        DVE.tensor_copy(dis[:], rs[:])

    loads = {}
    DVE.memset(c_sum[:], 0).then_inc(S("c_sum"), 1)
    counts_split(0)
    counts_dve(0)
    with DVE.Fori(0, REL - 1) as r:
        relation_dve(r, True)
    relation_dve(REL - 1, False)
    done["chunks"] += REL * 2 * KT
    done["groups"] += REL * 2
    meet()

    w1q = at("w1q", [128, KT, FFN0], BF16, R_RING)
    w2q = at("w2q", [128, FFN0 // 128, D], BF16, R_RING + 4096)
    gsum = small("gsum", [128, 2], F32)
    transpose_split(nat, 128, KT, xt_hi, xt_lo)
    wait(ALE, loads["c"])
    meet()
    for m in range(T):
        mk_t = sig(ALE.activation(nat[:, m, :], nat[:, m, :], ACT.Tanh), "act_step")
    c0, g0 = done["chunks"], done["groups"]
    dense_pe(0, c0, g0)
    wait(DVE, loads["w"])
    for i, w in enumerate((w1, w2)):
        DVE.tensor_reduce(gsum[:, i:i + 1], w[:].rearrange("p k f -> p (k f)"), AX.X, ALU.add, apply_absolute_value=True)
    mk = sig(DVE.drain(), "dve_step")
    wait(PE, mk)
    mk_g = sig(PE.matmul(ps[:, 5, 0:2], ones[:], gsum[:], start=True, stop=True), "pe_step")
    dense_pe(1, c0, g0)
    wait(DVE, mk_t, loads["x1"])
    for m in range(T):
        for n in (nat, x1):
            DVE.tensor_tensor(n[:, m, :], n[:, m, :], xn_hi[:, m, :], ALU.subtract if n is nat else ALU.add)
        DVE.drain()
        for n in (nat, x1):
            DVE.tensor_tensor(n[:, m, :], n[:, m, :], xn_lo[:, m, :], ALU.subtract if n is nat else ALU.add)
    def gate_evac(g):
        for m in range(T):
            wait_bank(DVE, g, m, c0, g0)
            c = slice(g * 512, g * 512 + 512)
            DVE.tensor_tensor(z[:, m, c], z[:, m, c], ps[0:P, m, :], ALU.add).then_inc(S("bank_free"), 1)
            DVE.wait_ge(S("bank_free"), (g + g0 + 1) * T + m + 1)
            if m:
                DVE.tensor_tensor(x1[:, m - 1, c], x1[:, m - 1, c], z[:, m - 1, c], ALU.add)
            DVE.tensor_tensor(z[:, m, c], z[:, m, c], nat[:, m, c], ALU.mult)
            DVE.drain()
            if g and m > 1:
                stats_tile(x1, m - 2)
        DVE.tensor_tensor(x1[:, T - 1, c], x1[:, T - 1, c], z[:, T - 1, c], ALU.add)
        if g:
            DVE.drain()
            for m in range(T - 2, T):
                stats_tile(x1, m)

    wait(DVE, loads["z"])
    DVE.drain()
    gate_evac(0)
    MAGIC = 1.5 * 2.0 ** 23
    wait(DVE, mk_g)
    DVE.tensor_scalar(gam[:], ps[:, 5, 0:2], 1.0 / (FFN0 * D), 1e-5, ALU.mult, ALU.add)
    DVE.drain()
    DVE.reciprocal(rgam[:], gam[:])
    DVE.drain()
    for i, (w, wq) in enumerate(((w1, w1q), (w2, w2q))):
        wf = w[:].rearrange("p k f -> p (k f)")
        DVE.tensor_scalar(wf, wf, rgam[:, i:i + 1], 1.0, ALU.mult, ALU.min)
        DVE.drain()
        DVE.tensor_scalar(wf, wf, -1.0, MAGIC, ALU.max, ALU.add)
        mk = sig(DVE.drain(), "dve_step")
        wait(ALE, mk)
        ALE.activation(wq[:].rearrange("p k f -> p (k f)"), wf, ACT.Copy, bias=-MAGIC)
    gate_evac(1)
    done["chunks"] += 2 * KT
    done["groups"] += 2
    DVE.drain()

    stats_finish()
    for m in range(T):
        ln_tile(x1, nat, m)
    DVE.drain()
    wait(DVE, loads["ln"])
    for m in range(T):
        stats_tile(nat, m)
    stats_finish()
    for m in range(T):
        DVE.scalar_tensor_tensor(nat[:, m, :], nat[:, m, :], mv[:, m, 0:1], lng[:], ALU.subtract, ALU.mult)
    DVE.drain()
    for m in range(T):
        DVE.scalar_tensor_tensor(nat[:, m, :], nat[:, m, :], rs[:, m:m + 1], lnb[:], ALU.mult, ALU.add)
    DVE.drain()
    meet()

    q_top8 = small("q_top8", [P, 8], F32)
    q_hot8 = small("q_hot8", [P, 15, 8], F32)
    q_thr = small("q_thr", [P, 15], F32)
    q_cnt15 = small("q_cnt15", [P, 15], F32)
    q_ok15 = small("q_ok15", [128, 15], F32)
    q_steps = small("q_steps", [128, 3], F32)
    q_halves = small("q_halves", [128, 3], F32)
    q_full = small("q_full", [P, 1], F32)
    q_many = small("q_many", [128, 1], I32)

    def find_rank(h, width, rank):
        n = T * width
        tag = f"q{width}"
        hf = h[:].rearrange("p t d -> p (t d)")
        key_hi = at(tag + "_hi", [P, n], I16, R_XN)
        key_lo = at(tag + "_lo", [P, n], U16, R_XN + 10240)
        mask = at(tag + "_mask", [P, n], BF16, R_EXTRA)
        pieces = 4 if n > 4 * 1024 else 2
        pn = n // pieces
        halves_of = lambda dt: hf.bitcast(dt).rearrange("p (n two) -> p n two", two=2)
        mk = sig(DVE.drain(), "dve_step")
        wait(ALE, mk)
        mk_lo = sig(ALE.activation(key_lo[:], halves_of(U16)[:, :, 0], ACT.Copy), "act_step")
        DVE.memset(q_rank[:], float(rank))
        DVE.tensor_scalar(key_hi[:], halves_of(I16)[:, :, 1], 0x7FFF, None, ALU.bitwise_and)
        DVE.drain()

        def count_pe(name, i):
            for c in range(n // 128):
                if c % (pn // 128) == 0:
                    PE.wait_ge(S(name + "_mask"), i * pieces + c // (pn // 128) + 1)
                t_ = PE.matmul(ps[:, 0, 0:1], mask[:, c * 128:(c + 1) * 128], ones_b[0:P, :], start=(c == 0),
                               stop=(c == n // 128 - 1))
            t_.then_inc(S(name + "_part"), 1)
            PE.wait_ge(S(name + "_copied"), i + 1)
            PE.matmul(ps[:, 1, 0:1], ones[:], q_part[:], start=True, stop=True).then_inc(S(name + "_count"), 1)

        def count_dve(name, i, keys):
            for j in range(pieces):
                DVE.tensor_scalar(mask[:, j * pn:(j + 1) * pn], keys[:, j * pn:(j + 1) * pn], q_cand[0:P, :], None,
                                  ALU.is_ge).then_inc(S(name + "_mask"), 1)
            DVE.wait_ge(S(name + "_part"), i + 1)
            DVE.tensor_copy(q_part[:], ps[:, 0, 0:1]).then_inc(S(name + "_copied"), 1)
            DVE.wait_ge(S(name + "_count"), i + 1)

        def bisect(name, keys, top, rounds, unroll):
            DVE.memset(q_cand[:], top)
            for j in range(unroll):
                DVE.memset(q_steps[:, j:j + 1], top / 2 ** j)
                DVE.memset(q_halves[:, j:j + 1], -top / 2 ** (j + 1))
            DVE.drain()
            with DVE.Fori(0, rounds // unroll) as i:
                for j in range(unroll):
                    count_dve(name, i * unroll + j, keys)
                    DVE.tensor_scalar(q_took[:], ps[:, 1, 0:1], q_rank[:], q_steps[:, j:j + 1], ALU.is_ge, ALU.mult)
                    DVE.drain()
                    DVE.scalar_tensor_tensor(q_cand[:], q_took[:], q_halves[:, j:j + 1], q_cand[:], ALU.add, ALU.add)
                    DVE.drain()
                DVE.tensor_scalar(q_steps[:], q_steps[:], 0.5 ** unroll, None, ALU.mult)
                DVE.tensor_scalar(q_halves[:], q_halves[:], 0.5 ** unroll, None, ALU.mult)
                DVE.drain()
            DVE.tensor_scalar(q_cand[:], q_cand[:], -0.5, None, ALU.add)
            DVE.drain()

        with PE.Fori(0, 5) as i:
            for j in range(3):
                count_pe(tag + "a", i * 3 + j)
        count_pe(tag + "b", 0)
        bisect(tag + "a", key_hi, 2.0 ** 14, 15, 3)
        DVE.tensor_copy(q_top[:], q_cand[:])
        DVE.drain()
        DVE.tensor_scalar(q_cand[:], q_cand[:], 1.0, None, ALU.add)
        DVE.drain()
        count_dve(tag + "b", 0, key_hi)
        DVE.tensor_tensor(q_rank[:], q_rank[:], ps[:, 1, 0:1], ALU.subtract)
        wait(DVE, mk_lo)
        DVE.scalar_tensor_tensor(key_lo[:], key_hi[:], q_top[0:P, :], key_lo[:], ALU.is_equal, ALU.mult)
        DVE.drain()
        DVE.max(q_top8[:], key_lo[:])
        DVE.drain()
        DVE.tensor_scalar(q_full[:], q_top8[:, 7:8], 0.5, None, ALU.is_gt)
        mk = sig(DVE.drain(), "dve_step")
        wait(PE, mk)
        mk = sig(PE.matmul(ps[:, 2, 0:1], ones[0:P, :], q_full[:], start=True, stop=True), "pe_step")
        DVE.memset(q_cand[:], 0.0)
        for r in range(4):
            step = 16.0 ** (3 - r)
            DVE.drain()
            DVE.tensor_scalar(q_thr[:], iota1_16[0:P, 0:15], step, q_cand[0:P, :], ALU.mult, ALU.add)
            DVE.drain()
            DVE.tensor_tensor(q_hot8[:], q_top8[:].unsqueeze(1).to_broadcast([P, 15, 8]),
                              q_thr[:].unsqueeze(2).to_broadcast([P, 15, 8]), ALU.is_ge)
            DVE.drain()
            DVE.tensor_reduce(q_cnt15[:], q_hot8[:], AX.X, ALU.add)
            m15 = sig(DVE.drain(), "dve_step")
            wait(PE, m15)
            m15 = sig(PE.matmul(ps[:, 3, 0:15], ones[0:P, :], q_cnt15[:], start=True, stop=True), "pe_step")
            wait(DVE, m15)
            DVE.tensor_scalar(q_ok15[:], ps[:, 3, 0:15], q_rank[:], None, ALU.is_ge, ALU.add, accum_out=q_took[:])
            DVE.drain()
            DVE.scalar_tensor_tensor(q_cand[:], q_took[:], step, q_cand[:], ALU.mult, ALU.add)
        wait(DVE, mk)
        DVE.tensor_scalar(q_many[:], ps[:, 2, 0:1], 0.5, None, ALU.is_gt)
        mk = sig(DVE.drain(), "dve_step")
        wait(PE, mk)
        with PE.Fori(0, 1) as _:
            with PE.If(PE.value_load(q_many[0:1, 0:1], min_val=0, max_val=1)):
                with PE.Fori(0, 16) as i:
                    count_pe(tag + "c", i)
        with DVE.Fori(0, 1) as _:
            with DVE.If(DVE.value_load(q_many[0:1, 0:1], min_val=0, max_val=1)):
                bisect(tag + "c", key_lo, 2.0 ** 15, 16, 1)
        DVE.tensor_copy(qcur[:], q_top[:])
        DVE.tensor_copy(qcand[:], q_cand[:])
        DVE.drain()
        DVE.tensor_scalar(qcur[:], qcur[:], 16, None, ALU.logical_shift_left)
        DVE.drain()
        DVE.tensor_tensor(qcur[:], qcur[:], qcand[:], ALU.bitwise_or)
        DVE.drain()

    def quant_scale(i):
        DVE.tensor_scalar(qs[:], qcur[:].bitcast(F32), 1e-5, None, ALU.max)
        DVE.drain()
        DVE.tensor_scalar(qrs[:], qs[:], gam[:, i:i + 1], 1.0 / 127.0, ALU.mult, ALU.mult)
        DVE.reciprocal(qs[:], qs[:])
        DVE.drain()
        DVE.tensor_scalar(qs[:], qs[:], 127.0, None, ALU.mult)
        DVE.drain()

    ps16 = ps[:].bitcast(BF16)

    def quant_product(h, hq, width, hqt, product):
        nk = width // 128
        back = {}

        def front(m):
            DVE.tensor_scalar(h[:, m, :], h[:, m, :], qs[0:P, :], 127.0, ALU.mult, ALU.min)
            DVE.drain()
            DVE.tensor_scalar(h[:, m, :], h[:, m, :], -128.0, MAGIC, ALU.max, ALU.add)
            wait(ALE, sig(DVE.drain(), "dve_step"))
            wait(PE, sig(ALE.activation(hq[:, m, :], h[:, m, :], ACT.Copy, bias=-MAGIC), "act_step"))
            if m >= 2:
                wait(PE, back[m - 2])
            for k in range(nk):
                t_ = PE.transpose(ps16[:, 6 + m % 2, k * 128:k * 128 + P], hq[:, m, k * 128:(k + 1) * 128], ident16[0:P, 0:P])
            return sig(t_, "pe_step")

        def rest(m, mk):
            wait(DVE, mk)
            back[m] = sig(DVE.tensor_copy(hqt[:, :, m * P:(m + 1) * P],
                                          ps16[:, 6 + m % 2, 0:nk * 128].rearrange("p (k n) -> p k n", k=nk)[:, :, 0:P]), "dve_step")
            wait(PE, back[m])
            product(m)

        marks = [front(0)]
        for m in range(T):
            if m + 1 < T:
                marks.append(front(m + 1))
            rest(m, marks[m])

    hq = at("hq", [P, T, D], BF16, R_EXTRA)
    hqt = at("hqt", [128, KT, NODES], BF16, R_XN)
    gl = at("gl", [P, T, FFN0], F32, R_NAT)
    glq = at("glq", [P, T, FFN0], BF16, R_EXTRA)
    glt = at("glt", [128, FFN0 // 128, NODES], BF16, R_XN)

    find_rank(nat, D, 3201)
    quant_scale(0)

    def up0(m):
        for k in range(KT):
            t_ = PE.matmul(ps[0:P, m, 0:FFN0], hqt[:, k, m * P:(m + 1) * P], w1q[:, k, :], start=(k == 0), stop=(k == KT - 1))
        up_marks.append(sig(t_, "pe_step"))

    up_marks = []
    quant_product(nat, hq, D, hqt, up0)
    for m in range(T):
        wait(ALE, up_marks[m])
        mk = sig(ALE.activation(gl[:, m, :], ps[0:P, m, 0:FFN0], ACT.Gelu, scale=qrs[0:P, :]), "act_step")
    wait(DVE, mk)
    meet()
    find_rank(gl, FFN0, 801)
    quant_scale(1)
    down_free = {}

    def down0(m):
        for h in range(2):
            n = 2 * m + h
            if n >= 6:
                wait(PE, down_free[n - 6])
            for k in range(FFN0 // 128):
                t_ = PE.matmul(ps[0:P, n % 6, :], glt[:, k, m * P:(m + 1) * P], w2q[:, k, h * 512:(h + 1) * 512], start=(k == 0),
                               stop=(k == FFN0 // 128 - 1))
            wait(DVE, sig(t_, "pe_step"))
            o = x1[:, m, h * 512:(h + 1) * 512]
            down_free[n] = sig(DVE.scalar_tensor_tensor(o, ps[0:P, n % 6, :], qrs[0:P, :], o, ALU.mult, ALU.add), "dve_step")
        DVE.drain()
        stats_tile(x1, m)

    quant_product(gl, glq, FFN0, glt, down0)
    DVE.drain()
    meet()

    ct_hi = at("ct_hi", [P, T, NP2], F32R, R_EXTRA + 2048)
    ct_lo = [at(f"ct_lo{k}", [P, NP2], F32R, R_A + 2 * T * D * 4 + k * 2560 if k < 3 else R_EXTRA + 2048 + 12544 + (k - 3) * 2528)
             for k in range(T)]
    c16 = at("c16", [P, T, NODES], I16, R_A + 2 * T * D * 4)
    c_nat = at("c_nat", [P, T, NODES], F32, R_NAT)
    hp_hi = at("hp_hi", [P, T, D], F32R, R_NAT)
    hp_lo = at("hp_lo", [P, T, D], F32R, R_XN)
    h_nat = at("h_nat", [P, T, D], F32, R_XN)
    mc = dma(c16[:].rearrange("p t d -> p (t d)"), c_dram[:], "ld_c")
    ln_split(x1, nat)

    def beside1(dense, evacuate):
        def ct_pe(k, m):
            if m < T - 1 or k >= T:
                return
            PE.wait_ge(S("ct_done"), k + 1)
            for t in range(T):
                dst = ps[0:P, 5, t * P:(t + 1) * P] if t < 4 else ps[0:P, 6, 0:P]
                t_ = PE.transpose(dst, c_nat[:, t, k * P:(k + 1) * P], ident[0:P, 0:P])
            t_.then_inc(S("ct_full"), 1)

        dense(0, ct_pe)
        wait(DVE, mc)
        DVE.tensor_copy(c_nat[:], c16[:])
        DVE.drain()
        for t in range(T):
            b = c_nat[:, t, t * P:(t + 1) * P]
            DVE.tensor_tensor(b, b, ident[0:P, 0:P], ALU.add)
        DVE.drain().then_inc(S("ct_done"), 1)
        for k in range(T):
            DVE.wait_ge(S("ct_full"), k + 1)
            parts = ((ps[0:P, 5, 0:C1], slice(0, C1)), (ps[0:P, 6, 0:C2], slice(C1, NODES)))
            for src, c in parts:
                DVE.tensor_copy(ct_hi[:, k, c], src)
            DVE.drain()
            for src, c in parts:
                t_ = DVE.tensor_tensor(ct_lo[k][:, c], src, ct_hi[:, k, c].bitcast(F32), ALU.subtract)
            t_.then_inc(S("ct_done"), 1)
        evacuate(0)
        with PE.Fori(1, G_PRE1) as g:
            dense(g)
        with DVE.Fori(1, 3) as g:
            evacuate(g)
        wait(DVE, *h_loaded)
        for t in range(T):
            DVE.tensor_scalar(h_nat[:, t, :], h_nat[:, t, :], dis[:, t:t + 1], None, ALU.mult)
        DVE.drain()
        for t in range(T):
            DVE.tensor_copy(hp_hi[:, t, :], h_nat[:, t, :])
        DVE.drain()
        for t in range(T):
            DVE.tensor_tensor(hp_lo[:, t, :], h_nat[:, t, :], hp_hi[:, t, :].bitcast(F32), ALU.subtract)
        with DVE.Fori(3, G_PRE1) as g:
            evacuate(g)

    h_loaded = []

    def load_h(stored):
        stored(1)
        for g in range(2):
            h_loaded.append(dma(h_nat[:, :, g * 512:(g + 1) * 512], pre[g].rearrange("t p f -> p t f"), "ld_h"))

    dense_to_pre(G_PRE1, B_PRE1, beside1, after_two=load_h)
    meet()
    free = []
    for n in range(2 * T):
        m, h = n // 2, n % 2
        if n >= 8:
            wait(PE, free[n - 8])
        for k in range(T):
            c = slice(m * P, (m + 1) * P)
            t_ = three(ps[0:P, n % 8, :], ct_hi[:, k, c], ct_lo[k][:, c],
                       hp_hi[:, k, h * 512:(h + 1) * 512], hp_lo[:, k, h * 512:(h + 1) * 512], k == 0, k == T - 1)
        wait(DVE, sig(t_, "pe_step"))
        o = x1[:, m, h * 512:(h + 1) * 512]
        free.append(sig(DVE.scalar_tensor_tensor(o, ps[0:P, n % 8, :], dis[:, m:m + 1], o, ALU.mult, ALU.add), "dve_step"))
    meet()
    attention(1, 2, a["pm1"])
    meet()
    transpose_split(nat, 128, KT, xt_hi, xt_lo)
    meet()
    wr = at("wr", [128, KT, NEXP], F32, R_EXTRA)
    wr_hi = at("wr_hi", [128, KT, NEXP], F32R, R_EXTRA + 256)
    wr_lo = at("wr_lo", [128, KT, NEXP], F32R, R_EXTRA + 512)
    rb = at("rb", [P, NEXP], F32, R_EXTRA + 768)
    pr = at("pr", [P, T, NEXP], F32, R_EXTRA + 1024)
    cw = at("cw", [P, T, NEXP], F32, R_EXTRA + 1280)
    gt = at("gt", [P, T, NEXP, NEXP], F32, R_EXTRA + 1536)
    eq = at("eq", [P, T, NEXP, NEXP], F32, R_EXTRA + 1536 + 1280)
    low = at("low", [P, NEXP, NEXP], F32, R_EXTRA + 1536 + 2560)
    sil = [at(f"sil{i}", [P, 2, HID], F32, R_RING + i * 1024) for i in range(4)]
    DVE.memset(low[:], 0.0)
    DVE.drain()
    for e in range(1, NEXP):
        DVE.memset(low[:, e, 0:e], 1.0)
    mk = dma(wr[:], a["wrt"], "ld_wr")
    mk = dma(rb[:], a["rb"].to_broadcast([P, NEXP]), "ld_wr")
    dense_add(x1, B_PROJ1, "proj1", stats_too=True)
    wait(DVE, mk)
    DVE.tensor_copy(wr_hi[:], wr[:])
    DVE.drain()
    DVE.tensor_tensor(wr_lo[:], wr[:], wr_hi[:].bitcast(F32), ALU.subtract)
    mk_wr = sig(DVE.drain(), "dve_step")
    meet()

    ln_split(x1, nat)
    wait(PE, mk_wr)
    for m in range(T):
        for k in range(KT):
            t_ = three(ps[0:P, 5, m * NEXP:(m + 1) * NEXP], xt_hi[:, k, m * P:(m + 1) * P], xt_lo[:, k, m * P:(m + 1) * P],
                       wr_hi[:, k, :], wr_lo[:, k, :], k == 0, k == KT - 1)
    mk = sig(t_, "pe_step")
    wait(DVE, mk)
    DVE.tensor_tensor(pr[:], ps[0:P, 5, 0:T * NEXP].rearrange("p (t e) -> p t e", t=T),
                      rb[:].unsqueeze(1).to_broadcast([P, T, NEXP]), ALU.add)
    mk = sig(DVE.drain(), "dve_step")
    wait(ALE, mk)
    mk = sig(ALE.activation(pr[:], pr[:], ACT.Sigmoid), "act_step")
    wait(DVE, mk)
    pj = pr[:].unsqueeze(2).to_broadcast([P, T, NEXP, NEXP])
    pe_ = pr[:].unsqueeze(3).to_broadcast([P, T, NEXP, NEXP])
    DVE.tensor_tensor(gt[:], pj, pe_, ALU.is_gt)
    DVE.tensor_tensor(eq[:], pj, pe_, ALU.is_equal)
    DVE.drain()
    DVE.tensor_tensor(eq[:], eq[:], low[:].unsqueeze(1).to_broadcast([P, T, NEXP, NEXP]), ALU.mult)
    DVE.drain()
    DVE.tensor_tensor(gt[:], gt[:], eq[:], ALU.add)
    DVE.drain()
    DVE.tensor_reduce(cw[:], gt[:], AX.X, ALU.add)
    DVE.drain()
    DVE.tensor_scalar(cw[:], cw[:], 2.0, None, ALU.is_lt)
    DVE.drain()
    DVE.tensor_tensor(cw[:], cw[:], pr[:], ALU.mult)
    DVE.drain()

    hid = at("hid", [P, T, (NEXP + 1) * HID], F32, R_XN)
    meet()
    c0, g0 = done["chunks"], done["groups"]
    with PE.Fori(0, G_UP) as g:
        dense_pe(g, c0, g0)
    n_sil = 0
    for g in range(G_UP + 1):
        experts = 2 if g < G_UP else 1
        if g == G_UP:
            for c in range(4):
                PE.wait_ge(S("split_done"), NST + c0 + g * KT + c + 1)
                for m in range(T):
                    if c == 0:
                        PE.wait_ge(S("bank_free"), (g + g0) * T + m + 1)
                    for kk in range(2):
                        k = 2 * c + kk
                        t_ = three(ps[0:P, m, 0:2 * HID], xt_hi[:, k, m * P:(m + 1) * P], xt_lo[:, k, m * P:(m + 1) * P],
                                   w_hi[:, c, kk * 256:kk * 256 + 256], w_lo[:, c, kk * 256:kk * 256 + 256],
                                   k == 0, k == KT - 1)
                    if m == T - 1:
                        t_.then_inc(S("w_used"), 1)
                    elif c == 3:
                        t_.then_inc(S("bank_full"), 1)
        for m in range(T):
            s_ = sil[n_sil % 4]
            blocks = ps[0:P, m, 0:256 * experts].rearrange("p (e w h) -> p e w h", w=2, h=HID)
            for eng in (ALE, DVE):
                if m < T - 1:
                    eng.wait_ge(S("bank_full"), (g + g0) * (T - 1) + m + 1)
                else:
                    eng.wait_ge(S("w_used"), NSL + c0 + (g * KT + KT if g < G_UP else g * KT + 4))
            if n_sil >= 4:
                ALE.wait_ge(S("sil_used"), n_sil - 3)
            mk = sig(ALE.activation(s_[:, 0:experts, :], blocks[:, :, 0, :], ACT.Silu), "sil_done")
            wait(DVE, mk)
            if experts == 2:
                for j in range(2):
                    e = 2 * g + j
                    t_ = DVE.scalar_tensor_tensor(hid[:, m, e * HID:(e + 1) * HID], s_[:, j, :], cw[:, m, e:e + 1],
                                                  blocks[:, j, 1, :], ALU.mult, ALU.mult)
            else:
                t_ = DVE.tensor_tensor(hid[:, m, NEXP * HID:], s_[:, 0, :], blocks[:, 0, 1, :], ALU.mult)
            t_.then_inc(S("bank_free"), 1)
            DVE.wait_ge(S("bank_free"), (g + g0 + 1) * T + m + 1)
            DVE.sem_inc(S("sil_used"), 1)
            n_sil += 1
    done["chunks"] += G_UP * KT + 4
    done["groups"] += G_UP + 1
    meet()
    ht_hi = at("ht_hi", [128, NEXP + 1, NP2], F32R, R_XT)
    ht_lo = at("ht_lo", [128, NEXP + 1, NP2], F32R, R_XT + 22592)
    transpose_split(hid, 128, NEXP + 1, ht_hi, ht_lo)
    meet()
    c0, g0 = done["chunks"], done["groups"]
    y = out.rearrange("(t p) d -> t p d", p=P)
    for h in range(2):
        for e in range(NEXP + 1):
            c = c0 + h * (NEXP + 1) + e
            q = c % NSL
            PE.wait_ge(S("split_done"), NST + c + 1)
            for m in range(T):
                if e == 0:
                    PE.wait_ge(S("bank_free"), (h + g0) * T + m + 1)
                t_ = three(ps[0:P, m, :], ht_hi[:, e, m * P:(m + 1) * P], ht_lo[:, e, m * P:(m + 1) * P],
                           w_hi[:, q, :], w_lo[:, q, :], e == 0, e == NEXP)
                if m == T - 1:
                    t_.then_inc(S("w_used"), 1)
                elif e == NEXP:
                    t_.then_inc(S("bank_full"), 1)
        for m in range(T):
            if m < T - 1:
                DVE.wait_ge(S("bank_full"), (h + g0) * (T - 1) + m + 1)
            else:
                DVE.wait_ge(S("w_used"), NSL + c0 + (h + 1) * (NEXP + 1))
            o = x1[:, m, h * 512:(h + 1) * 512]
            DVE.tensor_tensor(o, o, ps[0:P, m, :], ALU.add).then_inc(S("bank_free"), 1)
            ALE.wait_ge(S("bank_free"), (h + g0 + 1) * T + m + 1)
            mk = dma(y[m, :, h * 512:(h + 1) * 512], o, "st_out")
    wait(ALE, mk)


def kernel(**inputs):
    from concourse import bacc
    from concourse.bass_utils import run_bass_kernel_spmd

    v = {k: np.asarray(x) for k, x in inputs.items()}

    def chunks(wt):
        n = wt.shape[1] // 512
        return wt.reshape(KT, 128, n, 512).transpose(2, 0, 1, 3).reshape(n * KT, 128, 512)

    gate = v["L0_gnn_w_gate"]
    ups = np.stack([v["L1_ffn_Wg"], v["L1_ffn_Wu"]], axis=1).reshape(NEXP * 2 * HID, D).T
    shared = np.concatenate([v["L1_ffn_Wg_s"], v["L1_ffn_Wu_s"]], axis=0).T
    shared = shared.reshape(4, 2, 128, 2 * HID).transpose(0, 2, 1, 3).reshape(4, 128, 512)
    downs = np.concatenate([v["L1_ffn_Wd"], v["L1_ffn_Wd_s"][None]], axis=0)
    downs = downs.transpose(0, 2, 1).reshape(NEXP + 1, 128, 2, 512).transpose(2, 0, 1, 3).reshape(-1, 128, 512)
    stream = np.concatenate(
        [chunks(v["L0_gnn_root"]), chunks(gate[D:]), chunks(v["L0_mix_W_qkv"].T), chunks(v["L0_mix_W_proj"].T)]
        + [chunks(v["L0_gnn_weight"][r]) for r in range(REL)]
        + [chunks(gate[:D])]
        + [chunks(v[n].T) for n in ("L1_gnn_W", "L1_mix_Wq", "L1_mix_Wk", "L1_mix_Wv", "L1_mix_Wo")]
        + [chunks(ups), shared, downs])
    bias = np.concatenate([v[n] for n in ("L0_gnn_bias", "L0_gnn_b_gate", "L0_mix_b_qkv", "L0_mix_b_proj", "L1_gnn_b",
                                          "L1_mix_bq", "L1_mix_bk", "L1_mix_bv", "L1_mix_bo")]).reshape(NBIAS, 512)
    arrays = {
        "stream": stream, "bias": bias, "x": v["x"], "src": v["src"], "dst": v["dst"], "typ": v["edge_type_8"],
        "pm0": v["L0_mix_proj_mat"].T, "pm1": v["L1_mix_P"].T, "ln_g": v["L0_ffn_ln_g"][None], "ln_b": v["L0_ffn_ln_b"][None],
        "w1t": v["L0_ffn_w1"].T.reshape(KT, 128, FFN0).transpose(1, 0, 2),
        "w2t": v["L0_ffn_w2"].T.reshape(FFN0 // 128, 128, D).transpose(1, 0, 2),
        "wrt": v["L1_ffn_Wr"].T.reshape(KT, 128, NEXP).transpose(1, 0, 2), "rb": v["L1_ffn_rb"][None],
    }
    nc = bacc.Bacc("TRN2", target_bir_lowering=False, num_devices=1)
    feed, aps = {}, {}
    for k, x in arrays.items():
        feed["in_" + k] = np.ascontiguousarray(x)
        aps[k] = nc.dram_tensor("in_" + k, x.shape, mybir.dt.from_np(x.dtype), kind="ExternalInput").ap()
    out = nc.dram_tensor("out_x", [NODES, D], F32, kind="ExternalOutput").ap()
    build(nc, aps, out)
    r = run_bass_kernel_spmd(nc, [feed], core_ids=[0])
    return r.results[0]["out_x"]
```

```python
import numpy as np
import concourse.bass as bass
from concourse import mybir
from concourse.alu_op_type import AluOpType as ALU

F32 = mybir.dt.float32
F32R = mybir.dt.float32r
F16 = mybir.dt.float16
BF16 = mybir.dt.bfloat16
I32 = mybir.dt.int32
I16 = mybir.dt.int16
U16 = mybir.dt.uint16
ACT = mybir.ActivationFunctionType
AX = mybir.AxisListType

NODES, D = 625, 1024
P, T = 125, 5
KT = D // 128
REL = 8
EDGES, EC = 20625, 165
NBUCKET = REL * T
GROUP = 256
NGROUP = (EDGES + NBUCKET * (GROUP - 1)) // GROUP
NCHUNK = 2 * NGROUP
HEADS2 = 8
NEXP = 8
HID = 128
FFN0 = 256
NP2 = 626
C1, C2 = 500, 125
H0, H1 = 313, 312

G_PRE0 = 10
G_PROJ = 2
G_REL = 2 * REL
G_GATE = 2
G_PRE1 = 8
G_UP = 4
C_TAIL = 4 + 2 * (NEXP + 1)
NSTREAM = KT * (G_PRE0 + G_PROJ + G_REL + G_GATE + G_PRE1 + G_PROJ + G_UP) + C_TAIL
NST = 4
NSL = 8
B_PRE0, B_PROJ0, B_PRE1, B_PROJ1, NBIAS = 0, 10, 12, 20, 22


def build(nc, a, out):
    PE, DVE, ALE, POOL, SP = nc.tensor, nc.vector, nc.scalar, nc.gpsimd, nc.sync

    sems = {}

    def S(name):
        if name not in sems:
            sems[name] = nc.alloc_semaphore(name)
        return sems[name]

    place = [nc.sbuf_base + (-nc.sbuf_base) % 64]

    def region(size):
        o = place[0]
        place[0] += size + (-size) % 64
        assert place[0] <= nc.sbuf_usable_end, place[0]
        return o

    def at(name, shape, dt, offset):
        return nc.alloc_sbuf_tensor_at(name, shape, dt, offset=offset)

    R_STREAM = region(NST * 2048 + 2 * NSL * 2048)
    R_XT = region(2 * KT * NP2 * 4)
    R_A = region(50176)
    R_XN = region(2 * T * D * 2)
    R_NAT = region(T * D * 4)
    R_RING = region(T * 2048)
    R_EXTRA = region(20480)
    R_CONST = region(6144)
    R_SMALL = region(2560)

    w_stage = at("w_stage", [128, NST, 512], F32, R_STREAM)
    w_hi = at("w_hi", [128, NSL, 512], F32R, R_STREAM + NST * 2048)
    w_lo = at("w_lo", [128, NSL, 512], F32R, R_STREAM + NST * 2048 + NSL * 2048)
    xt_hi = at("xt_hi", [128, KT, NP2], F32R, R_XT)
    xt_lo = at("xt_lo", [128, KT, NP2], F32R, R_XT + KT * NP2 * 4)
    xn_hi = at("xn_hi", [P, T, D], F16, R_XN)
    xn_lo = at("xn_lo", [P, T, D], F16, R_XN + T * D * 2)
    nat = at("nat", [P, T, D], F32, R_NAT)
    ring = at("ring", [P, T, 512], F32, R_RING)
    ps = nc.alloc_psum_tensor("ps", [128, 8, 512], F32)

    cpl = [R_CONST]

    def const(name, shape, dt):
        o = cpl[0]
        n = int(np.prod(shape[1:])) * mybir.dt.size(dt)
        cpl[0] += n + (-n) % 32
        assert cpl[0] <= R_CONST + 6144
        return at(name, shape, dt, o)

    ident = const("ident", [128, 128], F32)
    ident16 = const("ident16", [128, 128], BF16)
    iota_i = const("iota_i", [128, NP2], I16)
    iota16 = const("iota16", [128, NP2], F16)
    iota1_16 = const("iota1_16", [128, NP2], F16)
    ones16 = const("ones16", [128, 128], F16)
    ones = const("ones", [128, 128], F32)
    ones_b = const("ones_b", [128, 1], BF16)
    zero = const("zero", [128, 1], F32)
    ltri = const("ltri", [128, 128], F32)
    spl = [R_SMALL]

    def small(name, shape, dt):
        o = spl[0]
        n = int(np.prod(shape[1:])) * mybir.dt.size(dt)
        spl[0] += n + (-n) % 32
        assert spl[0] <= R_SMALL + 2560, name
        return at(name, shape, dt, o)

    stats = small("stats", [P, T, 2, 6], F32)
    mv = small("mv", [P, T, 2], F32)
    va = small("va", [P, T], F32)
    rs = small("rs", [P, T], F32)
    t5 = small("t5", [P, T], F32)
    dis = small("dis", [P, T], F32)
    rs_first = small("rs_first", [P, T], F32)
    flag = small("flag", [128, 1], F32)
    flag_i = small("flag_i", [128, 1], I32)
    gam = small("gam", [128, 2], F32)
    rgam = small("rgam", [128, 2], F32)
    qcur = small("qcur", [128, 1], I32)
    qcand = small("qcand", [128, 1], I32)
    q_rank, q_cand, q_took, q_top, q_part = (
        small(n, [128, 1], F32) for n in ("q_rank", "q_cand", "q_took", "q_top", "q_part"))
    qs = small("qs", [128, 1], F32)
    qrs = small("qrs", [128, 1], F32)

    pre = nc.dram_tensor("pre", [G_PRE0, T, P, 512], F32, kind="Internal").ap()
    x1p = nc.dram_tensor("x1p", [P, T * D], F32, kind="Internal").ap()
    c_dram = nc.dram_tensor("c_dram", [P, T * NODES], I16, kind="Internal").ap()

    lanes = {"pe": PE, "dve": DVE, "act": ALE}
    phase_no = [0]

    def meet():
        phase_no[0] += 1
        for n, e in lanes.items():
            e.drain().then_inc(S("ph_" + n), 1)
        for n, e in lanes.items():
            for o in lanes:
                if o != n:
                    e.wait_ge(S("ph_" + o), phase_no[0])

    seq = {}

    def nxt(name, by=1):
        seq[name] = seq.get(name, 0) + by
        return seq[name]

    def sig(ins, name):
        ins.then_inc(S(name), 1)
        return (name, nxt(name))

    def dma(dst, src, name, eng=None):
        (eng or ALE).dma_start(dst, src).then_inc(S(name), 16)
        return (name, nxt(name, 16))

    def dma_after(mark, dst, src, name):
        ALE.wait_ge(S(mark[0]), mark[1])
        return dma(dst, src, name)

    def wait(eng, *marks):
        for name, v in marks:
            eng.wait_ge(S(name), v)

    stream = a["stream"]
    def load_chunk(c, q):
        SP.wait_ge(S("split_done"), c + 1)
        SP.dma_start(w_stage[:, q % NST, :],
                     stream[bass.ds(c, 1)].rearrange("a p f -> p (a f)")).then_inc(S(f"landed{q % NST}"), 16)

    nloop = NSTREAM // NSL
    with SP.Fori(0, nloop) as i:
        for q in range(NSL):
            load_chunk(i * NSL + q, q)
    for q in range(NSTREAM - nloop * NSL):
        load_chunk(nloop * NSL + q, q)

    POOL.iota(iota_i[:], pattern=[[1, NP2]], base=0, channel_multiplier=0)
    POOL.memset(ident[:], 0.0)
    POOL.memset(ones[:], 1.0)
    POOL.memset(zero[:], 0.0)
    POOL.drain()
    POOL.affine_select(out=ident[:], in_=ident[:], compare_op=ALU.not_equal, fill=1.0, base=0,
                       pattern=[[-1, 128]], channel_multiplier=1)
    POOL.affine_select(out=ltri[:], in_=ones[:], compare_op=ALU.is_gt, fill=0.0, base=0,
                       pattern=[[1, 128]], channel_multiplier=-1)
    POOL.drain().then_inc(S("consts"), 1)

    POOL.sem_inc(S("split_done"), NST)

    def split_chunk(c, q, turn):
        POOL.wait_ge(S(f"landed{q % NST}"), 16 * turn)
        POOL.wait_ge(S("w_used"), c + 1)
        POOL.tensor_tensor(w_hi[:, q, :], w_stage[:, q % NST, :], zero[:].to_broadcast([128, 512]),
                           ALU.add).then_inc(S("hi_done"), 1)
        POOL.wait_ge(S("hi_done"), c + 1)
        POOL.tensor_tensor(w_lo[:, q, :], w_stage[:, q % NST, :], w_hi[:, q, :].bitcast(F32),
                           ALU.subtract).then_inc(S("split_done"), 1)

    with POOL.Fori(0, nloop) as i:
        for q in range(NSL):
            split_chunk(i * NSL + q, q, 2 * i + q // NST + 1)
    for q in range(NSTREAM - nloop * NSL):
        split_chunk(nloop * NSL + q, q, 2 * nloop + q // NST + 1)

    PE.sem_inc(S("w_used"), NSL)

    DVE.wait_ge(S("consts"), 1)
    DVE.tensor_copy(iota16[:], iota_i[:])
    DVE.tensor_scalar(iota1_16[:], iota_i[:], 1.0, None, ALU.add)
    DVE.tensor_copy(ident16[:], ident[:])
    DVE.memset(ones16[:], 1.0)
    DVE.memset(ones_b[:], 1.0)

    done = {"chunks": 0, "groups": 0}
    DVE.sem_inc(S("bank_free"), T)

    def stats_tile(src, m, feature_halves=(0, 1)):
        for h in feature_halves:
            DVE.bn_stats(stats[:, m, h, :], src[:, m, h * 512:(h + 1) * 512])

    def stats_finish():
        DVE.drain()
        for m in range(T):
            DVE.bn_aggr(mv[:, m, :], stats[:, m, :, :])
        DVE.drain()
        DVE.tensor_scalar(va[:], mv[:, :, 1], 1e-5, None, ALU.add)
        mk = sig(DVE.drain(), "dve_step")
        wait(ALE, mk)
        mk = sig(ALE.activation(t5[:], va[:], ACT.Sqrt), "act_step")
        wait(DVE, mk)
        newton_rsqrt()

    def ln_tile(src, dst, m):
        return DVE.tensor_scalar(dst[:, m, :], src[:, m, :], mv[:, m, 0:1], rs[:, m:m + 1], ALU.subtract, ALU.mult)

    def ln_split(src, dst):
        stats_finish()
        low = {}

        def lower(m):
            b = 2 * (m % 4)
            wait(DVE, high[m])
            for j in range(2):
                t_ = DVE.tensor_tensor(xt_lo[:, 4 * j:4 * j + 4, m * P:(m + 1) * P], bank_view(b + j),
                                       xt_hi[:, 4 * j:4 * j + 4, m * P:(m + 1) * P].bitcast(F32), ALU.subtract)
            low[m] = sig(t_, "tr_lo")

        def bank_view(b):
            return ps[:, b, 0:4 * P].rearrange("p (k n) -> p k n", k=4)

        high = {}
        ahead = 3

        for m in range(T + ahead):
            if m >= ahead:
                lower(m - ahead)
            if m >= T:
                continue
            wait(PE, sig(ln_tile(src, dst, m), "dve_step"))
            if m >= 4:
                wait(PE, low[m - 4])
            b = 2 * (m % 4)
            for k in range(KT):
                t_ = PE.transpose(ps[:, b + k // 4, (k % 4) * P:(k % 4 + 1) * P], dst[:, m, k * 128:(k + 1) * 128],
                                  ident[0:P, 0:P])
            wait(ALE, sig(t_, "tr_full"))
            for j in range(2):
                t_ = ALE.activation(xt_hi[:, 4 * j:4 * j + 4, m * P:(m + 1) * P], bank_view(b + j), ACT.Copy)
            high[m] = sig(t_, "tr_hi")
        wait(PE, low[T - 1])

    def newton_rsqrt():
        DVE.reciprocal(rs[:], t5[:])
        DVE.drain()
        DVE.tensor_tensor(t5[:], rs[:], rs[:], ALU.mult)
        DVE.drain()
        DVE.tensor_tensor(t5[:], t5[:], va[:], ALU.mult)
        DVE.drain()
        DVE.tensor_scalar(t5[:], t5[:], -0.5, 1.5, ALU.mult, ALU.add)
        DVE.drain()
        DVE.tensor_tensor(rs[:], rs[:], t5[:], ALU.mult)
        DVE.drain()

    def transpose_split(src, width, nk, hi, lo):
        free = []
        for k in range(nk):
            b = 2 * (k % 4)
            if k >= 4:
                wait(PE, free[k - 4])
            for m in range(T):
                dst = ps[0:width, b, m * P:(m + 1) * P] if m < 4 else ps[0:width, b + 1, 0:P]
                t_ = PE.transpose(dst, src[:, m, k * width:(k + 1) * width], ident[0:P, 0:P])
            mk = sig(t_, "tr_full")
            wait(ALE, mk)
            ALE.activation(hi[0:width, k, 0:C1], ps[0:width, b, 0:C1], ACT.Copy)
            mk = sig(ALE.activation(hi[0:width, k, C1:NODES], ps[0:width, b + 1, 0:C2], ACT.Copy), "tr_hi")
            wait(DVE, mk)
            DVE.tensor_tensor(lo[0:width, k, 0:C1], ps[0:width, b, 0:C1],
                              hi[0:width, k, 0:C1].bitcast(F32), ALU.subtract)
            free.append(sig(DVE.tensor_tensor(lo[0:width, k, C1:NODES], ps[0:width, b + 1, 0:C2],
                                              hi[0:width, k, C1:NODES].bitcast(F32), ALU.subtract), "tr_lo"))

    def three(dst, l_hi, l_lo, r_hi, r_lo, first, last):
        PE.matmul(dst, l_hi, r_hi, start=first, stop=False)
        PE.matmul(dst, l_hi, r_lo, start=False, stop=False)
        return PE.matmul(dst, l_lo, r_hi, start=False, stop=last)

    def dense_pe(g, c0, g0, extra_wait=None, between=None):
        for k in range(KT):
            if extra_wait:
                extra_wait(k)
            PE.wait_ge(S("split_done"), NST + c0 + g * KT + k + 1)
            for m in range(T):
                if k == 0:
                    PE.wait_ge(S("bank_free"), (g + g0) * T + m + 1)
                last = three(ps[0:P, m, :], xt_hi[:, k, m * P:(m + 1) * P], xt_lo[:, k, m * P:(m + 1) * P],
                             w_hi[:, k, :], w_lo[:, k, :], k == 0, k == KT - 1)
                if m == T - 1:
                    last.then_inc(S("w_used"), 1)
                elif k == KT - 1:
                    last.then_inc(S("bank_full"), 1)
                if between:
                    between(k, m)

    def wait_bank(eng, g, m, c0, g0):
        if m < T - 1:
            eng.wait_ge(S("bank_full"), (g + g0) * (T - 1) + m + 1)
        else:
            eng.wait_ge(S("w_used"), NSL + c0 + (g + 1) * KT)

    def dense_to_pre(groups, bias0, side, after_two=None, beside_last=0):
        c0, g0 = done["chunks"], done["groups"]
        tag = f"pre{g0}"
        bias_t = at("bias_" + tag, [P, 512], F32, R_EXTRA)
        for m in range(T):
            ALE.sem_inc(S(f"st{tag}_{m}"), 16)

        def load_bias(g):
            ALE.wait_ge(S("bank_free"), (g + g0) * T + T)
            ALE.dma_start(bias_t[:], a["bias"][bass.ds(g + bias0, 1), :].to_broadcast([P, 512])).then_inc(S("b" + tag), 16)

        def store(g):
            for m in range(T):
                ALE.wait_ge(S("bank_free"), (g + g0 + 1) * T + m + 1)
                ALE.dma_start(pre[bass.ds(g, 1), m].rearrange("a p f -> p (a f)"), ring[:, m, :]).then_inc(S(f"st{tag}_{m}"), 16)

        def stored(g):
            for m in range(T):
                ALE.wait_ge(S(f"st{tag}_{m}"), 16 * g + 32)

        if after_two:
            with ALE.Fori(0, 2) as g:
                load_bias(g)
                store(g)
            after_two(stored)
        with ALE.Fori(2 if after_two else 0, groups - beside_last) as g:
            load_bias(g)
            store(g)

        def evacuate(g):
            DVE.wait_ge(S("b" + tag), 16 * g + 16)
            for m in range(T):
                wait_bank(DVE, g, m, c0, g0)
                DVE.wait_ge(S(f"st{tag}_{m}"), 16 * g + 16)
                DVE.tensor_tensor(ring[:, m, :], ps[0:P, m, :], bias_t[:], ALU.add).then_inc(S("bank_free"), 1)

        side(lambda g, between=None: dense_pe(g, c0, g0, between=between), evacuate, load_bias, store)
        stored(groups - 2)
        done["chunks"] += groups * KT
        done["groups"] += groups
        return lambda: stored(groups - 1)

    def dense_add(acc, bias0, name, stats_too=False, after_half=None):
        c0, g0 = done["chunks"], done["groups"]
        bias_t = at("bias_" + name, [P, 2, 512], F32, R_RING)
        mk = dma(bias_t[:], a["bias"][bias0:bias0 + 2, :].rearrange("(o g) f -> o g f", o=1).to_broadcast([P, 2, 512]),
                 "ld_" + name)
        wait(DVE, mk)
        for g in range(2):
            for m in range(T):
                o = acc[:, m, g * 512:(g + 1) * 512]
                DVE.tensor_tensor(o, o, bias_t[:, g, :], ALU.add)
        DVE.drain()
        for g in range(2):
            dense_pe(g, c0, g0)
            for m in range(T):
                wait_bank(DVE, g, m, c0, g0)
                o = acc[:, m, g * 512:(g + 1) * 512]
                DVE.tensor_tensor(o, o, ps[0:P, m, :], ALU.add).then_inc(S("bank_free"), 1)
                if stats_too:
                    DVE.drain()
                    stats_tile(acc, m, (g,))
            if after_half:
                after_half(g, ("bank_free", (g + g0 + 2) * T))
        DVE.drain()
        done["chunks"] += 2 * KT
        done["groups"] += 2

    def attention(layer, group0, pmt, last_stored):
        tag = f"at{layer}_"
        o = [R_XT]

        def tmp(name, shape, dt=F32):
            n = int(np.prod(shape[1:])) * 4
            p_ = o[0]
            o[0] += n + (-n) % 64
            assert o[0] <= R_XT + 2 * KT * NP2 * 4
            return at(tag + name, shape, dt, p_)

        qk = [tmp(f"qk{i}", [P, 2, T, 128]) for i in range(2)]
        vx = [tmp(f"vx{i}", [P, T, 130]) for i in range(4)]
        qt = tmp("qt", [128, 2, NODES])
        fts = [tmp(f"ft{i}", [P, 2, T, 128]) for i in range(2)]
        qft = tmp("qft", [128, NODES])
        kv = tmp("kv", [128, 130])
        bd = tmp("bd", [128, 128])
        mx = tmp("mx", [P, 2, 2 * T])
        den = tmp("den", [P, T, 2])
        eps_t = tmp("eps", [P, 1])
        scale = 64.0 ** -0.25
        loads, pe, evac = {}, {}, {}

        def load(h):
            if h >= 2:
                wait(ALE, pe["A", h - 2])
            if h >= 4:
                wait(ALE, pe["C", h - 4])
            if h == 4:
                last_stored()
            for i, dst in enumerate((qk[h % 2][:, 0], qk[h % 2][:, 1], vx[h % 4][:, :, 0:128])):
                g = group0 + 2 * i + h // 4
                c = (h % 4) * 128
                loads[h] = dma(dst, pre[g, :, :, c:c + 128].rearrange("t p f -> p t f"), tag + f"ld{h % 4}")

        load(0)
        load(1)
        DVE.memset(kv[:], 0.0)
        DVE.memset(bd[:], 0.0)
        DVE.memset(eps_t[:], 1e-4)
        for v_ in vx:
            DVE.memset(v_[:, :, 128:130], 1.0)
        mk = sig(DVE.drain(), "dve_step")
        wait(ALE, mk)
        dma(bd[0:64, 0:64], pmt, tag + "bd")
        mk_bd = dma(bd[64:128, 64:128], pmt, tag + "bd")

        def step_a(h):
            wait(PE, loads[h])
            if h:
                wait(PE, *evac["A", h - 1])
            for i in range(2):
                for m in range(T):
                    dst = ps[:, i, m * P:(m + 1) * P] if m < 4 else ps[:, 2, 128 * i:128 * i + P]
                    t_ = PE.transpose(dst, qk[h % 2][:, i, m, :], ident[0:P, 0:P])
            pe["A", h] = mk = sig(t_, tag + "pe")
            wait(DVE, mk)
            wait(ALE, mk)
            sc = scale if layer else 1.0
            DVE.tensor_scalar(qt[:, 0, 0:C1], ps[:, 0, 0:C1], sc, None, ALU.mult)
            mq = sig(DVE.tensor_scalar(qt[:, :, C1:NODES], ps[:, 2, 0:256].rearrange("p (i n) -> p i n", i=2)[:, :, 0:P],
                                       sc, None, ALU.mult), tag + "dve")
            mkk = sig(ALE.activation(qt[:, 1, 0:C1], ps[:, 1, 0:C1], ACT.Copy, scale=sc), tag + "act")
            evac["A", h] = (mq, mkk)

        def step_b(h):
            ft = fts[h % 2]
            wait(PE, *evac["A", h])
            if h == 0:
                wait(PE, mk_bd)
            for i in range(2):
                for m in range(T):
                    dst = ps[0:P, 3 + i, m * 128:(m + 1) * 128] if m < 4 else ps[0:P, 5, i * 128:(i + 1) * 128]
                    t_ = PE.matmul(dst, qt[:, i, m * P:(m + 1) * P], bd[:], start=True, stop=True)
            wait(DVE, sig(t_, tag + "pe"))
            if layer:
                for i in range(2):
                    DVE.tensor_scalar(ft[:, i, 0:4, :], ps[0:P, 3 + i, :].rearrange("p (t f) -> p t f", t=4), 0.0, 1e-6,
                                      ALU.max, ALU.add)
                mf = sig(DVE.tensor_scalar(ft[:, :, 4, :], ps[0:P, 5, 0:256].rearrange("p (i f) -> p i f", i=2), 0.0, 1e-6,
                                           ALU.max, ALU.add), tag + "dve")
            else:
                for i in range(2):
                    DVE.tensor_reduce(mx[:, i, 0:8], ps[0:P, 3 + i, :].rearrange("p (t f) -> p t f", f=64), AX.X, ALU.max)
                DVE.tensor_reduce(mx[:, :, 8:10], ps[0:P, 5, 0:256].rearrange("p (i t f) -> p i t f", i=2, f=64), AX.X, ALU.max)
                DVE.drain()
                for i in range(2):
                    DVE.tensor_tensor(ft[:, i, 0:4, :].rearrange("p t (s f) -> p (t s) f", s=2),
                                      ps[0:P, 3 + i, :].rearrange("p (t f) -> p t f", f=64),
                                      mx[:, i, 0:8].unsqueeze(2).to_broadcast([P, 8, 64]), ALU.subtract)
                mf = sig(DVE.tensor_tensor(ft[:, :, 4, :].rearrange("p i (s f) -> p i s f", s=2),
                                           ps[0:P, 5, 0:256].rearrange("p (i s f) -> p i s f", i=2, f=64),
                                           mx[:, :, 8:10].unsqueeze(3).to_broadcast([P, 2, 2, 64]), ALU.subtract),
                         tag + "dve")
            evac["B", h] = mf

        def exps(h):
            if not layer:
                wait(ALE, evac["B", h])
                fview = fts[h % 2][:].rearrange("p i t f -> p (i t) f")
                evac["B", h] = sig(ALE.activation(fview, fview, ACT.Exp, scale=scale, bias=eps_t[:]), tag + "act")

        def step_c(h):
            ft = fts[h % 2]
            wait(PE, evac["B", h])
            if h:
                wait(PE, evac["D", h - 1])
            for m in range(T):
                dst = ps[:, 6, m * P:(m + 1) * P] if m < 4 else ps[:, 7, 0:P]
                PE.transpose(dst, ft[:, 0, m, :], ident[0:P, 0:P])
            for m in range(T):
                t_ = PE.matmul(ps[:, 7, 128:258], ft[:, 1, m, :], vx[h % 4][:, m, :], start=(m == 0), stop=(m == T - 1),
                               skip_group_check=True)
            pe["C", h] = mk = sig(t_, tag + "pe")
            wait(ALE, mk)
            wait(DVE, mk)
            mq = sig(ALE.activation(qft[:, 0:C1], ps[:, 6, 0:C1], ACT.Copy), tag + "act")
            DVE.tensor_copy(qft[:, C1:NODES], ps[:, 7, 0:P])
            for s in range(2):
                r = slice(64 * s, 64 * s + 64)
                DVE.tensor_copy(kv[r, 64 * s:64 * s + 64], ps[r, 7, 128 + 64 * s:192 + 64 * s])
                DVE.tensor_copy(kv[r, 128 + s:129 + s], ps[r, 7, 256:257])
            evac["C", h] = (mq, sig(DVE.drain(), tag + "dve"))

        def step_d(h):
            wait(PE, *evac["C", h])
            for m in range(T):
                t_ = PE.matmul(ps[0:P, 6 + m // 3, 130 * (m % 3):130 * (m % 3) + 130], qft[:, m * P:(m + 1) * P], kv[:],
                               start=True, stop=True)
            wait(DVE, sig(t_, tag + "pe"))
            parts = ((6, 0, 3), (7, 3, 2))
            for bk, m0, n in parts:
                v_ = ps[0:P, bk, 0:130 * n].rearrange("p (t f) -> p t f", f=130)
                DVE.tensor_scalar(den[:, m0:m0 + n, :], v_[:, :, 128:130], 1e-6, None, ALU.add)
            DVE.drain()
            DVE.reciprocal(den[:], den[:])
            DVE.drain()
            for bk, m0, n in parts:
                v_ = ps[0:P, bk, 0:130 * n].rearrange("p (t f) -> p t f", f=130)
                t_ = DVE.tensor_tensor(nat[:, m0:m0 + n, h * 128:(h + 1) * 128].rearrange("p t (s f) -> p t s f", s=2),
                                       v_[:, :, 0:128].rearrange("p t (s f) -> p t s f", s=2),
                                       den[:, m0:m0 + n, :].unsqueeze(3).to_broadcast([P, n, 2, 64]), ALU.mult)
            evac["D", h] = sig(t_, tag + "dve")

        for h in range(HEADS2 + 2):
            if h >= 2:
                step_c(h - 2)
            if 1 <= h <= HEADS2:
                exps(h - 1)
            if h < HEADS2:
                step_a(h)
            if h >= 2:
                step_d(h - 2)
            if h < HEADS2:
                step_b(h)
            if h + 2 < HEADS2:
                load(h + 2)

    ed_src, ed_dst, ed_typ = (at(n, [P, EC], I32, R_A + 50176 - (i + 1) * 672) for i, n in enumerate(("ed_src", "ed_dst", "ed_typ")))
    for m in range(T):
        wait(DVE, dma(nat[:, m, :], a["x"][m * P:(m + 1) * P, :], f"ld_x{m}"))
        stats_tile(nat, m)
    for nm, dst in (("src", ed_src), ("dst", ed_dst), ("typ", ed_typ)):
        mk_edges = dma(dst[:], a[nm].rearrange("(p c) -> p c", c=EC), "ld_edges")

    ln_split(nat, nat)
    meet()

    def natural16():
        for m in range(T):
            DVE.tensor_copy(xn_hi[:, m, :], nat[:, m, :])
        DVE.drain()
        for m in range(T):
            DVE.tensor_tensor(xn_lo[:, m, :], nat[:, m, :], xn_hi[:, m, :], ALU.subtract)
        DVE.drain()

    adj = at("adj", [P, T, NBUCKET * P], I16, R_A)
    o_ = [R_A, R_EXTRA + 2048]

    def tmp(name, shape, dt, w=0):
        n = int(np.prod(shape[1:])) * mybir.dt.size(dt)
        p_ = o_[w]
        o_[w] += n + (-n) % 32
        assert o_[w] <= (R_A + 50176 - 3 * 672, R_EXTRA + 20480)[w], name
        return at(name, shape, dt, p_)

    scan = tmp("scan", [P, NBUCKET, EC], F32)
    key_hot = tmp("key_hot", [P, NBUCKET, EC], BF16)
    e_posi, e_tmpi = (tmp(n, [P, EC], I32) for n in ("e_posi", "e_tmpi"))
    e_tile, e_key, e_pos = (tmp(n, [P, EC], F32) for n in ("e_tile", "e_key", "e_pos"))
    b_tot, b_beg, b_off = (tmp(n, [P, NBUCKET], F32) for n in ("b_tot", "b_beg", "b_off"))
    b_grp, b_cum = (tmp(n, [128, NBUCKET], F32) for n in ("b_grp", "b_cum"))
    b_grpi = tmp("b_grpi", [128, NBUCKET], I32)
    gcol = tmp("gcol", [1, NGROUP // 4, 4], F32)
    gsumf = tmp("gsumf", [1, NGROUP // 4], F32)
    gb = at("gb", [1, NGROUP, NBUCKET], F32, R_A)
    ECP = EC + (-EC) % (3 * KT)
    e_src1, e_dl1, e_lo, e_hi = (tmp(n, [P, ECP], F32, 1) for n in ("e_src1", "e_dl1", "e_lo", "e_hi"))
    gpack = tmp("gpack", [1, NGROUP // 4], I32, 1)
    sc_per = ECP // (3 * KT)
    r_hot = R_NAT + 4 * 1280
    hot_lo = [at(f"hot_lo{i}", [P, 128], F16, r_hot + i * 256) for i in range(sc_per)]
    hot_hi = [at(f"hot_hi{i}", [P, 2, NCHUNK], F16, r_hot + sc_per * 256 + i * 960) for i in range(sc_per)]
    slot = tmp("slot", [128, 2, NCHUNK + 4], F32, 1)
    hot_s = [at(f"hot_s{i}", [128, NODES], F16, r_hot + i * 1280) for i in range(4)]
    hot_s += [tmp(f"hot_s{i}", [128, NODES], F16, 1) for i in range(4, 8)]
    hot_d = [tmp(f"hot_d{i}", [128, P], F16, 1) for i in range(8)]
    counts = [at(f"counts{i}", [P, T, P], I16, R_NAT + i * 1280) for i in range(4)]
    slot_ps = ps[:, 5, 0:2 * NCHUNK]

    def bucket_counts():
        wait(DVE, mk_edges)
        for n in (e_src1, e_dl1, e_lo, e_hi):
            DVE.memset(n[:, EC:ECP], -1.0)
        DVE.tensor_scalar(e_tile[:], ed_dst[:], float(P), None, ALU.is_ge)
        DVE.tensor_scalar(e_src1[:, 0:EC], ed_src[:], 1.0, None, ALU.add)
        DVE.drain()
        for j in range(2, T):
            DVE.tensor_scalar(e_key[:], ed_dst[:], float(j * P), None, ALU.is_ge)
            DVE.drain()
            DVE.tensor_tensor(e_tile[:], e_tile[:], e_key[:], ALU.add)
            DVE.drain()
        DVE.tensor_scalar(e_dl1[:, 0:EC], e_tile[:], -float(P), 1.0, ALU.mult, ALU.add)
        DVE.tensor_scalar(e_key[:], ed_typ[:], float(T), None, ALU.mult)
        DVE.drain()
        DVE.tensor_tensor(e_dl1[:, 0:EC], e_dl1[:, 0:EC], ed_dst[:], ALU.add)
        DVE.tensor_tensor(e_key[:], e_key[:], e_tile[:], ALU.add)
        DVE.drain()
        DVE.tensor_tensor(key_hot[:], e_key[:].unsqueeze(1).to_broadcast([P, NBUCKET, EC]),
                          iota16[0:P, 0:NBUCKET].unsqueeze(2).to_broadcast([P, NBUCKET, EC]), ALU.is_equal)
        DVE.drain()
        kh = key_hot[:].rearrange("p b c -> p (b c)")
        DVE.tensor_tensor_scan(scan[:].rearrange("p b c -> p (b c)"), kh, kh, 0.0, ALU.add, ALU.max)
        DVE.drain()
        DVE.memset(b_beg[:, 0:1], 0.0)
        DVE.tensor_copy(b_beg[:, 1:NBUCKET], scan[:, 0:NBUCKET - 1, EC - 1])
        DVE.drain()
        DVE.tensor_tensor(b_tot[:], scan[:, :, EC - 1], b_beg[:], ALU.subtract)
        return sig(DVE.drain(), "dve_step")

    def bucket_sums(mk):
        wait(PE, mk)
        PE.matmul(ps[0:P, 6, 0:NBUCKET], ltri[0:P, 0:P], b_tot[:], start=True, stop=True)
        return sig(PE.matmul(ps[:, 7, 0:NBUCKET], ones[0:P, :], b_tot[:], start=True, stop=True), "pe_step")

    def positions(mk, evacuate):
        wait(DVE, mk)
        DVE.tensor_reduce(flag[:], ps[:, 7, 0:NBUCKET], AX.X, ALU.max)
        DVE.tensor_scalar(b_grp[:], ps[:, 7, 0:NBUCKET], GROUP / 2 - 0.75, 1.0 / GROUP, ALU.add, ALU.mult)
        DVE.drain()
        DVE.tensor_scalar(flag_i[:], flag[:], 2048.0, None, ALU.is_gt)
        DVE.tensor_copy(b_grpi[:], b_grp[:])
        DVE.drain()
        DVE.tensor_copy(b_grp[:], b_grpi[:])
        DVE.drain()
        DVE.tensor_tensor_scan(b_cum[:], b_grp[:], b_grp[:], 0.0, ALU.add, ALU.max)
        DVE.drain()
        DVE.tensor_tensor(b_cum[:], b_cum[:], b_grp[:], ALU.subtract)
        DVE.drain()
        DVE.tensor_scalar(b_off[:], b_cum[0:P, :], float(GROUP), -1.0, ALU.mult, ALU.add)
        DVE.drain()
        DVE.tensor_tensor(b_off[:], b_off[:], ps[0:P, 6, 0:NBUCKET], ALU.add)
        DVE.drain()
        DVE.tensor_tensor(b_off[:], b_off[:], b_beg[:], ALU.subtract)
        DVE.drain()
        DVE.tensor_tensor(scan[:], scan[:], b_off[:].unsqueeze(2).to_broadcast([P, NBUCKET, EC]), ALU.add)
        DVE.drain()
        DVE.tensor_tensor(scan[:], scan[:], key_hot[:], ALU.mult)
        evacuate(1)
        DVE.drain()
        DVE.tensor_reduce(e_pos[:], scan[:].rearrange("p b c -> p c b"), AX.X, ALU.add)
        DVE.drain()
        DVE.tensor_copy(e_posi[:], e_pos[:])
        DVE.drain()
        DVE.tensor_scalar(e_tmpi[:], e_posi[:], 7, None, ALU.logical_shift_right)
        DVE.drain()
        DVE.tensor_copy(e_hi[:, 0:EC], e_tmpi[:])
        DVE.drain()
        DVE.tensor_scalar(e_tmpi[:], e_posi[:], 127, None, ALU.bitwise_and)
        DVE.drain()
        DVE.tensor_copy(e_lo[:, 0:EC], e_tmpi[:])
        DVE.tensor_tensor(gb[:], b_cum[0:1, :].unsqueeze(1).to_broadcast([1, NGROUP, NBUCKET]),
                          iota16[0:1, 0:NGROUP].unsqueeze(2).to_broadcast([1, NGROUP, NBUCKET]), ALU.is_le)
        DVE.drain()
        DVE.tensor_reduce(gcol[:].rearrange("o g j -> o (g j)"), gb[:], AX.X, ALU.add)
        DVE.drain()
        DVE.tensor_scalar(gsumf[:], gcol[:, :, 0], -float(1 + 2 ** 6 + 2 ** 12 + 2 ** 18), None, ALU.add)
        for j in range(1, 4):
            DVE.drain()
            DVE.scalar_tensor_tensor(gsumf[:], gcol[:, :, j], 2.0 ** (6 * j), gsumf[:], ALU.mult, ALU.add)
        DVE.drain()
        DVE.tensor_copy(gpack[:], gsumf[:])
        DVE.drain()
        evacuate(2)
        DVE.memset(adj[:], 0)
        DVE.drain()

    def scatter_dve(c, j):
        DVE.wait_ge(S("sc_pe"), c + 1)
        DVE.tensor_scalar(hot_lo[j][:], iota16[0:P, 0:128], e_lo[:, bass.ds(c, 1)], None, ALU.is_equal)
        DVE.tensor_scalar(hot_hi[j][:, 0, :], iota16[0:P, 0:NCHUNK], e_hi[:, bass.ds(c, 1)],
                          e_src1[:, bass.ds(c, 1)], ALU.is_equal, ALU.mult)
        DVE.tensor_scalar(hot_hi[j][:, 1, :], iota16[0:P, 0:NCHUNK], e_hi[:, bass.ds(c, 1)],
                          e_dl1[:, bass.ds(c, 1)], ALU.is_equal, ALU.mult).then_inc(S("sc_dve"), 1)

    def scatter_pe(c, j, last=False):
        PE.wait_ge(S("sc_dve"), c + 1)
        PE.matmul(slot_ps, hot_lo[j][:], hot_hi[j][:].rearrange("p a c -> p (a c)"), start=False,
                  stop=last).then_inc(S("sc_pe"), 1)

    def group_banks(gm):
        return ps[0:P, 5 + gm % 2, 0:C1], ps[0:P, 7, 128 * (gm % 2):128 * (gm % 2) + P]

    def hist_dve_hot(g, gm):
        for j in range(2):
            q = 2 * gm + j
            c = g * 2 + j
            DVE.wait_ge(S("hi_pe"), c + 1)
            DVE.tensor_scalar(hot_s[q][:], iota1_16[:, 0:NODES], slot[:, 0, bass.ds(c, 1)], None, ALU.is_equal)
            DVE.tensor_scalar(hot_d[q][:], iota1_16[:, 0:P], slot[:, 1, bass.ds(c, 1)], None,
                              ALU.is_equal).then_inc(S("hi_dve"), 1)

    def hist_copy(g, gm):
        b4, b1 = group_banks(gm)
        ALE.wait_ge(S("hi_pe"), 8 + 2 * g + 2)
        ALE.wait_ge(S("hi_add"), g + 1)
        ALE.activation(counts[gm][:, 4, :], b1, ACT.Copy).then_inc(S("hi_tile4"), 1)
        ALE.activation(counts[gm][:, 0:4, :], b4.rearrange("p (t d) -> p t d", t=4), ACT.Copy).then_inc(S("hi_rest"), 1)

    def hist_dve_add(g, gm, packed):
        bucket = nc.s_assert_within((packed >> (6 * gm)) & 63, 0, NBUCKET - 1,
                                    skip_runtime_bounds_check_because="a bucket's number is below NBUCKET")
        DVE.wait_ge(S("hi_tile4"), 2 + g + 1)
        DVE.wait_ge(S("hi_rest"), 2 + g + 1)
        DVE.wait_ge(S("hi_add"), 4 + g)
        o = adj[:, :, bass.ds(bucket * P, P)]
        DVE.tensor_tensor(o, o, counts[gm][:], ALU.add).then_inc(S("hi_add"), 1)

    def hist_pe_tile4(g, gm):
        PE.wait_ge(S("hi_tile4"), g + 2)
        for j in range(2):
            q = 2 * gm + j
            PE.matmul(group_banks(gm)[1], hot_s[q][:, 4 * P:5 * P], hot_d[q][:], start=(j == 0), stop=(j == 1),
                      skip_group_check=True).then_inc(S("hi_pe"), 1)

    def hist_pe(g, gm):
        hist_pe_tile4(g - 1, (gm - 1) % 4)
        b4, b1 = group_banks(gm)
        for j in range(2):
            q = 2 * gm + j
            PE.wait_ge(S("hi_dve"), g * 2 + j + 1)
            if j == 0:
                PE.wait_ge(S("hi_rest"), g + 1)
            for m in range(4):
                PE.matmul(b4[:, m * P:(m + 1) * P], hot_s[q][:, m * P:(m + 1) * P], hot_d[q][:],
                          start=(j == 0 and m == 0), stop=(j == 1), skip_group_check=True)

    def beside(dense, evacuate, load_bias, store):
        dense(0)
        mk = bucket_counts()
        mk = bucket_sums(mk)
        dense(1)
        evacuate(0)
        positions(mk, evacuate)
        dense(2)
        dense(3)
        natural16()
        evacuate(3)
        PE.sem_inc(S("sc_pe"), sc_per)
        zero16 = hot_s[4][0:P, 0:128]
        DVE.memset(zero16, 0.0)
        DVE.memset(hot_s[5][0:P, 0:2 * NCHUNK], 0.0)
        DVE.memset(slot[:, :, NCHUNK:NCHUNK + 4], 0.0)
        for q in (6, 7):
            DVE.memset(hot_s[q][:], 0.0)
            DVE.memset(hot_d[q][:], 0.0)
        mk = sig(DVE.drain(), "dve_step")
        wait(PE, mk)
        PE.matmul(slot_ps, zero16, hot_s[5][0:P, 0:2 * NCHUNK], start=True, stop=False)

        def scatter_step(i):
            def between(k, m):
                for j in range(sc_per):
                    if j * T // sc_per == m:
                        scatter_pe((i * KT + k) * sc_per + j, j)
            return between

        with PE.Fori(0, 3) as i:
            dense(i + 4, scatter_step(i))
        with DVE.Fori(0, 3) as i:
            for k in range(KT):
                for j in range(sc_per):
                    scatter_dve((i * KT + k) * sc_per + j, j)
            evacuate(i + 4)
        PE.matmul(slot_ps, zero16, hot_s[5][0:P, 0:2 * NCHUNK], start=False, stop=True).then_inc(S("sc_pe"), 1)
        DVE.wait_ge(S("sc_pe"), sc_per + ECP + 1)
        DVE.tensor_copy(slot[:, :, 0:NCHUNK], slot_ps.rearrange("p (a c) -> p a c", a=2))
        DVE.drain()
        DVE.sem_inc(S("hi_add"), 4)
        ALE.sem_inc(S("hi_tile4"), 2)
        ALE.sem_inc(S("hi_rest"), 2)
        PE.sem_inc(S("hi_pe"), 6)
        per = NGROUP // (3 * KT)
        assert per == T and per * 3 * KT == NGROUP
        with PE.Fori(0, 3) as i:
            dense(i + 7, lambda k, m: hist_pe((i * KT + k) * T + m, (k * T + m) % 4))
        hist_pe_tile4(NGROUP - 1, (NGROUP - 1) % 4)
        with ALE.Fori(0, 3) as i:
            load_bias(i + 7)
            for n in range(per * KT):
                if n == per * KT - 1:
                    store(i + 7)
                hist_copy(i * per * KT + n, n % 4)
        for n in range(2):
            hist_dve_hot(n, n)
        with DVE.Fori(0, 3) as i:
            for n in range(per * KT):
                if n == per * KT - 1:
                    evacuate(i + 7)
                hist_dve_hot(i * per * KT + n + 2, (n + 2) % 4)
                if n % 4 == 0:
                    packed = DVE.value_load(gpack[0:1, bass.ds(i * (per * KT // 4) + n // 4, 1)],
                                            min_val=0, max_val=2 ** 24 - 1)
                hist_dve_add(i * per * KT + n, n % 4, packed)

    last_stored = dense_to_pre(G_PRE0, B_PRE0, beside, beside_last=3)
    meet()

    attention(0, 4, a["pm0"], last_stored)
    meet()
    transpose_split(nat, 128, KT, xt_hi, xt_lo)
    meet()
    x_res = at("x_res", [P, T, D], F32, R_NAT)
    mk = dma(x_res[:], a["x"].rearrange("(t p) d -> p t d", p=P), "ld_x2")
    wait(DVE, mk)
    a_hi = at("a_hi", [P, T, NODES], F16, R_EXTRA)
    a_lo = at("a_lo", [P, T, NODES], F16, R_EXTRA + 6272)
    rcnt = at("rcnt", [128, NP2], F32, R_EXTRA + 2 * 6272)
    mtmp = [at(f"mtmp{i}", [128, H0], F32, R_EXTRA + 2 * 6272 + 2560 + i * 1280) for i in range(4)]
    halves = ((0, H0), (H0, H1))
    DVE.sem_inc(S("ag_free"), 3)
    DVE.sem_inc(S("mt_ready"), 1)
    PE.sem_inc(S("ag_full"), 1)

    def counts_split(r):
        DVE.wait_ge(S("ag_full"), r * 18 + 1)
        DVE.tensor_copy(a_hi[:], adj[:, :, bass.ds(r * NODES, NODES)]).then_inc(S("a_hi"), 1)
        DVE.wait_ge(S("a_hi"), r + 1)
        DVE.tensor_tensor(a_lo[:], adj[:, :, bass.ds(r * NODES, NODES)], a_hi[:], ALU.subtract).then_inc(S("a_ready"), 1)

    counts_split(0)
    x1p_halves = x1p.rearrange("p (t d) -> p t d", t=T)
    x1p_stored = []

    def store_half(g, evacuated):
        wait(ALE, evacuated)
        x1p_stored.append(dma(x1p_halves[:, :, g * 512:(g + 1) * 512], x_res[:, :, g * 512:(g + 1) * 512], f"st_x1p{g}"))

    dense_add(x_res, B_PROJ0, "proj0", after_half=store_half)

    u_loaded = []
    for g in range(2):
        wait(ALE, x1p_stored[g])
        u_loaded.append(dma(nat[:, :, g * 512:(g + 1) * 512], pre[g].rearrange("t p f -> p t f"), f"ld_u{g}"))
    c0, g0 = done["chunks"], done["groups"]
    many = PE.value_load(flag_i[0:1, 0:1], min_val=0, max_val=1)

    def ag_bank(i):
        return 5 + i % 3, *halves[i % 2]

    def counts_pe(r):
        PE.wait_ge(S("a_ready"), r + 1)
        for i in range(2):
            bank, h0, hn = ag_bank(i)
            PE.wait_ge(S("ag_free"), r * 18 + i + 1)

            def add(a16, t, first, last):
                return PE.matmul(ps[:, bank, 0:hn], ones16[0:P, :], a16[:, t, h0:h0 + hn], start=first, stop=last)

            for t in range(T - 1):
                add(a_hi, t, t == 0, False)
            with PE.If(many):
                for t in range(T):
                    add(a_lo, t, False, False)
            add(a_hi, T - 1, False, True).then_inc(S("ag_full"), 1)

    def relation_pe(r, more):
        for i in range(2, 18):
            bank, h0, hn = ag_bank(i)
            PE.wait_ge(S("ag_free"), r * 18 + i + 1)
            k = i // 2 - 1
            dst = ps[:, bank, 0:hn]

            def agg(x16, a16, t, first, last):
                return PE.matmul(dst, x16[:, t, k * 128:(k + 1) * 128], a16[:, t, h0:h0 + hn], start=first, stop=last)

            for t in range(T):
                agg(xn_hi, a_hi, t, t == 0, False)
            with PE.If(many):
                for t in range(T):
                    agg(xn_hi, a_lo, t, False, False)
                    agg(xn_lo, a_lo, t, False, False)
            for t in range(T):
                t_ = agg(xn_lo, a_hi, t, False, t == T - 1)
            t_.then_inc(S("ag_full"), 1)

        def mean_ready(k):
            PE.wait_ge(S("mt_ready"), 1 + r * 16 + 2 * k + 2)
        dense_pe(r * 2, c0, g0, mean_ready)
        if more:
            counts_pe(r + 1)
        dense_pe(r * 2 + 1, c0, g0)

    counts_pe(0)
    with PE.Fori(0, REL - 1) as r:
        relation_pe(r, True)
    with PE.Fori(REL - 1, REL) as r:
        relation_pe(r, False)
    with ALE.Fori(0, REL) as r:
        for i in range(2, 18):
            h0, hn = halves[i % 2]
            j = i - 2
            ALE.wait_ge(S("ag_scaled"), r * 16 + j + 1)
            ALE.activation(xt_hi[:, j // 2, h0:h0 + hn], mtmp[j % 4][:, 0:hn], ACT.Copy).then_inc(S("mt_hi"), 1)

    def counts_dve(r):
        for i in range(2):
            bank, h0, hn = ag_bank(i)
            DVE.wait_ge(S("ag_full"), r * 18 + i + 2)
            DVE.tensor_scalar(rcnt[:, h0:h0 + hn], ps[:, bank, 0:hn], 1.0, None, ALU.max).then_inc(S("ag_free"), 1)
        DVE.wait_ge(S("ag_free"), 3 + r * 18 + 2)
        DVE.reciprocal(rcnt[:, 0:NODES], rcnt[:, 0:NODES]).then_inc(S("rcnt"), 1)

    def relation_dve(r, more):
        DVE.wait_ge(S("rcnt"), r + 1)

        def low(j):
            h0, hn = halves[j % 2]
            DVE.wait_ge(S("mt_hi"), r * 16 + j + 1)
            DVE.tensor_tensor(xt_lo[:, j // 2, h0:h0 + hn], mtmp[j % 4][:, 0:hn],
                              xt_hi[:, j // 2, h0:h0 + hn].bitcast(F32), ALU.subtract).then_inc(S("mt_ready"), 1)

        for j in range(16):
            i = j + 2
            bank, h0, hn = ag_bank(i)
            DVE.wait_ge(S("ag_full"), r * 18 + i + 2)
            DVE.wait_ge(S("mt_ready"), 1 + r * 16 + max(j - 3, 0))
            DVE.tensor_tensor(mtmp[j % 4][:, 0:hn], ps[:, bank, 0:hn], rcnt[:, h0:h0 + hn],
                              ALU.mult).then_inc(S("ag_free"), 1)
            DVE.wait_ge(S("ag_free"), 3 + r * 18 + i + 1)
            DVE.sem_inc(S("ag_scaled"), 1)
            if j >= 1:
                low(j - 1)
        low(15)
        if more:
            counts_split(r + 1)
        DVE.wait_ge(S("c_sum"), r + 1)
        DVE.tensor_tensor(c_sum[:], c_sum[:], adj[:, :, bass.ds(r * NODES, NODES)], ALU.add).then_inc(S("c_sum"), 1)
        if not more:
            last_relation()
        for gg in range(2):
            if gg and more:
                counts_dve(r + 1)
            wait(DVE, u_loaded[gg])
            for m in range(T):
                wait_bank(DVE, r * 2 + gg, m, c0, g0)
                u_ = nat[:, m, gg * 512:(gg + 1) * 512]
                DVE.wait_ge(S("bank_free"), (r * 2 + g0) * T + T)
                DVE.tensor_tensor(u_, u_, ps[0:P, m, :], ALU.add).then_inc(S("bank_free"), 1)

    c_sum = at("c_sum", [P, T, NODES], I16, R_RING)
    z = at("z", [P, T, D], F32, R_A)
    x1 = at("x1", [P, T, D], F32, R_A + T * D * 4)
    lng = at("lng", [P, D], F32, R_A + 2 * T * D * 4)
    lnb = at("lnb", [P, D], F32, R_A + 2 * T * D * 4 + D * 4)
    w1 = at("w1", [128, KT, FFN0], F32, R_EXTRA)
    w2 = at("w2", [128, FFN0 // 128, D], F32, R_EXTRA + 8192)

    def last_relation():
        DVE.drain()
        DVE.tensor_reduce(va[:], c_sum[:], AX.X, ALU.add)
        DVE.drain()
        DVE.tensor_scalar(va[:], va[:], 1.0, None, ALU.add)
        mk = sig(DVE.drain(), "dve_step")
        wait(ALE, mk)
        loads["c"] = dma(c_dram[:], c_sum[:].rearrange("p t d -> p (t d)"), "st_c")
        loads["x1"] = dma(x1[:].rearrange("p t d -> p (t d)"), x1p[:], "ld_x1")
        dma(w1[:], a["w1t"], "ld_w12")
        loads["w"] = dma(w2[:], a["w2t"], "ld_w12")
        for g in range(2):
            loads["z"] = dma(z[:, :, g * 512:(g + 1) * 512], pre[2 + g].rearrange("t p f -> p t f"), "ld_z")
        dma(lng[:], a["ln_g"].to_broadcast([P, D]), "ld_ln")
        loads["ln"] = dma(lnb[:], a["ln_b"].to_broadcast([P, D]), "ld_ln")
        mk = sig(ALE.activation(t5[:], va[:], ACT.Sqrt), "act_step")
        wait(DVE, mk)
        newton_rsqrt()
        DVE.tensor_copy(dis[:], rs[:])

    loads = {}
    DVE.memset(c_sum[:], 0).then_inc(S("c_sum"), 1)
    counts_dve(0)
    with DVE.Fori(0, REL - 1) as r:
        relation_dve(r, True)
    relation_dve(REL - 1, False)
    done["chunks"] += REL * 2 * KT
    done["groups"] += REL * 2
    meet()

    w1q = at("w1q", [128, KT, FFN0], BF16, R_RING)
    w2q = at("w2q", [128, FFN0 // 128, D], BF16, R_RING + 4096)
    gsum = small("gsum", [128, 2], F32)
    transpose_split(nat, 128, KT, xt_hi, xt_lo)
    wait(ALE, loads["c"])
    meet()
    for m in range(T):
        mk_t = sig(ALE.activation(nat[:, m, :], nat[:, m, :], ACT.Tanh), "act_step")
    c0, g0 = done["chunks"], done["groups"]
    dense_pe(0, c0, g0)
    wait(DVE, loads["w"])
    for i, w in enumerate((w1, w2)):
        DVE.tensor_reduce(gsum[:, i:i + 1], w[:].rearrange("p k f -> p (k f)"), AX.X, ALU.add, apply_absolute_value=True)
    mk = sig(DVE.drain(), "dve_step")
    wait(PE, mk)
    mk_g = sig(PE.matmul(ps[:, 5, 0:2], ones[:], gsum[:], start=True, stop=True), "pe_step")
    dense_pe(1, c0, g0)
    wait(DVE, mk_t, loads["x1"])
    for m in range(T):
        for n in (nat, x1):
            DVE.tensor_tensor(n[:, m, :], n[:, m, :], xn_hi[:, m, :], ALU.subtract if n is nat else ALU.add)
        DVE.drain()
        for n in (nat, x1):
            DVE.tensor_tensor(n[:, m, :], n[:, m, :], xn_lo[:, m, :], ALU.subtract if n is nat else ALU.add)
    def gate_evac(g):
        c = slice(g * 512, g * 512 + 512)
        for m in range(T):
            DVE.tensor_tensor(z[:, m, c], z[:, m, c], nat[:, m, c], ALU.mult)
        DVE.drain()
        for m in range(T):
            DVE.tensor_tensor(x1[:, m, c], x1[:, m, c], z[:, m, c], ALU.add)
        DVE.drain()
        for m in range(T):
            wait_bank(DVE, g, m, c0, g0)
            DVE.tensor_tensor(z[:, m, c], nat[:, m, c], ps[0:P, m, :], ALU.mult).then_inc(S("bank_free"), 1)
            DVE.wait_ge(S("bank_free"), (g + g0 + 1) * T + m + 1)
            DVE.tensor_tensor(x1[:, m, c], x1[:, m, c], z[:, m, c], ALU.add)
            DVE.drain()
            stats_tile(x1, m, (g,))

    wait(DVE, loads["z"])
    DVE.drain()
    gate_evac(0)
    MAGIC = 1.5 * 2.0 ** 23
    wait(DVE, mk_g)
    DVE.tensor_scalar(gam[:], ps[:, 5, 0:2], 1.0 / (FFN0 * D), 1e-5, ALU.mult, ALU.add)
    DVE.drain()
    DVE.reciprocal(rgam[:], gam[:])
    DVE.drain()
    for i, (w, wq) in enumerate(((w1, w1q), (w2, w2q))):
        wf = w[:].rearrange("p k f -> p (k f)")
        DVE.tensor_scalar(wf, wf, rgam[:, i:i + 1], 1.0, ALU.mult, ALU.min)
        DVE.drain()
        DVE.tensor_scalar(wf, wf, -1.0, MAGIC, ALU.max, ALU.add)
        mk = sig(DVE.drain(), "dve_step")
        wait(ALE, mk)
        ALE.activation(wq[:].rearrange("p k f -> p (k f)"), wf, ACT.Copy, bias=-MAGIC)
    gate_evac(1)
    done["chunks"] += 2 * KT
    done["groups"] += 2
    DVE.drain()

    stats_finish()
    DVE.tensor_copy(rs_first[:], rs[:])
    DVE.tensor_tensor(t5[:], rs[:], rs[:], ALU.mult)
    DVE.drain()
    DVE.tensor_tensor(va[:], t5[:], mv[:, :, 1], ALU.mult)
    DVE.drain()
    DVE.tensor_scalar(va[:], va[:], 1e-5, None, ALU.add)
    mk = sig(DVE.drain(), "dve_step")
    wait(ALE, mk)
    mk = sig(ALE.activation(t5[:], va[:], ACT.Sqrt), "act_step")
    wait(DVE, mk)
    newton_rsqrt()
    DVE.tensor_tensor(rs[:], rs[:], rs_first[:], ALU.mult)
    DVE.drain()
    wait(DVE, loads["ln"])
    for m in range(T):
        DVE.scalar_tensor_tensor(nat[:, m, :], x1[:, m, :], mv[:, m, 0:1], lng[:], ALU.subtract, ALU.mult)
    DVE.drain()
    for m in range(T):
        DVE.scalar_tensor_tensor(nat[:, m, :], nat[:, m, :], rs[:, m:m + 1], lnb[:], ALU.mult, ALU.add)
    DVE.drain()
    meet()

    q_top8 = small("q_top8", [P, 8], F32)
    q_hot8 = small("q_hot8", [P, 15, 8], F32)
    q_thr = small("q_thr", [P, 15], F32)
    q_cnt15 = small("q_cnt15", [P, 15], F32)
    q_ok15 = small("q_ok15", [128, 15], F32)
    q_steps = small("q_steps", [128, 3], F32)
    q_halves = small("q_halves", [128, 3], F32)
    q_full = small("q_full", [P, 1], F32)
    q_many = small("q_many", [128, 1], I32)

    def find_rank(h, width, rank):
        n = T * width
        tag = f"q{width}"
        hf = h[:].rearrange("p t d -> p (t d)")
        key_hi = at(tag + "_hi", [P, n], I16, R_XN)
        key_lo = at(tag + "_lo", [P, n], U16, R_XN + 10240)
        mask = at(tag + "_mask", [P, n], BF16, R_EXTRA)
        pieces = (12, 12, 10, 6) if n > 4 * 1024 else (6, 4)
        starts = [sum(pieces[:j]) for j in range(len(pieces))]
        assert sum(pieces) * 128 == n
        halves_of = lambda dt: hf.bitcast(dt).rearrange("p (n two) -> p n two", two=2)
        mk = sig(DVE.drain(), "dve_step")
        wait(ALE, mk)
        mk_lo = sig(ALE.activation(key_lo[:], halves_of(U16)[:, :, 0], ACT.Copy), "act_step")
        DVE.memset(q_rank[:], float(rank))
        DVE.tensor_scalar(key_hi[:], halves_of(I16)[:, :, 1], 0x7FFF, None, ALU.bitwise_and)
        DVE.drain()

        def count_pe(name, i):
            for c in range(n // 128):
                if c in starts:
                    PE.wait_ge(S(name + "_mask"), i * len(pieces) + starts.index(c) + 1)
                t_ = PE.matmul(ps[:, 0, 0:1], mask[:, c * 128:(c + 1) * 128], ones_b[0:P, :], start=(c == 0),
                               stop=(c == n // 128 - 1))
            t_.then_inc(S(name + "_part"), 1)
            PE.wait_ge(S(name + "_copied"), i + 1)
            PE.matmul(ps[:, 1, 0:1], ones[:], q_part[:], start=True, stop=True).then_inc(S(name + "_count"), 1)

        def count_dve(name, i, keys, beside=None):
            for j, n_ in enumerate(pieces):
                c = slice(starts[j] * 128, (starts[j] + n_) * 128)
                DVE.tensor_scalar(mask[:, c], keys[:, c], q_took[0:P, :], q_cand[0:P, :], ALU.subtract,
                                  ALU.is_ge).then_inc(S(name + "_mask"), 1)
            DVE.wait_ge(S(name + "_part"), i + 1)
            DVE.tensor_copy(q_part[:], ps[:, 0, 0:1]).then_inc(S(name + "_copied"), 1)
            if beside:
                beside()
                DVE.drain()
            DVE.wait_ge(S(name + "_count"), i + 1)

        def bisect(name, keys, top, rounds, unroll):
            DVE.memset(q_cand[:], top)
            DVE.memset(q_took[:], 0.0)
            for j in range(unroll):
                DVE.memset(q_steps[:, j:j + 1], top / 2 ** j)
                DVE.memset(q_halves[:, j:j + 1], -top / 2 ** (j + 1))
            DVE.drain()
            with DVE.Fori(0, rounds // unroll) as i:
                for j in range(unroll):
                    count_dve(name, i * unroll + j, keys, lambda: DVE.scalar_tensor_tensor(
                        q_cand[:], q_took[:], q_halves[:, j:j + 1], q_cand[:], ALU.add, ALU.add))
                    DVE.tensor_scalar(q_took[:], ps[:, 1, 0:1], q_rank[:], q_steps[:, j:j + 1], ALU.is_ge, ALU.mult)
                    DVE.drain()
                DVE.tensor_scalar(q_steps[:], q_steps[:], 0.5 ** unroll, None, ALU.mult)
                DVE.tensor_scalar(q_halves[:], q_halves[:], 0.5 ** unroll, None, ALU.mult)
                DVE.drain()
            DVE.scalar_tensor_tensor(q_cand[:], q_cand[:], -0.5, q_took[:], ALU.add, ALU.add)
            DVE.drain()

        with PE.Fori(0, 5) as i:
            for j in range(3):
                count_pe(tag + "a", i * 3 + j)
        count_pe(tag + "b", 0)
        bisect(tag + "a", key_hi, 2.0 ** 14, 15, 3)
        DVE.tensor_copy(q_top[:], q_cand[:])
        DVE.memset(q_took[:], 1.0)
        DVE.drain()
        count_dve(tag + "b", 0, key_hi)
        DVE.tensor_tensor(q_rank[:], q_rank[:], ps[:, 1, 0:1], ALU.subtract)
        wait(DVE, mk_lo)
        DVE.scalar_tensor_tensor(key_lo[:], key_hi[:], q_top[0:P, :], key_lo[:], ALU.is_equal, ALU.mult)
        DVE.drain()
        DVE.max(q_top8[:], key_lo[:])
        DVE.drain()
        DVE.tensor_scalar(q_full[:], q_top8[:, 7:8], 0.5, None, ALU.is_gt)
        mk = sig(DVE.drain(), "dve_step")
        wait(PE, mk)
        mk = sig(PE.matmul(ps[:, 2, 0:1], ones[0:P, :], q_full[:], start=True, stop=True), "pe_step")
        DVE.memset(q_cand[:], 0.0)
        for r in range(4):
            step = 16.0 ** (3 - r)
            DVE.drain()
            DVE.tensor_scalar(q_thr[:], iota1_16[0:P, 0:15], step, q_cand[0:P, :], ALU.mult, ALU.add)
            DVE.drain()
            DVE.tensor_tensor(q_hot8[:], q_top8[:].unsqueeze(1).to_broadcast([P, 15, 8]),
                              q_thr[:].unsqueeze(2).to_broadcast([P, 15, 8]), ALU.is_ge)
            DVE.drain()
            DVE.tensor_reduce(q_cnt15[:], q_hot8[:], AX.X, ALU.add)
            m15 = sig(DVE.drain(), "dve_step")
            wait(PE, m15)
            m15 = sig(PE.matmul(ps[:, 3, 0:15], ones[0:P, :], q_cnt15[:], start=True, stop=True), "pe_step")
            wait(DVE, m15)
            DVE.tensor_scalar(q_ok15[:], ps[:, 3, 0:15], q_rank[:], None, ALU.is_ge, ALU.add, accum_out=q_took[:])
            DVE.drain()
            DVE.scalar_tensor_tensor(q_cand[:], q_took[:], step, q_cand[:], ALU.mult, ALU.add)
        wait(DVE, mk)
        DVE.tensor_scalar(q_many[:], ps[:, 2, 0:1], 0.5, None, ALU.is_gt)
        mk = sig(DVE.drain(), "dve_step")
        wait(PE, mk)
        with PE.Fori(0, 1) as _:
            with PE.If(PE.value_load(q_many[0:1, 0:1], min_val=0, max_val=1)):
                with PE.Fori(0, 16) as i:
                    count_pe(tag + "c", i)
        with DVE.Fori(0, 1) as _:
            with DVE.If(DVE.value_load(q_many[0:1, 0:1], min_val=0, max_val=1)):
                bisect(tag + "c", key_lo, 2.0 ** 15, 16, 1)
        DVE.tensor_copy(qcur[:], q_top[:])
        DVE.tensor_copy(qcand[:], q_cand[:])
        DVE.drain()
        DVE.tensor_scalar(qcur[:], qcur[:], 16, None, ALU.logical_shift_left)
        DVE.drain()
        DVE.tensor_tensor(qcur[:], qcur[:], qcand[:], ALU.bitwise_or)
        DVE.drain()

    def quant_scale(i):
        DVE.tensor_scalar(qs[:], qcur[:].bitcast(F32), 1e-5, None, ALU.max)
        DVE.drain()
        DVE.tensor_scalar(qrs[:], qs[:], gam[:, i:i + 1], 1.0 / 127.0, ALU.mult, ALU.mult)
        DVE.reciprocal(qs[:], qs[:])
        DVE.drain()
        DVE.tensor_scalar(qs[:], qs[:], 127.0, None, ALU.mult)
        DVE.drain()

    ps16 = ps[:].bitcast(BF16)

    def quant_product(h, hq, width, hqt, product):
        nk = width // 128
        back = {}

        def front(m):
            DVE.tensor_scalar(h[:, m, :], h[:, m, :], qs[0:P, :], 127.0, ALU.mult, ALU.min)
            DVE.drain()
            DVE.tensor_scalar(h[:, m, :], h[:, m, :], -128.0, MAGIC, ALU.max, ALU.add)
            wait(ALE, sig(DVE.drain(), "dve_step"))
            wait(PE, sig(ALE.activation(hq[:, m, :], h[:, m, :], ACT.Copy, bias=-MAGIC), "act_step"))
            if m >= 2:
                wait(PE, back[m - 2])
            for k in range(nk):
                t_ = PE.transpose(ps16[:, 6 + m % 2, k * 128:k * 128 + P], hq[:, m, k * 128:(k + 1) * 128], ident16[0:P, 0:P])
            return sig(t_, "pe_step")

        def rest(m, mk):
            wait(DVE, mk)
            back[m] = sig(DVE.tensor_copy(hqt[:, :, m * P:(m + 1) * P],
                                          ps16[:, 6 + m % 2, 0:nk * 128].rearrange("p (k n) -> p k n", k=nk)[:, :, 0:P]), "dve_step")
            wait(PE, back[m])
            product(m)

        marks = [front(0)]
        for m in range(T):
            if m + 1 < T:
                marks.append(front(m + 1))
            rest(m, marks[m])

    hq = at("hq", [P, T, D], BF16, R_EXTRA)
    hqt = at("hqt", [128, KT, NODES], BF16, R_XN)
    gl = at("gl", [P, T, FFN0], F32, R_NAT)
    glq = at("glq", [P, T, FFN0], BF16, R_EXTRA)
    glt = at("glt", [128, FFN0 // 128, NODES], BF16, R_XN)

    find_rank(nat, D, 3201)
    quant_scale(0)

    def up0(m):
        for k in range(KT):
            t_ = PE.matmul(ps[0:P, m, 0:FFN0], hqt[:, k, m * P:(m + 1) * P], w1q[:, k, :], start=(k == 0), stop=(k == KT - 1))
        up_marks.append(sig(t_, "pe_step"))

    up_marks = []
    quant_product(nat, hq, D, hqt, up0)
    for m in range(T):
        wait(ALE, up_marks[m])
        mk = sig(ALE.activation(gl[:, m, :], ps[0:P, m, 0:FFN0], ACT.Gelu, scale=qrs[0:P, :]), "act_step")
    wait(DVE, mk)
    meet()
    find_rank(gl, FFN0, 801)
    quant_scale(1)
    down_free = {}

    def down0(m):
        for h in range(2):
            n = 2 * m + h
            if n >= 6:
                wait(PE, down_free[n - 6])
            for k in range(FFN0 // 128):
                t_ = PE.matmul(ps[0:P, n % 6, :], glt[:, k, m * P:(m + 1) * P], w2q[:, k, h * 512:(h + 1) * 512], start=(k == 0),
                               stop=(k == FFN0 // 128 - 1))
            wait(DVE, sig(t_, "pe_step"))
            o = x1[:, m, h * 512:(h + 1) * 512]
            down_free[n] = sig(DVE.scalar_tensor_tensor(o, ps[0:P, n % 6, :], qrs[0:P, :], o, ALU.mult, ALU.add), "dve_step")
        DVE.drain()
        stats_tile(x1, m)

    quant_product(gl, glq, FFN0, glt, down0)
    DVE.drain()
    meet()

    ct_hi = at("ct_hi", [P, T, NP2], F32R, R_EXTRA + 2048)
    ct_lo = [at(f"ct_lo{k}", [P, NP2], F32R, R_A + 2 * T * D * 4 + k * 2560 if k < 3 else R_EXTRA + 2048 + 12544 + (k - 3) * 2528)
             for k in range(T)]
    c16 = at("c16", [P, T, NODES], I16, R_A + 2 * T * D * 4)
    c_nat = at("c_nat", [P, T, NODES], F32, R_NAT)
    hp_hi = at("hp_hi", [P, T, D], F32R, R_NAT)
    hp_lo = at("hp_lo", [P, T, D], F32R, R_XN)
    h_nat = at("h_nat", [P, T, D], F32, R_XN)
    mc = dma(c16[:].rearrange("p t d -> p (t d)"), c_dram[:], "ld_c")
    ln_split(x1, nat)

    def beside1(dense, evacuate, load_bias, store):
        def ct_pe(k, m):
            if m < T - 1 or k >= T:
                return
            PE.wait_ge(S("ct_done"), k + 1)
            for t in range(T):
                dst = ps[0:P, 5, t * P:(t + 1) * P] if t < 4 else ps[0:P, 6, 0:P]
                t_ = PE.transpose(dst, c_nat[:, t, k * P:(k + 1) * P], ident[0:P, 0:P])
            t_.then_inc(S("ct_full"), 1)

        dense(0, ct_pe)
        wait(DVE, mc)
        DVE.tensor_copy(c_nat[:], c16[:])
        DVE.drain()
        for t in range(T):
            b = c_nat[:, t, t * P:(t + 1) * P]
            DVE.tensor_tensor(b, b, ident[0:P, 0:P], ALU.add)
        DVE.drain().then_inc(S("ct_done"), 1)
        for k in range(T):
            DVE.wait_ge(S("ct_full"), k + 1)
            parts = ((ps[0:P, 5, 0:C1], slice(0, C1)), (ps[0:P, 6, 0:C2], slice(C1, NODES)))
            for src, c in parts:
                DVE.tensor_copy(ct_hi[:, k, c], src)
            DVE.drain()
            for src, c in parts:
                t_ = DVE.tensor_tensor(ct_lo[k][:, c], src, ct_hi[:, k, c].bitcast(F32), ALU.subtract)
            t_.then_inc(S("ct_done"), 1)
        evacuate(0)
        with PE.Fori(1, G_PRE1) as g:
            dense(g)
        with DVE.Fori(1, 3) as g:
            evacuate(g)
        wait(DVE, *h_loaded)
        for t in range(T):
            DVE.tensor_scalar(h_nat[:, t, :], h_nat[:, t, :], dis[:, t:t + 1], None, ALU.mult)
        DVE.drain()
        for t in range(T):
            DVE.tensor_copy(hp_hi[:, t, :], h_nat[:, t, :])
        DVE.drain()
        for t in range(T):
            DVE.tensor_tensor(hp_lo[:, t, :], h_nat[:, t, :], hp_hi[:, t, :].bitcast(F32), ALU.subtract)
        with DVE.Fori(3, G_PRE1) as g:
            evacuate(g)

    h_loaded = []

    def load_h(stored):
        stored(1)
        for g in range(2):
            h_loaded.append(dma(h_nat[:, :, g * 512:(g + 1) * 512], pre[g].rearrange("t p f -> p t f"), "ld_h"))

    last_stored = dense_to_pre(G_PRE1, B_PRE1, beside1, after_two=load_h)
    meet()
    free = []
    for n in range(2 * T):
        m, h = n // 2, n % 2
        if n >= 8:
            wait(PE, free[n - 8])
        for k in range(T):
            c = slice(m * P, (m + 1) * P)
            t_ = three(ps[0:P, n % 8, :], ct_hi[:, k, c], ct_lo[k][:, c],
                       hp_hi[:, k, h * 512:(h + 1) * 512], hp_lo[:, k, h * 512:(h + 1) * 512], k == 0, k == T - 1)
        wait(DVE, sig(t_, "pe_step"))
        o = x1[:, m, h * 512:(h + 1) * 512]
        free.append(sig(DVE.scalar_tensor_tensor(o, ps[0:P, n % 8, :], dis[:, m:m + 1], o, ALU.mult, ALU.add), "dve_step"))
    meet()
    attention(1, 2, a["pm1"], last_stored)
    meet()
    transpose_split(nat, 128, KT, xt_hi, xt_lo)
    meet()
    wr = at("wr", [128, KT, NEXP], F32, R_EXTRA)
    wr_hi = at("wr_hi", [128, KT, NEXP], F32R, R_EXTRA + 256)
    wr_lo = at("wr_lo", [128, KT, NEXP], F32R, R_EXTRA + 512)
    rb = at("rb", [P, NEXP], F32, R_EXTRA + 768)
    pr = at("pr", [P, T, NEXP], F32, R_EXTRA + 1024)
    cw = at("cw", [P, T, NEXP], F32, R_EXTRA + 1280)
    gt = at("gt", [P, T, NEXP, NEXP], F32, R_EXTRA + 1536)
    eq = at("eq", [P, T, NEXP, NEXP], F32, R_EXTRA + 1536 + 1280)
    low = at("low", [P, NEXP, NEXP], F32, R_EXTRA + 1536 + 2560)
    lgt = at("lgt", [NEXP, NP2], F32, R_EXTRA + 4608)
    sil = [at(f"sil{i}", [P, 2, HID], F32, R_RING + i * 1024) for i in range(4)]
    DVE.memset(low[:], 0.0)
    DVE.drain()
    for e in range(1, NEXP):
        DVE.memset(low[:, e, 0:e], 1.0)
    mk = dma(wr[:], a["wrt"], "ld_wr")
    mk = dma(rb[:], a["rb"].to_broadcast([P, NEXP]), "ld_wr")
    dense_add(x1, B_PROJ1, "proj1", stats_too=True)
    wait(DVE, mk)
    DVE.tensor_copy(wr_hi[:], wr[:])
    DVE.drain()
    DVE.tensor_tensor(wr_lo[:], wr[:], wr_hi[:].bitcast(F32), ALU.subtract)
    for n in (xt_hi, xt_lo):
        DVE.tensor_copy(n[:, :, NODES:NP2], zero[:].unsqueeze(1).to_broadcast([128, KT, 1]))
    mk_wr = sig(DVE.drain(), "dve_step")
    meet()

    ln_split(x1, nat)
    wait(PE, mk_wr)
    for i, (h0, hn) in enumerate(((0, 314), (314, 312))):
        for k in range(KT):
            t_ = three(ps[0:NEXP, 5 + i, 0:hn], wr_hi[:, k, :], wr_lo[:, k, :], xt_hi[:, k, h0:h0 + hn], xt_lo[:, k, h0:h0 + hn],
                       k == 0, k == KT - 1)
        mk = sig(t_, "pe_step")
        wait(DVE, mk)
        mk_lg = sig(DVE.tensor_copy(lgt[:, h0:h0 + hn], ps[0:NEXP, 5 + i, 0:hn]), "dve_step")

    hid = at("hid", [P, T, (NEXP + 1) * HID], F32, R_XN)
    c0, g0 = done["chunks"], done["groups"]

    def turn(k, m):
        if (k, m) == (0, T - 1):
            wait(PE, mk_lg)
            for t in range(T):
                t_ = PE.transpose(ps[0:P, 7, t * NEXP:(t + 1) * NEXP], lgt[:, t * P:(t + 1) * P], ident[0:NEXP, 0:NEXP])
            t_.then_inc(S("router"), 1)

    dense_pe(0, c0, g0, between=turn)
    with PE.Fori(1, G_UP) as g:
        dense_pe(g, c0, g0)
    DVE.wait_ge(S("router"), 1)
    DVE.tensor_tensor(pr[:], ps[0:P, 7, 0:T * NEXP].rearrange("p (t e) -> p t e", t=T),
                      rb[:].unsqueeze(1).to_broadcast([P, T, NEXP]), ALU.add)
    mk = sig(DVE.drain(), "dve_step")
    wait(ALE, mk)
    mk = sig(ALE.activation(pr[:], pr[:], ACT.Sigmoid), "act_step")
    wait(DVE, mk)
    pj = pr[:].unsqueeze(2).to_broadcast([P, T, NEXP, NEXP])
    pe_ = pr[:].unsqueeze(3).to_broadcast([P, T, NEXP, NEXP])
    DVE.tensor_tensor(gt[:], pj, pe_, ALU.is_gt)
    DVE.tensor_tensor(eq[:], pj, pe_, ALU.is_equal)
    DVE.drain()
    DVE.tensor_tensor(eq[:], eq[:], low[:].unsqueeze(1).to_broadcast([P, T, NEXP, NEXP]), ALU.mult)
    DVE.drain()
    DVE.tensor_tensor(gt[:], gt[:], eq[:], ALU.add)
    DVE.drain()
    DVE.tensor_reduce(cw[:], gt[:], AX.X, ALU.add)
    DVE.drain()
    DVE.tensor_scalar(cw[:], cw[:], 2.0, None, ALU.is_lt)
    DVE.drain()
    DVE.tensor_tensor(cw[:], cw[:], pr[:], ALU.mult)
    DVE.drain()

    n_sil = 0
    for g in range(G_UP + 1):
        experts = 2 if g < G_UP else 1
        if g == G_UP:
            for c in range(4):
                PE.wait_ge(S("split_done"), NST + c0 + g * KT + c + 1)
                for m in range(T):
                    if c == 0:
                        PE.wait_ge(S("bank_free"), (g + g0) * T + m + 1)
                    for kk in range(2):
                        k = 2 * c + kk
                        t_ = three(ps[0:P, m, 0:2 * HID], xt_hi[:, k, m * P:(m + 1) * P], xt_lo[:, k, m * P:(m + 1) * P],
                                   w_hi[:, c, kk * 256:kk * 256 + 256], w_lo[:, c, kk * 256:kk * 256 + 256],
                                   k == 0, k == KT - 1)
                    if m == T - 1:
                        t_.then_inc(S("w_used"), 1)
                    elif c == 3:
                        t_.then_inc(S("bank_full"), 1)
        for m in range(T):
            s_ = sil[n_sil % 4]
            blocks = ps[0:P, m, 0:256 * experts].rearrange("p (e w h) -> p e w h", w=2, h=HID)
            for eng in (ALE, DVE):
                if m < T - 1:
                    eng.wait_ge(S("bank_full"), (g + g0) * (T - 1) + m + 1)
                else:
                    eng.wait_ge(S("w_used"), NSL + c0 + (g * KT + KT if g < G_UP else g * KT + 4))
            if n_sil >= 4:
                ALE.wait_ge(S("sil_used"), n_sil - 3)
            mk = sig(ALE.activation(s_[:, 0:experts, :], blocks[:, :, 0, :], ACT.Silu), "sil_done")
            wait(DVE, mk)
            if experts == 2:
                for j in range(2):
                    e = 2 * g + j
                    t_ = DVE.scalar_tensor_tensor(hid[:, m, e * HID:(e + 1) * HID], s_[:, j, :], cw[:, m, e:e + 1],
                                                  blocks[:, j, 1, :], ALU.mult, ALU.mult)
            else:
                t_ = DVE.tensor_tensor(hid[:, m, NEXP * HID:], s_[:, 0, :], blocks[:, 0, 1, :], ALU.mult)
            t_.then_inc(S("bank_free"), 1)
            DVE.wait_ge(S("bank_free"), (g + g0 + 1) * T + m + 1)
            DVE.sem_inc(S("sil_used"), 1)
            n_sil += 1
    done["chunks"] += G_UP * KT + 4
    done["groups"] += G_UP + 1
    meet()
    ht_hi = at("ht_hi", [128, NEXP + 1, NP2], F32R, R_XT)
    ht_lo = at("ht_lo", [128, NEXP + 1, NP2], F32R, R_XT + 22592)
    transpose_split(hid, 128, NEXP + 1, ht_hi, ht_lo)
    meet()
    c0, g0 = done["chunks"], done["groups"]
    y = out.rearrange("(t p) d -> t p d", p=P)
    for h in range(2):
        for e in range(NEXP + 1):
            c = c0 + h * (NEXP + 1) + e
            q = c % NSL
            PE.wait_ge(S("split_done"), NST + c + 1)
            for m in range(T):
                if e == 0:
                    PE.wait_ge(S("bank_free"), (h + g0) * T + m + 1)
                t_ = three(ps[0:P, m, :], ht_hi[:, e, m * P:(m + 1) * P], ht_lo[:, e, m * P:(m + 1) * P],
                           w_hi[:, q, :], w_lo[:, q, :], e == 0, e == NEXP)
                if m == T - 1:
                    t_.then_inc(S("w_used"), 1)
                elif e == NEXP:
                    t_.then_inc(S("bank_full"), 1)
        for m in range(T):
            if m < T - 1:
                DVE.wait_ge(S("bank_full"), (h + g0) * (T - 1) + m + 1)
            else:
                DVE.wait_ge(S("w_used"), NSL + c0 + (h + 1) * (NEXP + 1))
            o = x1[:, m, h * 512:(h + 1) * 512]
            DVE.tensor_tensor(o, o, ps[0:P, m, :], ALU.add).then_inc(S("bank_free"), 1)
            ALE.wait_ge(S("bank_free"), (h + g0 + 1) * T + m + 1)
            mk = dma(y[m, :, h * 512:(h + 1) * 512], o, "st_out")
    wait(ALE, mk)


def kernel(**inputs):
    from concourse import bacc
    from concourse.bass_utils import run_bass_kernel_spmd

    v = {k: np.asarray(x) for k, x in inputs.items()}

    def chunks(wt):
        n = wt.shape[1] // 512
        return wt.reshape(KT, 128, n, 512).transpose(2, 0, 1, 3).reshape(n * KT, 128, 512)

    gate = v["L0_gnn_w_gate"]
    ups = np.stack([v["L1_ffn_Wg"], v["L1_ffn_Wu"]], axis=1).reshape(NEXP * 2 * HID, D).T
    shared = np.concatenate([v["L1_ffn_Wg_s"], v["L1_ffn_Wu_s"]], axis=0).T
    shared = shared.reshape(4, 2, 128, 2 * HID).transpose(0, 2, 1, 3).reshape(4, 128, 512)
    downs = np.concatenate([v["L1_ffn_Wd"], v["L1_ffn_Wd_s"][None]], axis=0)
    downs = downs.transpose(0, 2, 1).reshape(NEXP + 1, 128, 2, 512).transpose(2, 0, 1, 3).reshape(-1, 128, 512)
    stream = np.concatenate(
        [chunks(v["L0_gnn_root"]), chunks(gate[D:]), chunks(v["L0_mix_W_qkv"].T), chunks(v["L0_mix_W_proj"].T)]
        + [chunks(v["L0_gnn_weight"][r]) for r in range(REL)]
        + [chunks(gate[:D])]
        + [chunks(v[n].T) for n in ("L1_gnn_W", "L1_mix_Wq", "L1_mix_Wk", "L1_mix_Wv", "L1_mix_Wo")]
        + [chunks(ups), shared, downs])
    bias = np.concatenate([v[n] for n in ("L0_gnn_bias", "L0_gnn_b_gate", "L0_mix_b_qkv", "L0_mix_b_proj", "L1_gnn_b",
                                          "L1_mix_bq", "L1_mix_bk", "L1_mix_bv", "L1_mix_bo")]).reshape(NBIAS, 512)
    arrays = {
        "stream": stream, "bias": bias, "x": v["x"], "src": v["src"], "dst": v["dst"], "typ": v["edge_type_8"],
        "pm0": v["L0_mix_proj_mat"].T, "pm1": v["L1_mix_P"].T, "ln_g": v["L0_ffn_ln_g"][None], "ln_b": v["L0_ffn_ln_b"][None],
        "w1t": v["L0_ffn_w1"].T.reshape(KT, 128, FFN0).transpose(1, 0, 2),
        "w2t": v["L0_ffn_w2"].T.reshape(FFN0 // 128, 128, D).transpose(1, 0, 2),
        "wrt": v["L1_ffn_Wr"].T.reshape(KT, 128, NEXP).transpose(1, 0, 2), "rb": v["L1_ffn_rb"][None],
    }
    nc = bacc.Bacc("TRN2", target_bir_lowering=False, num_devices=1)
    feed, aps = {}, {}
    for k, x in arrays.items():
        feed["in_" + k] = np.ascontiguousarray(x)
        aps[k] = nc.dram_tensor("in_" + k, x.shape, mybir.dt.from_np(x.dtype), kind="ExternalInput").ap()
    out = nc.dram_tensor("out_x", [NODES, D], F32, kind="ExternalOutput").ap()
    build(nc, aps, out)
    r = run_bass_kernel_spmd(nc, [feed], core_ids=[0])
    return r.results[0]["out_x"]
```
